# Optimizing a Trainium2 kernel written in Bass

```python
import numpy as np
import jax
import jax.numpy as jnp

def _softmax(x, axis=-1):
    return jax.nn.softmax(x, axis=axis)

def _gelu(x):
    return jax.nn.gelu(x, approximate=True)

def _silu(x):
    return jax.nn.silu(x)

def _sigmoid(x):
    return jax.nn.sigmoid(x)

def _layernorm(x, axis=-1, eps=1e-05):
    m = jnp.mean(x, axis=axis, keepdims=True)
    v = jnp.var(x, axis=axis, keepdims=True)
    return (x - m) / jnp.sqrt(v + eps)

def _scatter_add(tgt, idx, src, axis=0):
    return tgt.at[idx].add(src)

def _segment_sum(src, seg, n):
    return jax.ops.segment_sum(src, seg, n)
kernel_name = 'mk_gps_d4_gnn_r32_3acf6d'

def setup_inputs(seed: int=0):
    np.random.seed(seed)
    _w = jnp.asarray

    def _rec_inputs():
        import jax
        import jax.numpy as jnp
        _gk = jax.random.key(seed)
        x = -0.0002117 + 1 * jax.random.normal(jax.random.fold_in(_gk, 1), (3125, 256), jnp.float32)
        src = jax.random.randint(jax.random.fold_in(_gk, 2), (50000,), 0, 3125, jnp.int32)
        dst = jnp.minimum((3125 * jax.random.uniform(jax.random.fold_in(_gk, 3), (50000,)) ** 2.0).astype(jnp.int32), 99999)
        _o = jnp.argsort(dst, stable=True)
        src = src[_o]
        dst = dst[_o]
        edge_weight = jax.random.uniform(jax.random.fold_in(_gk, 13), (50000,), jnp.float32, 0.0, 0.999998)
        node_vec = jax.random.uniform(jax.random.fold_in(_gk, 14), (3125,), jnp.float32, 0.0, 10025.9)
        return (x, src, dst, edge_weight, node_vec)
    x, src, dst, edge_weight, node_vec = _rec_inputs()

    def _L0_gnn_setup():
        import jax, jax.numpy as jnp
        import numpy as np
        N_NODES = 3125
        key = jax.random.key(seed)
        k1, k2, k3, k4 = jax.random.split(key, 4)
        E = 50000
        D_IN, D_OUT = (256, 256)
        feat = jax.random.normal(k1, (N_NODES, D_IN), dtype=jnp.float32)
        src = jax.random.randint(k2, (E,), 0, N_NODES, dtype=jnp.int32)
        dst = jax.random.randint(k3, (E,), 0, N_NODES, dtype=jnp.int32)
        limit = np.sqrt(6.0 / (D_IN + D_OUT)).astype(np.float32)
        weight = jax.random.uniform(k4, (D_IN, D_OUT), dtype=jnp.float32, minval=-limit, maxval=limit)
        bias = jnp.zeros((D_OUT,), dtype=jnp.float32)
        return {'feat': feat, 'src': src, 'dst': dst, 'weight': weight, 'bias': bias}
    _L0_gnn_all = _L0_gnn_setup()
    _L0_gnn_in = {k: v for k, v in _L0_gnn_all.items() if k in ('weight', 'bias')}
    del _L0_gnn_all

    def _L0_mix_setup():
        import jax, jax.numpy as jnp
        import numpy as np
        D_MODEL = 256
        NHEAD = 8
        D_HEAD = D_MODEL // NHEAD
        DIM_FF = 1024
        B, L = (4, 512)
        LN_EPS = 1e-05

        def _layernorm(x, g, b):
            mu = jnp.mean(x, axis=-1, keepdims=True)
            var = jnp.mean((x - mu) ** 2, axis=-1, keepdims=True)
            return (x - mu) * jax.lax.rsqrt(var + LN_EPS) * g + b

        def _phi(x):
            return jnp.where(x > 0, x + 1.0, jnp.exp(x))
        key = jax.random.key(seed)
        ks = jax.random.split(key, 16)
        s_in = 1.0 / np.sqrt(D_MODEL)
        s_ff = 1.0 / np.sqrt(DIM_FF)
        inp = {'x': jax.random.normal(ks[0], (B, L, D_MODEL), dtype=jnp.float32), 'Wq': jax.random.normal(ks[1], (D_MODEL, D_MODEL), dtype=jnp.float32) * s_in, 'bq': jnp.zeros((D_MODEL,), jnp.float32), 'Wk': jax.random.normal(ks[2], (D_MODEL, D_MODEL), dtype=jnp.float32) * s_in, 'bk': jnp.zeros((D_MODEL,), jnp.float32), 'Wv': jax.random.normal(ks[3], (D_MODEL, D_MODEL), dtype=jnp.float32) * s_in, 'bv': jnp.zeros((D_MODEL,), jnp.float32), 'Wo': jax.random.normal(ks[4], (D_MODEL, D_MODEL), dtype=jnp.float32) * s_in, 'bo': jnp.zeros((D_MODEL,), jnp.float32), 'W1': jax.random.normal(ks[5], (D_MODEL, DIM_FF), dtype=jnp.float32) * s_in, 'b1': jnp.zeros((DIM_FF,), jnp.float32), 'W2': jax.random.normal(ks[6], (DIM_FF, D_MODEL), dtype=jnp.float32) * s_ff, 'b2': jnp.zeros((D_MODEL,), jnp.float32), 'ln1_g': jnp.ones((D_MODEL,), jnp.float32), 'ln1_b': jnp.zeros((D_MODEL,), jnp.float32), 'ln2_g': jnp.ones((D_MODEL,), jnp.float32), 'ln2_b': jnp.zeros((D_MODEL,), jnp.float32)}
        return inp
    _L0_mix_all = _L0_mix_setup()
    _L0_mix_in = {k: v for k, v in _L0_mix_all.items() if k in ('Wq', 'bq', 'Wk', 'bk', 'Wv', 'bv', 'Wo', 'bo', 'W1', 'b1', 'W2', 'b2', 'ln1_g', 'ln1_b', 'ln2_g', 'ln2_b')}
    del _L0_mix_all

    def _L0_ffn_setup():
        import jax, jax.numpy as jnp
        import numpy as np
        BN_EPS = 0.001

        def _bn(h, g, b, m, v):
            return g * (h - m) * jax.lax.rsqrt(v + BN_EPS) + b
        key = jax.random.key(seed)
        ks = jax.random.split(key, 8)
        B, F, Df = (256, 64, 256)
        E, H, D = (8, 256, 256)
        s1 = 1.0 / np.sqrt(Df)
        s2 = 1.0 / np.sqrt(H)
        return {'x': jax.random.normal(ks[0], (B, F, Df), jnp.float32), 'Wr': jax.random.normal(ks[1], (Df, E), jnp.float32) * s1, 'br': jnp.zeros((E,), jnp.float32), 'W1': jax.random.normal(ks[2], (E, Df, H), jnp.float32) * s1, 'b1': jnp.zeros((E, H), jnp.float32), 'g1': jnp.ones((E, H), jnp.float32), 'be1': jnp.zeros((E, H), jnp.float32), 'm1': jnp.zeros((E, H), jnp.float32), 'v1': jnp.ones((E, H), jnp.float32), 'W2': jax.random.normal(ks[3], (E, H, H), jnp.float32) * s2, 'b2': jnp.zeros((E, H), jnp.float32), 'g2': jnp.ones((E, H), jnp.float32), 'be2': jnp.zeros((E, H), jnp.float32), 'm2': jnp.zeros((E, H), jnp.float32), 'v2': jnp.ones((E, H), jnp.float32), 'Wo': jax.random.normal(ks[4], (E, H, D), jnp.float32) * s2, 'bo': jnp.zeros((E, D), jnp.float32)}
    _L0_ffn_all = _L0_ffn_setup()
    _L0_ffn_in = {k: v for k, v in _L0_ffn_all.items() if k in ('Wr', 'br', 'W1', 'b1', 'g1', 'be1', 'm1', 'v1', 'W2', 'b2', 'g2', 'be2', 'm2', 'v2', 'Wo', 'bo')}
    del _L0_ffn_all

    def _L1_gnn_setup():
        import jax, jax.numpy as jnp
        import numpy as np
        NEG_SLOPE = 0.2
        WINDOW = 5

        def build_edge_index(n):
            srcs, dsts = ([], [])
            for d in range(1, WINDOW + 1):
                i = np.arange(d, n)
                srcs.append(i)
                dsts.append(i - d)
                srcs.append(i - d)
                dsts.append(i)
            i = np.arange(n)
            srcs.append(i)
            dsts.append(i)
            return jnp.asarray(np.stack([np.concatenate(srcs), np.concatenate(dsts)]), dtype=jnp.int32)

        def gat_layer(x, src, dst, W, a_src, a_dst, b, heads, out_ch, concat, n):
            h = (x @ W.T).reshape(n, heads, out_ch)
            alpha_src = jnp.sum(h * a_src, axis=-1)
            alpha_dst = jnp.sum(h * a_dst, axis=-1)
            e = jax.nn.leaky_relu(alpha_src[src] + alpha_dst[dst], NEG_SLOPE)
            m = jax.ops.segment_max(e, dst, num_segments=n)
            e = jnp.exp(e - m[dst])
            s = jax.ops.segment_sum(e, dst, num_segments=n)
            alpha = e / (s[dst] + 1e-16)
            out = jax.ops.segment_sum(alpha[:, :, None] * h[src], dst, num_segments=n)
            out = out.reshape(n, heads * out_ch) if concat else out.mean(axis=1)
            return out + b
        key = jax.random.key(seed)
        N, F, C, H = (625, 256, 128, 4)
        ks = jax.random.split(key, 8)
        inp = {'sequence_features': jax.random.normal(ks[0], (N, F), dtype=jnp.float32), 'timestamps': jnp.cumsum(jax.random.uniform(ks[1], (N,), dtype=jnp.float32)), 'edge_index': build_edge_index(N), 'W1': jax.random.normal(ks[2], (H * C, F), dtype=jnp.float32) * 0.05, 'a_src1': jax.random.normal(ks[3], (1, H, C), dtype=jnp.float32) * 0.05, 'a_dst1': jax.random.normal(ks[4], (1, H, C), dtype=jnp.float32) * 0.05, 'b1': jnp.zeros((H * C,), dtype=jnp.float32), 'W2': jax.random.normal(ks[5], (F, H * C), dtype=jnp.float32) * 0.05, 'a_src2': jax.random.normal(ks[6], (1, 1, F), dtype=jnp.float32) * 0.05, 'a_dst2': jax.random.normal(ks[7], (1, 1, F), dtype=jnp.float32) * 0.05, 'b2': jnp.zeros((F,), dtype=jnp.float32)}
        return inp
    _L1_gnn_all = _L1_gnn_setup()
    _L1_gnn_in = {k: v for k, v in _L1_gnn_all.items() if k in ('W1', 'a_src1', 'a_dst1', 'b1', 'W2', 'a_src2', 'a_dst2', 'b2')}
    del _L1_gnn_all

    def _L1_mix_setup():
        import jax, jax.numpy as jnp
        import numpy as np
        EPS = 1e-05

        def _layernorm(x, weight, bias):
            mean = jnp.mean(x, axis=-1, keepdims=True)
            std = jnp.std(x, axis=-1, keepdims=True, ddof=1)
            out = (x - mean) / (std + EPS)
            return weight * out + bias
        key = jax.random.key(seed)
        B, N, C = (4, 1024, 256)
        H, hc = (8, C // 8)
        kx, = jax.random.split(key, 1)
        x = jax.random.normal(kx, (B, N, C), dtype=jnp.float32)
        return {'x': x, 'kln_weight': jnp.ones((H, 1, hc), dtype=jnp.float32), 'kln_bias': jnp.zeros((H, 1, hc), dtype=jnp.float32), 'vln_weight': jnp.ones((H, 1, hc), dtype=jnp.float32), 'vln_bias': jnp.zeros((H, 1, hc), dtype=jnp.float32)}
    _L1_mix_all = _L1_mix_setup()
    _L1_mix_in = {k: v for k, v in _L1_mix_all.items() if k in ('kln_weight', 'kln_bias', 'vln_weight', 'vln_bias')}
    del _L1_mix_all

    def _L1_ffn_setup():
        import jax, jax.numpy as jnp
        import numpy as np
        B, S, D, F, E, K = (8, 64, 256, 1024, 8, 2)
        key = jax.random.key(seed)
        ks = jax.random.split(key, 10)
        s = 0.02
        return {'x': jax.random.normal(ks[0], (B, S, D), dtype=jnp.float32), 'Wr': jax.random.normal(ks[1], (D, E), dtype=jnp.float32) * s, 'W1s': jax.random.normal(ks[2], (D, F), dtype=jnp.float32) * s, 'b1s': jnp.zeros((F,), dtype=jnp.float32), 'W2s': jax.random.normal(ks[3], (F, D), dtype=jnp.float32) * s, 'b2s': jnp.zeros((D,), dtype=jnp.float32), 'W1p': jax.random.normal(ks[4], (E, D, F), dtype=jnp.float32) * s, 'b1p': jnp.zeros((E, F), dtype=jnp.float32), 'W2p': jax.random.normal(ks[5], (E, F, D), dtype=jnp.float32) * s, 'b2p': jnp.zeros((E, D), dtype=jnp.float32)}
    _L1_ffn_all = _L1_ffn_setup()
    _L1_ffn_in = {k: v for k, v in _L1_ffn_all.items() if k in ('Wr', 'W1s', 'b1s', 'W2s', 'b2s', 'W1p', 'b1p', 'W2p', 'b2p')}
    del _L1_ffn_all

    def _L2_gnn_setup():
        import jax, jax.numpy as jnp
        import numpy as np
        N = 50000
        E = 25000
        F_DIM = 256
        H = 4
        C = 64
        SLOPE = 0.2

        def gat_layer(x, src, dst, W, a_src, a_dst, bias, heads, out_ch):
            n = x.shape[0]
            xW = (x @ W).reshape(n, heads, out_ch)
            alpha_s = jnp.sum(xW * a_src, axis=-1)
            alpha_d = jnp.sum(xW * a_dst, axis=-1)
            e = jax.nn.leaky_relu(alpha_s[src] + alpha_d[dst], SLOPE)
            m = jax.ops.segment_max(e, dst, num_segments=n)
            w = jnp.exp(e - m[dst])
            z = jax.ops.segment_sum(w, dst, num_segments=n)
            alpha = w / z[dst]
            out = jax.ops.segment_sum(xW[src] * alpha[:, :, None], dst, num_segments=n)
            return out.reshape(n, heads * out_ch) + bias
        key = jax.random.key(seed)
        ks = jax.random.split(key, 11)
        s = 0.05
        return {'x': jax.random.normal(ks[0], (N, F_DIM), jnp.float32), 'edge_index': jax.random.randint(ks[1], (2, E), 0, N), 'W1': jax.random.normal(ks[2], (F_DIM, H * C), jnp.float32) * s, 'a_src1': jax.random.normal(ks[3], (H, C), jnp.float32) * s, 'a_dst1': jax.random.normal(ks[4], (H, C), jnp.float32) * s, 'b1': jnp.zeros((H * C,), jnp.float32), 'W2': jax.random.normal(ks[5], (H * C, F_DIM), jnp.float32) * s, 'a_src2': jax.random.normal(ks[6], (1, F_DIM), jnp.float32) * s, 'a_dst2': jax.random.normal(ks[7], (1, F_DIM), jnp.float32) * s, 'b2': jnp.zeros((F_DIM,), jnp.float32)}
    _L2_gnn_all = _L2_gnn_setup()
    _L2_gnn_in = {k: v for k, v in _L2_gnn_all.items() if k in ('W1', 'a_src1', 'a_dst1', 'b1', 'W2', 'a_src2', 'a_dst2', 'b2')}
    del _L2_gnn_all

    def _L2_mix_setup():
        import jax, jax.numpy as jnp
        import numpy as np
        DIM = 256
        HEADS = 4
        DIM_HEAD = 32
        NUM_MEM = 4
        HIDDEN = HEADS * DIM_HEAD
        SCALE = DIM_HEAD ** (-0.5)

        def rmsnorm(x, g):
            n = jnp.linalg.norm(x, axis=-1, keepdims=True)
            return x / jnp.maximum(n, 1e-12) * g * x.shape[-1] ** 0.5
        key = jax.random.key(seed)
        ks = jax.random.split(key, 8)
        B, N = (4, 512)
        return {'x': jax.random.normal(ks[0], (B, N, DIM), jnp.float32), 't': jax.random.normal(ks[1], (B,), jnp.float32), 'w_qkv': jax.random.normal(ks[2], (DIM, 3 * HIDDEN), jnp.float32) * 0.02, 'mem_kv': jax.random.normal(ks[3], (2, HEADS, DIM_HEAD, NUM_MEM), jnp.float32), 'w_out': jax.random.normal(ks[4], (HIDDEN, DIM), jnp.float32) * 0.02, 'b_out': jnp.zeros((DIM,), jnp.float32), 'g_out': jnp.ones((DIM,), jnp.float32), 'g_pre': jnp.ones((DIM,), jnp.float32)}
    _L2_mix_all = _L2_mix_setup()
    _L2_mix_in = {k: v for k, v in _L2_mix_all.items() if k in ('t', 'w_qkv', 'mem_kv', 'w_out', 'b_out', 'g_out', 'g_pre')}
    del _L2_mix_all

    def _L2_ffn_setup():
        import jax, jax.numpy as jnp
        import numpy as np
        B, S, D = (8, 128, 256)
        H = 4 * D
        CAPACITY = 0.5
        key = jax.random.key(seed)
        ks = jax.random.split(key, 6)
        x = jax.random.normal(ks[0], (B, S, D), dtype=jnp.float32)
        attention_mask = jnp.zeros((B, 1, 1, S), dtype=jnp.float32)
        wr = jax.random.normal(ks[1], (D, 1), dtype=jnp.float32) * 0.02
        br = jnp.zeros((1,), dtype=jnp.float32)
        w1 = jax.random.normal(ks[2], (D, H), dtype=jnp.float32) * 0.02
        b1 = jnp.zeros((H,), dtype=jnp.float32)
        w2 = jax.random.normal(ks[3], (H, D), dtype=jnp.float32) * 0.02
        b2 = jnp.zeros((D,), dtype=jnp.float32)
        return {'x': x, 'attention_mask': attention_mask, 'wr': wr, 'br': br, 'w1': w1, 'b1': b1, 'w2': w2, 'b2': b2}
    _L2_ffn_all = _L2_ffn_setup()
    _L2_ffn_in = {k: v for k, v in _L2_ffn_all.items() if k in ('attention_mask', 'wr', 'br', 'w1', 'b1', 'w2', 'b2')}
    del _L2_ffn_all

    def _L3_gnn_setup():
        import jax, jax.numpy as jnp
        import numpy as np
        from jax import lax
        N, E, D = (256, 8192, 256)
        NH, FOUT = (4, 64)
        D_STATE, D_CONV, DT_RANK = (16, 4, 16)

        def _layer_norm(x, g, b, eps=1e-05):
            mu = jnp.mean(x, -1, keepdims=True)
            var = jnp.var(x, -1, keepdims=True)
            return (x - mu) * lax.rsqrt(var + eps) * g + b

        def _mamba(xs, in_proj_w, conv_w, conv_b, x_proj_w, dt_proj_w, dt_proj_b, A_log, D_param, out_proj_w):
            n = xs.shape[0]
            xz = xs @ in_proj_w.T
            xc, z = jnp.split(xz, 2, axis=-1)
            K = conv_w.shape[1]
            xp = jnp.pad(xc, ((K - 1, 0), (0, 0)))
            xc = sum((xp[k:k + n] * conv_w[:, k] for k in range(K))) + conv_b
            xc = jax.nn.silu(xc)
            dbc = xc @ x_proj_w.T
            dt = jax.nn.softplus(dbc[:, :DT_RANK] @ dt_proj_w.T + dt_proj_b)
            Bm = dbc[:, DT_RANK:DT_RANK + D_STATE]
            Cm = dbc[:, DT_RANK + D_STATE:]
            A = -jnp.exp(A_log)
            dA = jnp.exp(dt[:, :, None] * A)
            dBx = (dt * xc)[:, :, None] * Bm[:, None, :]

            def step(h, t):
                dA_t, dBx_t, C_t = t
                h = dA_t * h + dBx_t
                return (h, h @ C_t)
            _, y = lax.scan(step, jnp.zeros((xc.shape[1], D_STATE), xs.dtype), (dA, dBx, Cm))
            y = y + xc * D_param
            y = y * jax.nn.silu(z)
            return y @ out_proj_w.T

        def _forward(x, edge_index, deg_noise, gat_w, gat_a_src, gat_a_tgt, gat_b, ln_local_g, ln_local_b, ln_global_g, ln_global_b, ln2_g, ln2_b, in_proj_w, conv_w, conv_b, x_proj_w, dt_proj_w, dt_proj_b, A_log, D_param, out_proj_w, wl, wg, ff1_w, ff1_b, ff2_w, ff2_b):
            n = x.shape[0]
            src, tgt = (edge_index[0], edge_index[1])
            proj = (x @ gat_w.T).reshape(n, NH, FOUT)
            s_src = jnp.sum(proj * gat_a_src, -1)
            s_tgt = jnp.sum(proj * gat_a_tgt, -1)
            e = jax.nn.leaky_relu(s_src[src] + s_tgt[tgt], 0.2)
            exp_e = jnp.exp(e - jnp.max(e))
            denom = jax.ops.segment_sum(exp_e, tgt, num_segments=n)
            attn = exp_e / (denom[tgt] + 1e-16)
            agg = jax.ops.segment_sum(proj[src] * attn[:, :, None], tgt, num_segments=n)
            h_local = jax.nn.elu((agg + x.reshape(n, NH, FOUT)).reshape(n, NH * FOUT) + gat_b)
            h_local = _layer_norm(h_local, ln_local_g, ln_local_b)
            deg = jax.ops.segment_sum(jnp.ones((src.shape[0],), x.dtype), src, num_segments=n)
            perm = jnp.argsort(deg + deg_noise, stable=True)
            inv = jnp.argsort(perm)
            y = _mamba(x[perm], in_proj_w, conv_w, conv_b, x_proj_w, dt_proj_w, dt_proj_b, A_log, D_param, out_proj_w)
            h_attn = _layer_norm(x + y[inv], ln_global_g, ln_global_b)
            gate = jax.nn.sigmoid(h_local @ wl.T + h_attn @ wg.T)
            h = gate * h_local + (1.0 - gate) * h_attn
            ff = jax.nn.relu(h @ ff1_w.T + ff1_b) @ ff2_w.T + ff2_b
            return _layer_norm(h + ff, ln2_g, ln2_b)
        key = jax.random.key(seed)
        ks = jax.random.split(key, 24)
        w = lambda i, shape, s=0.05: jax.random.normal(ks[i], shape, dtype=jnp.float32) * s
        return {'x': jax.random.normal(ks[0], (N, D), dtype=jnp.float32), 'edge_index': jax.random.randint(ks[1], (2, E), 0, N, dtype=jnp.int32), 'edge_prob': jax.random.uniform(ks[2], (E,), dtype=jnp.float32), 'deg_noise': jax.random.uniform(ks[3], (N,), dtype=jnp.float32), 'gat_w': w(4, (NH * FOUT, D)), 'gat_a_src': w(5, (NH, FOUT)), 'gat_a_tgt': w(6, (NH, FOUT)), 'gat_b': jnp.zeros((NH * FOUT,), jnp.float32), 'ln_local_g': jnp.ones((D,), jnp.float32), 'ln_local_b': jnp.zeros((D,), jnp.float32), 'ln_global_g': jnp.ones((D,), jnp.float32), 'ln_global_b': jnp.zeros((D,), jnp.float32), 'ln2_g': jnp.ones((D,), jnp.float32), 'ln2_b': jnp.zeros((D,), jnp.float32), 'in_proj_w': w(7, (2 * D, D)), 'conv_w': w(8, (D, D_CONV), 0.2), 'conv_b': jnp.zeros((D,), jnp.float32), 'x_proj_w': w(9, (DT_RANK + 2 * D_STATE, D)), 'dt_proj_w': w(10, (D, DT_RANK)), 'dt_proj_b': w(11, (D,), 0.1) - 4.0, 'A_log': jnp.log(jnp.tile(jnp.arange(1, D_STATE + 1, dtype=jnp.float32), (D, 1))), 'D_param': jnp.ones((D,), jnp.float32), 'out_proj_w': w(12, (D, D)), 'wl': w(13, (D, D)), 'wg': w(14, (D, D)), 'ff1_w': w(15, (2 * D, D)), 'ff1_b': jnp.zeros((2 * D,), jnp.float32), 'ff2_w': w(16, (D, 2 * D)), 'ff2_b': jnp.zeros((D,), jnp.float32)}
    _L3_gnn_all = _L3_gnn_setup()
    _L3_gnn_in = {k: v for k, v in _L3_gnn_all.items() if k in ('gat_w', 'gat_a_src', 'gat_a_tgt', 'gat_b', 'ln_local_g', 'ln_local_b', 'ln_global_g', 'ln_global_b', 'ln2_g', 'ln2_b', 'in_proj_w', 'conv_w', 'conv_b', 'x_proj_w', 'dt_proj_w', 'dt_proj_b', 'A_log', 'D_param', 'out_proj_w', 'wl', 'wg', 'ff1_w', 'ff1_b', 'ff2_w', 'ff2_b')}
    del _L3_gnn_all

    def _L3_mix_setup():
        import jax, jax.numpy as jnp
        import numpy as np
        NHEAD = 8
        ATT_EPS = 1e-06
        LN_EPS = 1e-05

        def _layernorm(x, g, b):
            mu = jnp.mean(x, axis=-1, keepdims=True)
            var = jnp.mean(jnp.square(x - mu), axis=-1, keepdims=True)
            return (x - mu) * jax.lax.rsqrt(var + LN_EPS) * g + b
        key = jax.random.key(seed)
        ks = jax.random.split(key, 7)
        N, L, C = (4, 512, 256)
        s = 1.0 / np.sqrt(C)
        return {'x': jax.random.normal(ks[0], (N, L, C), jnp.float32), 'Wq': jax.random.normal(ks[1], (C, C), jnp.float32) * s, 'Wk': jax.random.normal(ks[2], (C, C), jnp.float32) * s, 'Wv': jax.random.normal(ks[3], (C, C), jnp.float32) * s, 'Wm': jax.random.normal(ks[4], (C, C), jnp.float32) * s, 'W1': jax.random.normal(ks[5], (2 * C, 2 * C), jnp.float32) * (1.0 / np.sqrt(2 * C)), 'W2': jax.random.normal(ks[6], (2 * C, C), jnp.float32) * (1.0 / np.sqrt(2 * C)), 'g1': jnp.ones((C,), jnp.float32), 'b1': jnp.zeros((C,), jnp.float32), 'g2': jnp.ones((C,), jnp.float32), 'b2': jnp.zeros((C,), jnp.float32)}
    _L3_mix_all = _L3_mix_setup()
    _L3_mix_in = {k: v for k, v in _L3_mix_all.items() if k in ('Wq', 'Wk', 'Wv', 'Wm', 'W1', 'W2', 'g1', 'b1', 'g2', 'b2')}
    del _L3_mix_all

    def _L3_ffn_setup():
        import math
        import jax, jax.numpy as jnp
        import numpy as np
        CAPACITY_FACTOR = 1.25
        key = jax.random.key(seed)
        ks = jax.random.split(key, 5)
        B, L, D, F, E = (8, 256, 256, 1024, 8)
        h = jax.random.normal(ks[0], (B, L, D), dtype=jnp.float32)
        gate_w = jax.random.normal(ks[1], (D, E), dtype=jnp.float32) * 0.02
        gate_b = jnp.zeros((E,), dtype=jnp.float32)
        w1 = jax.random.normal(ks[2], (E, D, F), dtype=jnp.float32) * (1.0 / math.sqrt(D))
        b1 = jnp.zeros((E, F), dtype=jnp.float32)
        w2 = jax.random.normal(ks[3], (E, F, D), dtype=jnp.float32) * (1.0 / math.sqrt(F))
        b2 = jnp.zeros((E, D), dtype=jnp.float32)
        return {'h': h, 'gate_w': gate_w, 'gate_b': gate_b, 'w1': w1, 'b1': b1, 'w2': w2, 'b2': b2}
    _L3_ffn_all = _L3_ffn_setup()
    _L3_ffn_in = {k: v for k, v in _L3_ffn_all.items() if k in ('gate_w', 'gate_b', 'w1', 'b1', 'w2', 'b2')}
    del _L3_ffn_all
    return {'x': x, 'src': src, 'dst': dst, 'edge_weight': edge_weight, 'node_vec': node_vec, 'L0_gnn_weight': _L0_gnn_in['weight'], 'L0_gnn_bias': _L0_gnn_in['bias'], 'L0_mix_Wq': _L0_mix_in['Wq'], 'L0_mix_bq': _L0_mix_in['bq'], 'L0_mix_Wk': _L0_mix_in['Wk'], 'L0_mix_bk': _L0_mix_in['bk'], 'L0_mix_Wv': _L0_mix_in['Wv'], 'L0_mix_bv': _L0_mix_in['bv'], 'L0_mix_Wo': _L0_mix_in['Wo'], 'L0_mix_bo': _L0_mix_in['bo'], 'L0_mix_W1': _L0_mix_in['W1'], 'L0_mix_b1': _L0_mix_in['b1'], 'L0_mix_W2': _L0_mix_in['W2'], 'L0_mix_b2': _L0_mix_in['b2'], 'L0_mix_ln1_g': _L0_mix_in['ln1_g'], 'L0_mix_ln1_b': _L0_mix_in['ln1_b'], 'L0_mix_ln2_g': _L0_mix_in['ln2_g'], 'L0_mix_ln2_b': _L0_mix_in['ln2_b'], 'L0_ffn_Wr': _L0_ffn_in['Wr'], 'L0_ffn_br': _L0_ffn_in['br'], 'L0_ffn_W1': _L0_ffn_in['W1'], 'L0_ffn_b1': _L0_ffn_in['b1'], 'L0_ffn_g1': _L0_ffn_in['g1'], 'L0_ffn_be1': _L0_ffn_in['be1'], 'L0_ffn_m1': _L0_ffn_in['m1'], 'L0_ffn_v1': _L0_ffn_in['v1'], 'L0_ffn_W2': _L0_ffn_in['W2'], 'L0_ffn_b2': _L0_ffn_in['b2'], 'L0_ffn_g2': _L0_ffn_in['g2'], 'L0_ffn_be2': _L0_ffn_in['be2'], 'L0_ffn_m2': _L0_ffn_in['m2'], 'L0_ffn_v2': _L0_ffn_in['v2'], 'L0_ffn_Wo': _L0_ffn_in['Wo'], 'L0_ffn_bo': _L0_ffn_in['bo'], 'L1_gnn_W1': _L1_gnn_in['W1'], 'L1_gnn_a_src1': _L1_gnn_in['a_src1'], 'L1_gnn_a_dst1': _L1_gnn_in['a_dst1'], 'L1_gnn_b1': _L1_gnn_in['b1'], 'L1_gnn_W2': _L1_gnn_in['W2'], 'L1_gnn_a_src2': _L1_gnn_in['a_src2'], 'L1_gnn_a_dst2': _L1_gnn_in['a_dst2'], 'L1_gnn_b2': _L1_gnn_in['b2'], 'L1_mix_kln_weight': _L1_mix_in['kln_weight'], 'L1_mix_kln_bias': _L1_mix_in['kln_bias'], 'L1_mix_vln_weight': _L1_mix_in['vln_weight'], 'L1_mix_vln_bias': _L1_mix_in['vln_bias'], 'L1_ffn_Wr': _L1_ffn_in['Wr'], 'L1_ffn_W1s': _L1_ffn_in['W1s'], 'L1_ffn_b1s': _L1_ffn_in['b1s'], 'L1_ffn_W2s': _L1_ffn_in['W2s'], 'L1_ffn_b2s': _L1_ffn_in['b2s'], 'L1_ffn_W1p': _L1_ffn_in['W1p'], 'L1_ffn_b1p': _L1_ffn_in['b1p'], 'L1_ffn_W2p': _L1_ffn_in['W2p'], 'L1_ffn_b2p': _L1_ffn_in['b2p'], 'L2_gnn_W1': _L2_gnn_in['W1'], 'L2_gnn_a_src1': _L2_gnn_in['a_src1'], 'L2_gnn_a_dst1': _L2_gnn_in['a_dst1'], 'L2_gnn_b1': _L2_gnn_in['b1'], 'L2_gnn_W2': _L2_gnn_in['W2'], 'L2_gnn_a_src2': _L2_gnn_in['a_src2'], 'L2_gnn_a_dst2': _L2_gnn_in['a_dst2'], 'L2_gnn_b2': _L2_gnn_in['b2'], 'L2_mix_t': _L2_mix_in['t'], 'L2_mix_w_qkv': _L2_mix_in['w_qkv'], 'L2_mix_mem_kv': _L2_mix_in['mem_kv'], 'L2_mix_w_out': _L2_mix_in['w_out'], 'L2_mix_b_out': _L2_mix_in['b_out'], 'L2_mix_g_out': _L2_mix_in['g_out'], 'L2_mix_g_pre': _L2_mix_in['g_pre'], 'L2_ffn_attention_mask': _L2_ffn_in['attention_mask'], 'L2_ffn_wr': _L2_ffn_in['wr'], 'L2_ffn_br': _L2_ffn_in['br'], 'L2_ffn_w1': _L2_ffn_in['w1'], 'L2_ffn_b1': _L2_ffn_in['b1'], 'L2_ffn_w2': _L2_ffn_in['w2'], 'L2_ffn_b2': _L2_ffn_in['b2'], 'L3_gnn_gat_w': _L3_gnn_in['gat_w'], 'L3_gnn_gat_a_src': _L3_gnn_in['gat_a_src'], 'L3_gnn_gat_a_tgt': _L3_gnn_in['gat_a_tgt'], 'L3_gnn_gat_b': _L3_gnn_in['gat_b'], 'L3_gnn_ln_local_g': _L3_gnn_in['ln_local_g'], 'L3_gnn_ln_local_b': _L3_gnn_in['ln_local_b'], 'L3_gnn_ln_global_g': _L3_gnn_in['ln_global_g'], 'L3_gnn_ln_global_b': _L3_gnn_in['ln_global_b'], 'L3_gnn_ln2_g': _L3_gnn_in['ln2_g'], 'L3_gnn_ln2_b': _L3_gnn_in['ln2_b'], 'L3_gnn_in_proj_w': _L3_gnn_in['in_proj_w'], 'L3_gnn_conv_w': _L3_gnn_in['conv_w'], 'L3_gnn_conv_b': _L3_gnn_in['conv_b'], 'L3_gnn_x_proj_w': _L3_gnn_in['x_proj_w'], 'L3_gnn_dt_proj_w': _L3_gnn_in['dt_proj_w'], 'L3_gnn_dt_proj_b': _L3_gnn_in['dt_proj_b'], 'L3_gnn_A_log': _L3_gnn_in['A_log'], 'L3_gnn_D_param': _L3_gnn_in['D_param'], 'L3_gnn_out_proj_w': _L3_gnn_in['out_proj_w'], 'L3_gnn_wl': _L3_gnn_in['wl'], 'L3_gnn_wg': _L3_gnn_in['wg'], 'L3_gnn_ff1_w': _L3_gnn_in['ff1_w'], 'L3_gnn_ff1_b': _L3_gnn_in['ff1_b'], 'L3_gnn_ff2_w': _L3_gnn_in['ff2_w'], 'L3_gnn_ff2_b': _L3_gnn_in['ff2_b'], 'L3_mix_Wq': _L3_mix_in['Wq'], 'L3_mix_Wk': _L3_mix_in['Wk'], 'L3_mix_Wv': _L3_mix_in['Wv'], 'L3_mix_Wm': _L3_mix_in['Wm'], 'L3_mix_W1': _L3_mix_in['W1'], 'L3_mix_W2': _L3_mix_in['W2'], 'L3_mix_g1': _L3_mix_in['g1'], 'L3_mix_b1': _L3_mix_in['b1'], 'L3_mix_g2': _L3_mix_in['g2'], 'L3_mix_b2': _L3_mix_in['b2'], 'L3_ffn_gate_w': _L3_ffn_in['gate_w'], 'L3_ffn_gate_b': _L3_ffn_in['gate_b'], 'L3_ffn_w1': _L3_ffn_in['w1'], 'L3_ffn_b1': _L3_ffn_in['b1'], 'L3_ffn_w2': _L3_ffn_in['w2'], 'L3_ffn_b2': _L3_ffn_in['b2']}

def reference(x, src, dst, edge_weight, node_vec, L0_gnn_weight, L0_gnn_bias, L0_mix_Wq, L0_mix_bq, L0_mix_Wk, L0_mix_bk, L0_mix_Wv, L0_mix_bv, L0_mix_Wo, L0_mix_bo, L0_mix_W1, L0_mix_b1, L0_mix_W2, L0_mix_b2, L0_mix_ln1_g, L0_mix_ln1_b, L0_mix_ln2_g, L0_mix_ln2_b, L0_ffn_Wr, L0_ffn_br, L0_ffn_W1, L0_ffn_b1, L0_ffn_g1, L0_ffn_be1, L0_ffn_m1, L0_ffn_v1, L0_ffn_W2, L0_ffn_b2, L0_ffn_g2, L0_ffn_be2, L0_ffn_m2, L0_ffn_v2, L0_ffn_Wo, L0_ffn_bo, L1_gnn_W1, L1_gnn_a_src1, L1_gnn_a_dst1, L1_gnn_b1, L1_gnn_W2, L1_gnn_a_src2, L1_gnn_a_dst2, L1_gnn_b2, L1_mix_kln_weight, L1_mix_kln_bias, L1_mix_vln_weight, L1_mix_vln_bias, L1_ffn_Wr, L1_ffn_W1s, L1_ffn_b1s, L1_ffn_W2s, L1_ffn_b2s, L1_ffn_W1p, L1_ffn_b1p, L1_ffn_W2p, L1_ffn_b2p, L2_gnn_W1, L2_gnn_a_src1, L2_gnn_a_dst1, L2_gnn_b1, L2_gnn_W2, L2_gnn_a_src2, L2_gnn_a_dst2, L2_gnn_b2, L2_mix_t, L2_mix_w_qkv, L2_mix_mem_kv, L2_mix_w_out, L2_mix_b_out, L2_mix_g_out, L2_mix_g_pre, L2_ffn_attention_mask, L2_ffn_wr, L2_ffn_br, L2_ffn_w1, L2_ffn_b1, L2_ffn_w2, L2_ffn_b2, L3_gnn_gat_w, L3_gnn_gat_a_src, L3_gnn_gat_a_tgt, L3_gnn_gat_b, L3_gnn_ln_local_g, L3_gnn_ln_local_b, L3_gnn_ln_global_g, L3_gnn_ln_global_b, L3_gnn_ln2_g, L3_gnn_ln2_b, L3_gnn_in_proj_w, L3_gnn_conv_w, L3_gnn_conv_b, L3_gnn_x_proj_w, L3_gnn_dt_proj_w, L3_gnn_dt_proj_b, L3_gnn_A_log, L3_gnn_D_param, L3_gnn_out_proj_w, L3_gnn_wl, L3_gnn_wg, L3_gnn_ff1_w, L3_gnn_ff1_b, L3_gnn_ff2_w, L3_gnn_ff2_b, L3_mix_Wq, L3_mix_Wk, L3_mix_Wv, L3_mix_Wm, L3_mix_W1, L3_mix_W2, L3_mix_g1, L3_mix_b1, L3_mix_g2, L3_mix_b2, L3_ffn_gate_w, L3_ffn_gate_b, L3_ffn_w1, L3_ffn_b1, L3_ffn_w2, L3_ffn_b2):
    import jax
    import jax.numpy as jnp

    def _L0_gnn_ref(feat, src, dst, weight, bias):
        import jax, jax.numpy as jnp
        import numpy as np
        N_NODES = 3125
        ones = jnp.ones(src.shape[0], dtype=feat.dtype)
        out_deg = jax.ops.segment_sum(ones, src, num_segments=N_NODES)
        in_deg = jax.ops.segment_sum(ones, dst, num_segments=N_NODES)
        pre = jnp.power(jnp.clip(out_deg, 1.0), -0.5)[:, None]
        h = feat * pre
        agg = jax.ops.segment_sum(h[src], dst, num_segments=N_NODES)
        rst = agg @ weight
        post = jnp.power(jnp.clip(in_deg, 1.0), -0.5)[:, None]
        rst = rst * post + bias
        return rst

    def _L0_mix_ref(x, Wq, bq, Wk, bk, Wv, bv, Wo, bo, W1, b1, W2, b2, ln1_g, ln1_b, ln2_g, ln2_b):
        import jax, jax.numpy as jnp
        import numpy as np
        D_MODEL = 256
        NHEAD = 8
        D_HEAD = D_MODEL // NHEAD
        DIM_FF = 1024
        B, L = (4, 512)
        LN_EPS = 1e-05

        def _layernorm(x, g, b):
            mu = jnp.mean(x, axis=-1, keepdims=True)
            var = jnp.mean((x - mu) ** 2, axis=-1, keepdims=True)
            return (x - mu) * jax.lax.rsqrt(var + LN_EPS) * g + b

        def _phi(x):
            return jnp.where(x > 0, x + 1.0, jnp.exp(x))
        Bq, Lq, _ = x.shape
        q = (x @ Wq + bq).reshape(Bq, Lq, NHEAD, D_HEAD)
        k = (x @ Wk + bk).reshape(Bq, Lq, NHEAD, D_HEAD)
        v = (x @ Wv + bv).reshape(Bq, Lq, NHEAD, D_HEAD)
        q_phi = _phi(q)
        k_phi = _phi(k)
        kv = jnp.einsum('blhd,blhe->bhde', k_phi, v)
        k_sum = k_phi.sum(axis=1)
        z = 1.0 / (jnp.einsum('blhd,bhd->blh', q_phi, k_sum) + 1e-06)
        out = jnp.einsum('blhd,bhde,blh->blhe', q_phi, kv, z)
        out = out.reshape(Bq, Lq, D_MODEL) @ Wo + bo
        x = _layernorm(x + out, ln1_g, ln1_b)
        ff = jax.nn.relu(x @ W1 + b1) @ W2 + b2
        x = _layernorm(x + ff, ln2_g, ln2_b)
        return x

    def _L0_ffn_ref(x, Wr, br, W1, b1, g1, be1, m1, v1, W2, b2, g2, be2, m2, v2, Wo, bo):
        import jax, jax.numpy as jnp
        import numpy as np
        BN_EPS = 0.001

        def _bn(h, g, b, m, v):
            return g * (h - m) * jax.lax.rsqrt(v + BN_EPS) + b
        feat = jnp.mean(x, axis=0)
        w = jax.nn.softmax(feat @ Wr + br, axis=-1)
        h = jnp.einsum('bfd,edh->bfeh', x, W1) + b1
        h = jax.nn.relu(_bn(h, g1, be1, m1, v1))
        h = jnp.einsum('bfeh,ehk->bfek', h, W2) + b2
        h = jax.nn.relu(_bn(h, g2, be2, m2, v2))
        y = jnp.einsum('bfeh,ehd->bfed', h, Wo) + bo
        return jnp.einsum('bfed,fe->bfd', y, w)

    def _L1_gnn_ref(sequence_features, timestamps, edge_index, W1, a_src1, a_dst1, b1, W2, a_src2, a_dst2, b2):
        import jax, jax.numpy as jnp
        import numpy as np
        NEG_SLOPE = 0.2
        WINDOW = 5

        def build_edge_index(n):
            srcs, dsts = ([], [])
            for d in range(1, WINDOW + 1):
                i = np.arange(d, n)
                srcs.append(i)
                dsts.append(i - d)
                srcs.append(i - d)
                dsts.append(i)
            i = np.arange(n)
            srcs.append(i)
            dsts.append(i)
            return jnp.asarray(np.stack([np.concatenate(srcs), np.concatenate(dsts)]), dtype=jnp.int32)

        def gat_layer(x, src, dst, W, a_src, a_dst, b, heads, out_ch, concat, n):
            h = (x @ W.T).reshape(n, heads, out_ch)
            alpha_src = jnp.sum(h * a_src, axis=-1)
            alpha_dst = jnp.sum(h * a_dst, axis=-1)
            e = jax.nn.leaky_relu(alpha_src[src] + alpha_dst[dst], NEG_SLOPE)
            m = jax.ops.segment_max(e, dst, num_segments=n)
            e = jnp.exp(e - m[dst])
            s = jax.ops.segment_sum(e, dst, num_segments=n)
            alpha = e / (s[dst] + 1e-16)
            out = jax.ops.segment_sum(alpha[:, :, None] * h[src], dst, num_segments=n)
            out = out.reshape(n, heads * out_ch) if concat else out.mean(axis=1)
            return out + b
        n = sequence_features.shape[0]
        src, dst = (edge_index[0], edge_index[1])
        x = gat_layer(sequence_features, src, dst, W1, a_src1, a_dst1, b1, heads=4, out_ch=128, concat=True, n=n)
        x = jax.nn.elu(x)
        x = gat_layer(x, src, dst, W2, a_src2, a_dst2, b2, heads=1, out_ch=256, concat=False, n=n)
        return x

    def _L1_mix_ref(x, kln_weight, kln_bias, vln_weight, vln_bias):
        import jax, jax.numpy as jnp
        import numpy as np
        EPS = 1e-05

        def _layernorm(x, weight, bias):
            mean = jnp.mean(x, axis=-1, keepdims=True)
            std = jnp.std(x, axis=-1, keepdims=True, ddof=1)
            out = (x - mean) / (std + EPS)
            return weight * out + bias
        B, N, C = x.shape
        H = kln_weight.shape[0]
        hc = C // H
        qkv = x.reshape(B, N, H, hc).transpose(0, 2, 1, 3)
        q = qkv
        k = _layernorm(qkv, kln_weight, kln_bias)
        v = _layernorm(qkv, vln_weight, vln_bias)
        kv = jnp.einsum('bhnd,bhne->bhde', k, v) / N
        out = jnp.einsum('bhnd,bhde->bhne', q, kv)
        out = out.transpose(0, 2, 1, 3).reshape(B, N, C)
        return out + x

    def _L1_ffn_ref(x, Wr, W1s, b1s, W2s, b2s, W1p, b1p, W2p, b2p):
        import jax, jax.numpy as jnp
        import numpy as np
        B, S, D, F, E, K = (8, 64, 256, 1024, 8, 2)
        gelu = lambda t: jax.nn.gelu(t, approximate=False)
        shared = gelu(x @ W1s + b1s) @ W2s + b2s
        rw = jax.nn.softmax(x @ Wr, axis=-1)
        topw, topi = jax.lax.top_k(rw, K)
        topw = topw / jnp.sum(topw, axis=-1, keepdims=True)
        mask = jnp.sum(jax.nn.one_hot(topi, E, dtype=topw.dtype) * topw[..., None], axis=-2)
        h = gelu(jnp.einsum('bsd,edf->bsef', x, W1p) + b1p)
        priv = jnp.einsum('bsef,efd->bsed', h, W2p) + b2p
        routed = jnp.einsum('bsed,bse->bsd', priv, mask)
        return shared + routed

    def _L2_gnn_ref(x, edge_index, W1, a_src1, a_dst1, b1, W2, a_src2, a_dst2, b2):
        import jax, jax.numpy as jnp
        import numpy as np
        N = 50000
        E = 25000
        F_DIM = 256
        H = 4
        C = 64
        SLOPE = 0.2

        def gat_layer(x, src, dst, W, a_src, a_dst, bias, heads, out_ch):
            n = x.shape[0]
            xW = (x @ W).reshape(n, heads, out_ch)
            alpha_s = jnp.sum(xW * a_src, axis=-1)
            alpha_d = jnp.sum(xW * a_dst, axis=-1)
            e = jax.nn.leaky_relu(alpha_s[src] + alpha_d[dst], SLOPE)
            m = jax.ops.segment_max(e, dst, num_segments=n)
            w = jnp.exp(e - m[dst])
            z = jax.ops.segment_sum(w, dst, num_segments=n)
            alpha = w / z[dst]
            out = jax.ops.segment_sum(xW[src] * alpha[:, :, None], dst, num_segments=n)
            return out.reshape(n, heads * out_ch) + bias
        loop = jnp.arange(N)
        src = jnp.concatenate([edge_index[0], loop])
        dst = jnp.concatenate([edge_index[1], loop])
        h = jax.nn.elu(gat_layer(x, src, dst, W1, a_src1, a_dst1, b1, H, C))
        return gat_layer(h, src, dst, W2, a_src2, a_dst2, b2, 1, F_DIM)

    def _L2_mix_ref(x, t, w_qkv, mem_kv, w_out, b_out, g_out, g_pre):
        import jax, jax.numpy as jnp
        import numpy as np
        DIM = 256
        HEADS = 4
        DIM_HEAD = 32
        NUM_MEM = 4
        HIDDEN = HEADS * DIM_HEAD
        SCALE = DIM_HEAD ** (-0.5)

        def rmsnorm(x, g):
            n = jnp.linalg.norm(x, axis=-1, keepdims=True)
            return x / jnp.maximum(n, 1e-12) * g * x.shape[-1] ** 0.5
        b, n, c = x.shape
        xn = rmsnorm(x, g_pre)
        qkv = xn @ w_qkv
        q, k, v = jnp.split(qkv, 3, axis=-1)

        def to_heads(z):
            return z.reshape(b, n, HEADS, DIM_HEAD).transpose(0, 2, 3, 1)
        q, k, v = map(to_heads, (q, k, v))
        mk = jnp.broadcast_to(mem_kv[0], (b, HEADS, DIM_HEAD, NUM_MEM))
        mv = jnp.broadcast_to(mem_kv[1], (b, HEADS, DIM_HEAD, NUM_MEM))
        k = jnp.concatenate([mk, k], axis=-1)
        v = jnp.concatenate([mv, v], axis=-1)
        q = jax.nn.softmax(q, axis=-2) * SCALE
        k = jax.nn.softmax(k, axis=-1)
        context = jnp.einsum('bhdn,bhen->bhde', k, v)
        out = jnp.einsum('bhde,bhdn->bhen', context, q)
        out = out.transpose(0, 3, 1, 2).reshape(b, n, HIDDEN)
        out = rmsnorm(out @ w_out + b_out, g_out)
        return out + x

    def _L2_ffn_ref(x, attention_mask, wr, br, w1, b1, w2, b2):
        import jax, jax.numpy as jnp
        import numpy as np
        B, S, D = (8, 128, 256)
        H = 4 * D
        CAPACITY = 0.5
        b, s, d = x.shape
        weights = (jnp.einsum('bsd,do->bso', x, wr) + br)[..., 0]
        k = max(1, int(CAPACITY * s))
        kk = k - 1 if k > 1 else 1
        _, idx = jax.lax.top_k(weights, k)
        sel_idx = idx[:, :kk]
        sel = jnp.take_along_axis(x, sel_idx[:, :, None], axis=1)
        h = jax.nn.gelu(jnp.einsum('bkd,dh->bkh', sel, w1) + b1)
        y = jnp.einsum('bkh,hd->bkd', h, w2) + b2
        w_sel = jnp.take_along_axis(weights, sel_idx, axis=1)
        y = y * w_sel[..., None]
        batch_idx = jnp.arange(b)[:, None]
        processed = jnp.zeros_like(x).at[batch_idx, sel_idx].set(y)
        return processed + x

    def _L3_gnn_ref(x, edge_index, edge_prob, deg_noise, gat_w, gat_a_src, gat_a_tgt, gat_b, ln_local_g, ln_local_b, ln_global_g, ln_global_b, ln2_g, ln2_b, in_proj_w, conv_w, conv_b, x_proj_w, dt_proj_w, dt_proj_b, A_log, D_param, out_proj_w, wl, wg, ff1_w, ff1_b, ff2_w, ff2_b):
        import jax, jax.numpy as jnp
        import numpy as np
        from jax import lax
        N, E, D = (256, 8192, 256)
        NH, FOUT = (4, 64)
        D_STATE, D_CONV, DT_RANK = (16, 4, 16)

        def _layer_norm(x, g, b, eps=1e-05):
            mu = jnp.mean(x, -1, keepdims=True)
            var = jnp.var(x, -1, keepdims=True)
            return (x - mu) * lax.rsqrt(var + eps) * g + b

        def _mamba(xs, in_proj_w, conv_w, conv_b, x_proj_w, dt_proj_w, dt_proj_b, A_log, D_param, out_proj_w):
            n = xs.shape[0]
            xz = xs @ in_proj_w.T
            xc, z = jnp.split(xz, 2, axis=-1)
            K = conv_w.shape[1]
            xp = jnp.pad(xc, ((K - 1, 0), (0, 0)))
            xc = sum((xp[k:k + n] * conv_w[:, k] for k in range(K))) + conv_b
            xc = jax.nn.silu(xc)
            dbc = xc @ x_proj_w.T
            dt = jax.nn.softplus(dbc[:, :DT_RANK] @ dt_proj_w.T + dt_proj_b)
            Bm = dbc[:, DT_RANK:DT_RANK + D_STATE]
            Cm = dbc[:, DT_RANK + D_STATE:]
            A = -jnp.exp(A_log)
            dA = jnp.exp(dt[:, :, None] * A)
            dBx = (dt * xc)[:, :, None] * Bm[:, None, :]

            def step(h, t):
                dA_t, dBx_t, C_t = t
                h = dA_t * h + dBx_t
                return (h, h @ C_t)
            _, y = lax.scan(step, jnp.zeros((xc.shape[1], D_STATE), xs.dtype), (dA, dBx, Cm))
            y = y + xc * D_param
            y = y * jax.nn.silu(z)
            return y @ out_proj_w.T

        def _forward(x, edge_index, deg_noise, gat_w, gat_a_src, gat_a_tgt, gat_b, ln_local_g, ln_local_b, ln_global_g, ln_global_b, ln2_g, ln2_b, in_proj_w, conv_w, conv_b, x_proj_w, dt_proj_w, dt_proj_b, A_log, D_param, out_proj_w, wl, wg, ff1_w, ff1_b, ff2_w, ff2_b):
            n = x.shape[0]
            src, tgt = (edge_index[0], edge_index[1])
            proj = (x @ gat_w.T).reshape(n, NH, FOUT)
            s_src = jnp.sum(proj * gat_a_src, -1)
            s_tgt = jnp.sum(proj * gat_a_tgt, -1)
            e = jax.nn.leaky_relu(s_src[src] + s_tgt[tgt], 0.2)
            exp_e = jnp.exp(e - jnp.max(e))
            denom = jax.ops.segment_sum(exp_e, tgt, num_segments=n)
            attn = exp_e / (denom[tgt] + 1e-16)
            agg = jax.ops.segment_sum(proj[src] * attn[:, :, None], tgt, num_segments=n)
            h_local = jax.nn.elu((agg + x.reshape(n, NH, FOUT)).reshape(n, NH * FOUT) + gat_b)
            h_local = _layer_norm(h_local, ln_local_g, ln_local_b)
            deg = jax.ops.segment_sum(jnp.ones((src.shape[0],), x.dtype), src, num_segments=n)
            perm = jnp.argsort(deg + deg_noise, stable=True)
            inv = jnp.argsort(perm)
            y = _mamba(x[perm], in_proj_w, conv_w, conv_b, x_proj_w, dt_proj_w, dt_proj_b, A_log, D_param, out_proj_w)
            h_attn = _layer_norm(x + y[inv], ln_global_g, ln_global_b)
            gate = jax.nn.sigmoid(h_local @ wl.T + h_attn @ wg.T)
            h = gate * h_local + (1.0 - gate) * h_attn
            ff = jax.nn.relu(h @ ff1_w.T + ff1_b) @ ff2_w.T + ff2_b
            return _layer_norm(h + ff, ln2_g, ln2_b)
        return _forward(x, edge_index, deg_noise, gat_w, gat_a_src, gat_a_tgt, gat_b, ln_local_g, ln_local_b, ln_global_g, ln_global_b, ln2_g, ln2_b, in_proj_w, conv_w, conv_b, x_proj_w, dt_proj_w, dt_proj_b, A_log, D_param, out_proj_w, wl, wg, ff1_w, ff1_b, ff2_w, ff2_b)

    def _L3_mix_ref(x, Wq, Wk, Wv, Wm, W1, W2, g1, b1, g2, b2):
        import jax, jax.numpy as jnp
        import numpy as np
        NHEAD = 8
        ATT_EPS = 1e-06
        LN_EPS = 1e-05

        def _layernorm(x, g, b):
            mu = jnp.mean(x, axis=-1, keepdims=True)
            var = jnp.mean(jnp.square(x - mu), axis=-1, keepdims=True)
            return (x - mu) * jax.lax.rsqrt(var + LN_EPS) * g + b
        N, L, C = x.shape
        H = NHEAD
        D = C // H
        q = (x @ Wq).reshape(N, L, H, D)
        k = (x @ Wk).reshape(N, L, H, D)
        v = (x @ Wv).reshape(N, L, H, D)
        Q = jax.nn.elu(q) + 1.0
        K = jax.nn.elu(k) + 1.0
        v = v / L
        KV = jnp.einsum('nshd,nshv->nhdv', K, v)
        Z = 1.0 / (jnp.einsum('nlhd,nhd->nlh', Q, K.sum(axis=1)) + ATT_EPS)
        msg = jnp.einsum('nlhd,nhdv,nlh->nlhv', Q, KV, Z) * L
        msg = msg.reshape(N, L, C) @ Wm
        msg = _layernorm(msg, g1, b1)
        h = jnp.concatenate([x, msg], axis=-1) @ W1
        h = jax.nn.relu(h) @ W2
        msg = _layernorm(h, g2, b2)
        return x + msg

    def _L3_ffn_ref(h, gate_w, gate_b, w1, b1, w2, b2):
        import math
        import jax, jax.numpy as jnp
        import numpy as np
        CAPACITY_FACTOR = 1.25
        B, L, D = h.shape
        E = gate_w.shape[1]
        T = B * L
        C = max(1, math.ceil(CAPACITY_FACTOR * T / E))
        x = h.reshape(T, D)
        logits = x @ gate_w + gate_b
        probs = jax.nn.softmax(logits, axis=-1)
        idx = jnp.argmax(probs, axis=-1)
        prb = jnp.take_along_axis(probs, idx[:, None], axis=1)[:, 0]
        one_hot = jax.nn.one_hot(idx, E, dtype=jnp.float32)
        pos = (jnp.cumsum(one_hot, axis=0) * one_hot).sum(-1).astype(jnp.int32) - 1
        kept = pos < C
        pos_safe = jnp.where(kept, pos, C)
        buf = jnp.zeros((E, C, D), dtype=h.dtype).at[idx, pos_safe].set(x, mode='drop')
        hmid = jax.nn.relu(jnp.einsum('ecd,edf->ecf', buf, w1) + b1[:, None, :])
        ybuf = jnp.einsum('ecf,efd->ecd', hmid, w2) + b2[:, None, :]
        pos_g = jnp.minimum(pos, C - 1)
        y_tok = ybuf[idx, pos_g] * (prb * kept)[:, None]
        y = y_tok.reshape(B, L, D)
        y = jnp.nan_to_num(y, nan=0.0, posinf=10000.0, neginf=-10000.0)
        return y
    edge_index = jnp.stack([src, dst])
    xn = _layernorm(x, axis=-1)
    x = x + _L0_gnn_ref(xn, src, dst, L0_gnn_weight, L0_gnn_bias) + _L0_mix_ref(xn[None], L0_mix_Wq, L0_mix_bq, L0_mix_Wk, L0_mix_bk, L0_mix_Wv, L0_mix_bv, L0_mix_Wo, L0_mix_bo, L0_mix_W1, L0_mix_b1, L0_mix_W2, L0_mix_b2, L0_mix_ln1_g, L0_mix_ln1_b, L0_mix_ln2_g, L0_mix_ln2_b)[0]
    x = x + _L0_ffn_ref(_layernorm(x, axis=-1)[None], L0_ffn_Wr, L0_ffn_br, L0_ffn_W1, L0_ffn_b1, L0_ffn_g1, L0_ffn_be1, L0_ffn_m1, L0_ffn_v1, L0_ffn_W2, L0_ffn_b2, L0_ffn_g2, L0_ffn_be2, L0_ffn_m2, L0_ffn_v2, L0_ffn_Wo, L0_ffn_bo)[0]
    xn = _layernorm(x, axis=-1)
    x = x + _L1_gnn_ref(xn, node_vec, edge_index, L1_gnn_W1, L1_gnn_a_src1, L1_gnn_a_dst1, L1_gnn_b1, L1_gnn_W2, L1_gnn_a_src2, L1_gnn_a_dst2, L1_gnn_b2) + _L1_mix_ref(xn[None], L1_mix_kln_weight, L1_mix_kln_bias, L1_mix_vln_weight, L1_mix_vln_bias)[0]
    x = x + _L1_ffn_ref(_layernorm(x, axis=-1)[None], L1_ffn_Wr, L1_ffn_W1s, L1_ffn_b1s, L1_ffn_W2s, L1_ffn_b2s, L1_ffn_W1p, L1_ffn_b1p, L1_ffn_W2p, L1_ffn_b2p)[0]
    xn = _layernorm(x, axis=-1)
    x = x + _L2_gnn_ref(xn, edge_index, L2_gnn_W1, L2_gnn_a_src1, L2_gnn_a_dst1, L2_gnn_b1, L2_gnn_W2, L2_gnn_a_src2, L2_gnn_a_dst2, L2_gnn_b2) + _L2_mix_ref(xn[None], L2_mix_t, L2_mix_w_qkv, L2_mix_mem_kv, L2_mix_w_out, L2_mix_b_out, L2_mix_g_out, L2_mix_g_pre)[0]
    x = x + _L2_ffn_ref(_layernorm(x, axis=-1)[None], L2_ffn_attention_mask, L2_ffn_wr, L2_ffn_br, L2_ffn_w1, L2_ffn_b1, L2_ffn_w2, L2_ffn_b2)[0]
    xn = _layernorm(x, axis=-1)
    x = x + _L3_gnn_ref(xn, edge_index, edge_weight, node_vec, L3_gnn_gat_w, L3_gnn_gat_a_src, L3_gnn_gat_a_tgt, L3_gnn_gat_b, L3_gnn_ln_local_g, L3_gnn_ln_local_b, L3_gnn_ln_global_g, L3_gnn_ln_global_b, L3_gnn_ln2_g, L3_gnn_ln2_b, L3_gnn_in_proj_w, L3_gnn_conv_w, L3_gnn_conv_b, L3_gnn_x_proj_w, L3_gnn_dt_proj_w, L3_gnn_dt_proj_b, L3_gnn_A_log, L3_gnn_D_param, L3_gnn_out_proj_w, L3_gnn_wl, L3_gnn_wg, L3_gnn_ff1_w, L3_gnn_ff1_b, L3_gnn_ff2_w, L3_gnn_ff2_b) + _L3_mix_ref(xn[None], L3_mix_Wq, L3_mix_Wk, L3_mix_Wv, L3_mix_Wm, L3_mix_W1, L3_mix_W2, L3_mix_g1, L3_mix_b1, L3_mix_g2, L3_mix_b2)[0]
    x = x + _L3_ffn_ref(_layernorm(x, axis=-1)[None], L3_ffn_gate_w, L3_ffn_gate_b, L3_ffn_w1, L3_ffn_b1, L3_ffn_w2, L3_ffn_b2)[0]
    return x

_drawn_inputs = setup_inputs


def setup_inputs(seed=0):
    import zlib

    import numpy as np

    out = dict(_drawn_inputs(seed))
    spreads = {'L0_gnn_bias': (0.0, 0.1),
     'L0_mix_bq': (0.0, 0.8),
     'L0_mix_bk': (0.0, 0.8),
     'L0_mix_bv': (0.0, 0.1),
     'L0_mix_bo': (0.0, 0.1),
     'L0_mix_b1': (0.0, 0.1),
     'L0_mix_b2': (0.0, 0.1),
     'L0_mix_ln1_g': (1.0, 0.2),
     'L0_mix_ln1_b': (0.0, 0.1),
     'L0_mix_ln2_g': (1.0, 0.2),
     'L0_mix_ln2_b': (0.0, 0.1),
     'L0_ffn_br': (0.0, 0.376),
     'L0_ffn_b1': (0.0, 0.561),
     'L0_ffn_g1': (1.0, 0.579),
     'L0_ffn_be1': (0.0, 0.575),
     'L0_ffn_m1': (0.0, 0.566),
     'L0_ffn_v1': (1.0, 0.6),
     'L0_ffn_b2': (0.0, 0.387),
     'L0_ffn_g2': (1.0, 0.2),
     'L0_ffn_be2': (0.0, 0.397),
     'L0_ffn_m2': (0.0, 0.38),
     'L0_ffn_v2': (1.0, 0.6),
     'L0_ffn_bo': (0.0, 0.1),
     'L1_gnn_b1': (0.0, 0.349),
     'L1_gnn_b2': (0.0, 0.313),
     'L1_mix_kln_weight': (1.0, 0.2),
     'L1_mix_kln_bias': (0.0, 0.1),
     'L1_mix_vln_weight': (1.0, 0.2),
     'L1_mix_vln_bias': (0.0, 0.1),
     'L1_ffn_b1s': (0.0, 0.8),
     'L1_ffn_b2s': (0.0, 0.348),
     'L1_ffn_b1p': (0.0, 0.8),
     'L1_ffn_b2p': (0.0, 0.463),
     'L2_gnn_b1': (0.0, 0.638),
     'L2_gnn_b2': (0.0, 0.474),
     'L2_mix_b_out': (0.0, 0.1),
     'L2_mix_g_out': (1.0, 0.2),
     'L2_mix_g_pre': (1.0, 0.6),
     'L2_ffn_b1': (0.0, 0.8),
     'L2_ffn_b2': (0.0, 0.8),
     'L3_gnn_gat_b': (0.0, 0.8),
     'L3_gnn_ln_local_g': (1.0, 0.6),
     'L3_gnn_ln_local_b': (0.0, 0.8),
     'L3_gnn_ln_global_g': (1.0, 0.6),
     'L3_gnn_ln_global_b': (0.0, 0.8),
     'L3_gnn_ln2_g': (1.0, 0.6),
     'L3_gnn_ln2_b': (0.0, 0.683),
     'L3_gnn_conv_b': (0.0, 2.0),
     'L3_gnn_D_param': (1.0, 0.6),
     'L3_gnn_ff1_b': (0.0, 0.8),
     'L3_gnn_ff2_b': (0.0, 0.726),
     'L3_mix_g1': (1.0, 0.6),
     'L3_mix_b1': (0.0, 0.8),
     'L3_mix_g2': (1.0, 0.6),
     'L3_mix_b2': (0.0, 0.64),
     'L3_ffn_gate_b': (0.0, 0.707),
     'L3_ffn_b1': (0.0, 0.8),
     'L3_ffn_b2': (0.0, 2.0)}
    factors = {'node_vec': 8.0,
     'L0_mix_Wq': 8.0,
     'L0_mix_Wk': 8.0,
     'L0_mix_Wv': 4.054,
     'L1_gnn_a_src1': 7.761,
     'L1_gnn_a_dst1': 8.0,
     'L1_gnn_a_src2': 8.0,
     'L1_gnn_a_dst2': 8.0,
     'L1_ffn_W1p': 3.175,
     'L1_ffn_W2p': 2.958,
     'L2_gnn_a_src1': 8.0,
     'L2_gnn_a_dst1': 8.0,
     'L2_gnn_a_src2': 8.0,
     'L2_gnn_a_dst2': 64.0,
     'L2_mix_w_qkv': 6.235,
     'L2_mix_mem_kv': 8.0,
     'L2_mix_w_out': 7.037,
     'L2_ffn_wr': 8.0,
     'L2_ffn_w1': 8.0,
     'L2_ffn_w2': 8.0,
     'L3_gnn_gat_a_src': 8.0,
     'L3_gnn_gat_a_tgt': 37.508,
     'L3_gnn_in_proj_w': 8.0,
     'L3_gnn_conv_w': 8.0,
     'L3_gnn_x_proj_w': 8.0,
     'L3_gnn_dt_proj_w': 8.0,
     'L3_gnn_dt_proj_b': 60.45,
     'L3_gnn_A_log': 27.169,
     'L3_gnn_out_proj_w': 8.0,
     'L3_gnn_wl': 4.865,
     'L3_gnn_wg': 5.017,
     'L3_mix_Wq': 37.396,
     'L3_mix_Wk': 33.179,
     'L3_ffn_gate_w': 4.236,
     'L3_ffn_w1': 4.693,
     'L3_ffn_w2': 3.84}
    for name, (base, spread) in spreads.items():
        noise = np.random.default_rng([zlib.crc32(name.encode()), seed]).standard_normal(out[name].shape)
        drawn = base * np.exp(spread * noise) if base else spread * noise
        out[name] = jnp.asarray(drawn.astype(out[name].dtype))
    for name, factor in factors.items():
        out[name] = (out[name] * factor).astype(out[name].dtype)
    return out
```

```python
from contextlib import ExitStack

import concourse.bass as bass
from concourse import mybir
from concourse.alu_op_type import AluOpType as ALU

F32 = mybir.dt.float32
BF16 = mybir.dt.bfloat16
I32 = mybir.dt.int32
ACT = mybir.ActivationFunctionType
AX = mybir.AxisListType
ts = bass.ts

N = 3125
E = 50000
D = 256
KD = D // 128
P = 125
T = N // P
U = 5
CW = 448
NCH = 7
NC = NCH * CW
EF = E // P
EB = 8
ET = -(-((E + T * 127) // 128) // (2 * EB)) * 2 * EB
CHAINS = 4
NEG = -1e30
BLOCKS = 8


class Stage:

    count = 0

    def __init__(self, nc):
        self.nc = nc
        self.mem = ExitStack()
        self.sems = []
        Stage.count += 1
        self.n = Stage.count

    def sb(self, name, shape, dt=F32):
        return self.mem.enter_context(self.nc.sbuf_tensor(f"{name}_{self.n}", shape, dt))

    def sem(self, name):
        s = self.nc.alloc_semaphore(f"{name}_{self.n}")
        self.sems.append(s)
        return s

    def __enter__(self):
        return self

    def __exit__(self, *exc):
        if exc[0] is None and self.sems:
            self.nc.clear_and_free_semaphores(self.sems)
            self.nc.all_engine_barrier()
        self.mem.close()


class Chain:

    def __init__(self, eng, sem, base=0):
        self.eng, self.sem, self.base, self.n = eng, sem, base, 0

    def __call__(self, ins):
        self.n += 1
        ins.then_inc(self.sem, 1)
        self.eng.wait_ge(self.sem, self.base + self.n)


def blocks(v, n=128):
    return v.rearrange("(m p) -> p m", p=n)


def over(ap, n):
    return bass.AP(ap.tensor, ap.offset, [[0, n]] + [list(d) for d in ap.ap])


def norm_cols(nc, G, src, dst, eps=1e-5, gain=None, shift=None, add=None, rms=False):
    with Stage(nc) as s:
        cen, sq, rstd = s.sb("cen", [128, KD, CW]), s.sb("sq", [128, KD, CW]), s.sb("rstd", [128, CW])
        gs = s.sb("gs", [128, 2, KD])
        loaded, mean_done, cen_done, sq_done, var_done, root_done, steps, out_done = [
            s.sem(x) for x in ("loaded", "mean", "cen", "sq", "var", "root", "steps", "out")]
        n_loads = (gain is not None) + (shift is not None)
        PS = G.PS
        with nc.Block() as block:
            @block.sync
            def _(sp):
                if gain is not None:
                    sp.dma_start(gs[:, 0, :], blocks(gain)).then_inc(loaded, 16)
                if shift is not None:
                    sp.dma_start(gs[:, 1, :], blocks(shift)).then_inc(loaded, 16)

            @block.tensor
            def _(pe):
                with pe.Fori(0, NCH) as i:
                    if not rms:
                        pe.wait_ge(out_done, i + 1)
                        for k in range(KD):
                            mm = pe.matmul(PS[:, 0, 0:CW], G.mean[:, :], src[:, k, ts(i, CW)],
                                           start=(k == 0), stop=(k == KD - 1))
                        mm.then_inc(mean_done, 1)
                    pe.wait_ge(sq_done, i + 1)
                    for k in range(KD):
                        mm = pe.matmul(PS[:, 1, 0:CW], (G.ones if rms else G.mean)[:, :], sq[:, k, :],
                                       start=(k == 0), stop=(k == KD - 1))
                    mm.then_inc(var_done, 1)

            @block.scalar
            def _(act):
                with act.Fori(0, NCH) as i:
                    if rms:
                        act.wait_ge(out_done, i + 1)
                        act.activation(sq[:, :, :], src[:, :, ts(i, CW)], ACT.Square).then_inc(sq_done, 1)
                    else:
                        act.wait_ge(cen_done, i + 1)
                        act.activation(sq[:, :, :], cen[:, :, :], ACT.Square).then_inc(sq_done, 1)
                    act.wait_ge(var_done, i + 1)
                    if rms:
                        act.activation(rstd[:, :], PS[:, 1, 0:CW], ACT.Sqrt).then_inc(root_done, 1)
                    else:
                        act.activation(rstd[:, :], PS[:, 1, 0:CW], ACT.Sqrt, bias=G.eps[:, 0:1]).then_inc(root_done, 1)

            @block.vector
            def _(v):
                v.sem_inc(out_done, 1)
                if n_loads:
                    v.wait_ge(loaded, 16 * n_loads)
                with v.Fori(0, NCH) as i:
                    K = (2 if rms else 1) + KD * ((gain is not None or shift is not None) + (add is not None))
                    c = Chain(v, steps, i * K)
                    if rms:
                        v.wait_ge(root_done, i + 1)
                        c(v.tensor_scalar(rstd[:, :], rstd[:, :], 1e-12, float(D) ** -0.5, ALU.max, ALU.mult))
                        cs = src[:, :, ts(i, CW)]
                    else:
                        v.wait_ge(mean_done, i + 1)
                        for k in range(KD):
                            mm = v.tensor_tensor(cen[:, k, :], src[:, k, ts(i, CW)], PS[:, 0, 0:CW], ALU.subtract)
                        mm.then_inc(cen_done, 1)
                        v.wait_ge(root_done, i + 1)
                        cs = cen[:, :, :]
                    c(v.reciprocal(rstd[:, :], rstd[:, :]))
                    for k in range(KD):
                        to = cen[:, k, :] if add is not None else dst[:, k, ts(i, CW)]
                        ins = v.tensor_tensor(to, cs[:, k, :], rstd[:, :], ALU.mult)
                        if gain is not None or shift is not None:
                            c(ins)
                            g = gs[:, 0, k:k + 1] if gain is not None else 1.0
                            b = gs[:, 1, k:k + 1] if shift is not None else 0.0
                            ins = v.tensor_scalar(to, to, g, b, ALU.mult, ALU.add)
                        if add is not None:
                            c(ins)
                            ins = v.tensor_tensor(dst[:, k, ts(i, CW)], add[:, k, ts(i, CW)], to, ALU.add)
                    assert c.n == K
                    ins.then_inc(out_done, 1)


def dense_cols(nc, G, src, kc, w, mo, out, bias=None, func=ACT.Identity, add=False, kp=128, mp=128):
    NB = min(mo, 4)
    with Stage(nc) as s:
        W, B = s.sb("W", [kp, kc, mo * mp]), s.sb("B", [mp, mo])
        loaded, mm_done, out_done, zeroed, turns = [s.sem(x) for x in ("loaded", "mm", "out", "zeroed", "turns")]
        with nc.Block() as block:
            @block.sync
            def _(sp):
                sp.dma_start(W[:, :, :], w.rearrange("(k p) m -> p k m", p=kp)).then_inc(loaded, 16)
                if bias is not None:
                    sp.dma_start(B[:, :], blocks(bias, mp)).then_inc(loaded, 16)
            n_loads = 16 * (1 + (bias is not None))

            @block.tensor
            def _(pe):
                pe.wait_ge(loaded, n_loads)
                with pe.Fori(0, NCH) as i:
                    for m in range(mo):
                        pe.wait_ge(out_done, i * mo + m + 1)
                        if kp < 128:
                            pe.sem_inc(turns, 1)
                        for k in range(kc):
                            mm = pe.matmul(G.PS[0:mp, m % NB, 0:CW], W[:, k, ts(m, mp)], src[:, k, ts(i, CW)],
                                           start=(k == 0), stop=(k == kc - 1))
                        mm.then_inc(mm_done, 1)

            def evacuate(eng, one):
                eng.sem_inc(out_done, NB)
                if bias is None:
                    eng.memzero(B[:, :]).then_inc(zeroed, 1)
                    eng.wait_ge(zeroed, 1)
                else:
                    eng.wait_ge(loaded, n_loads)
                with eng.Fori(0, NCH) as i:
                    for m in range(mo):
                        eng.wait_ge(mm_done, i * mo + m + 1)
                        one(i, m).then_inc(out_done, 1)

            if add:
                @block.vector
                def _(v):
                    evacuate(v, lambda i, m: v.scalar_tensor_tensor(
                        out=out[:, m, ts(i, CW)], in0=G.PS[0:mp, m % NB, 0:CW], scalar=B[:, m:m + 1],
                        in1=out[:, m, ts(i, CW)], op0=ALU.add, op1=ALU.add))
            else:
                @block.scalar
                def _(act):
                    evacuate(act, lambda i, m: act.activation(
                        out[:, m, ts(i, CW)], G.PS[0:mp, m % NB, 0:CW], func, bias=B[:, m:m + 1]))


def project_rows(nc, G, src, kc, parts, M, dst, bias=(), kp=128, mul=None):
    with Stage(nc) as s:
        W = s.sb("W", [kp, kc, M])
        B = s.sb("B", [P, M]) if bias else None
        X = s.sb("X", [kp, U, kc, P])
        loaded, copied, mm_done, out_done = [s.sem(x) for x in ("loaded", "copied", "mm", "out")]
        n_loads = 16 * (len(parts) + len(bias))
        with nc.Block() as block:
            @block.sync
            def _(sp):
                for w, c in parts:
                    sp.dma_start(W[:, :, c:c + w.shape[1]], w.rearrange("(k p) m -> p k m", p=kp)).then_inc(loaded, 16)
                for b, c in bias:
                    sp.dma_start(B[:, c:c + b.shape[0]], over(b, P)).then_inc(loaded, 16)

            @block.scalar
            def _(act):
                act.sem_inc(mm_done, U)
                with act.Fori(0, T // U) as i:
                    for u in range(U):
                        act.wait_ge(mm_done, i * U + u + 1)
                        act.activation(X[:, u, :, :], src[:, :, ts(i * U + u, P)], ACT.Copy).then_inc(copied, 1)

            @block.tensor
            def _(pe):
                pe.wait_ge(loaded, n_loads)
                with pe.Fori(0, T // U) as i:
                    for u in range(U):
                        pe.wait_ge(copied, i * U + u + 1)
                        pe.wait_ge(out_done, i * U + u + 1)
                        for k in range(kc):
                            mm = pe.matmul(G.PS[0:P, u, 0:M], X[:, u, k, :], W[:, k, :],
                                           start=(k == 0), stop=(k == kc - 1))
                        mm.then_inc(mm_done, 1)

            @block.vector
            def _(v):
                v.sem_inc(out_done, U)
                v.wait_ge(loaded, n_loads)
                with v.Fori(0, T // U) as i:
                    for u in range(U):
                        t = i * U + u
                        v.wait_ge(mm_done, U + t + 1)
                        to = dst[:, ts(t, 1), :].rearrange("p a m -> p (a m)")
                        if bias:
                            ins = v.tensor_tensor(to, G.PS[0:P, u, 0:M], B[:, :], ALU.add)
                        elif mul is not None:
                            ins = v.tensor_scalar(to, G.PS[0:P, u, 0:M], mul[:, ts(t, 1)], None, ALU.mult)
                        else:
                            ins = v.tensor_copy(to, G.PS[0:P, u, 0:M])
                        ins.then_inc(out_done, 1)


def rows_to_cols(nc, G, rows, M, dst, add=False):
    mo = M // 128
    with Stage(nc) as s:
        X = s.sb("X", [P, U, M])
        copied, turned, out_done = [s.sem(x) for x in ("copied", "turned", "out")]
        with nc.Block() as block:
            @block.scalar
            def _(act):
                act.sem_inc(turned, U)
                with act.Fori(0, T // U) as i:
                    for u in range(U):
                        act.wait_ge(turned, i * U + u + 1)
                        act.activation(X[:, u, :], rows[:, ts(i * U + u, 1), :].rearrange("p a m -> p (a m)"),
                                       ACT.Copy).then_inc(copied, 1)

            @block.tensor
            def _(pe):
                with pe.Fori(0, T // U) as i:
                    for u in range(U):
                        pe.wait_ge(copied, i * U + u + 1)
                        pe.wait_ge(out_done, i * U + u + 1)
                        for m in range(mo):
                            mm = pe.transpose(G.PS[:, u, m * P:(m + 1) * P], X[:, u, ts(m, 128)], G.ident[0:P, 0:P])
                        mm.then_inc(turned, 1)

            @block.vector
            def _(v):
                v.sem_inc(out_done, U)
                if not add:
                    v.memset(dst[:, :, N:NC], 0.0)
                with v.Fori(0, T // U) as i:
                    for u in range(U):
                        t = i * U + u
                        v.wait_ge(turned, U + t + 1)
                        ps = G.PS[:, u, 0:mo * P].rearrange("p (m n) -> p m n", m=mo)
                        if add:
                            ins = v.tensor_tensor(dst[:, :, ts(t, P)], dst[:, :, ts(t, P)], ps, ALU.add)
                        else:
                            ins = v.tensor_copy(dst[:, :, ts(t, P)], ps)
                        ins.then_inc(out_done, 1)


def spread_gate(nc, G, gates, n, dram):
    W = T * n
    turns = [(a, min(120, W - a)) for a in range(0, W, 120)]
    with Stage(nc) as s:
        R = s.sb("R", [128, len(turns), P])
        turned, copied, stored = [s.sem(x) for x in ("turned", "copied", "stored")]
        flat = gates.rearrange("p t e -> p (t e)")
        with nc.Block() as block:
            @block.tensor
            def _(pe):
                for j, (a, w) in enumerate(turns):
                    pe.transpose(G.PS[0:w, j, 0:P], flat[:, a:a + w], G.ident[0:P, 0:P]).then_inc(turned, 1)

            @block.vector
            def _(v):
                for j, (a, w) in enumerate(turns):
                    v.wait_ge(turned, j + 1)
                    v.tensor_copy(R[0:w, j, :], G.PS[0:w, j, 0:P]).then_inc(copied, 1)

            @block.sync
            def _(sp):
                sp.wait_ge(copied, len(turns))
                done = 0
                for j, (a, w) in enumerate(turns):
                    for t in range(a // n, (a + w) // n):
                        sp.dma_start(dram[0:n, t * P:(t + 1) * P], R[t * n - a:t * n - a + n, j, :]).then_inc(stored, 16)
                        done += 1
                sp.wait_ge(stored, 16 * done)


def ffn(nc, G, src, kc, w1, b1, w2, b2, F, func, out, n_exp, gate, layers=None):
    MH = F // 128
    NP = min(2, n_exp)
    with Stage(nc) as s:
        W1 = [s.sb(f"W1{j}", [128, kc, F]) for j in range(NP)]
        W2 = [s.sb(f"W2{j}", [128, MH, D]) for j in range(NP)]
        B1 = [s.sb(f"B1{j}", [128, MH]) for j in range(NP)]
        B2 = [s.sb(f"B2{j}", [128, KD]) for j in range(NP)]
        g_sb = [s.sb(f"g{j}", [128, NC]) for j in range(NP)] if gate is not None else None
        H = s.sb("H", [128, 4, CW])
        Y = s.sb("Y", [128, KD, CW])
        n_loads = 5 if gate is not None else 4
        loaded = [s.sem(f"loaded{j}") for j in range(NP)]
        up_done, h_done, down_done, y_done, out_done, exp_done = [
            s.sem(x) for x in ("up", "h", "down", "y", "out", "expert")]

        def rounds(eng, body):
            with eng.Fori(0, n_exp // NP) as r:
                for j in range(NP):
                    with eng.Fori(0, NCH) as c:
                        body(j, c, (r * NP + j) * NCH + c, r)

        with nc.Block() as block:
            @block.sync
            def _(sp):
                sp.sem_inc(exp_done, NP)
                with sp.Fori(0, n_exp // NP) as r:
                    for j in range(NP):
                        e = r * NP + j
                        sp.wait_ge(exp_done, e + 1)
                        one = lambda ap: ap[ts(e, 1)]
                        sp.dma_start(W1[j][:, :, :], one(w1).rearrange("a (k p) f -> p (a k) f", p=128)).then_inc(loaded[j], 16)
                        sp.dma_start(W2[j][:, :, :], one(w2).rearrange("a (m p) d -> p (a m) d", p=128)).then_inc(loaded[j], 16)
                        sp.dma_start(B1[j][:, :], one(b1).rearrange("a (m p) -> p (a m)", p=128)).then_inc(loaded[j], 16)
                        sp.dma_start(B2[j][:, :], one(b2).rearrange("a (m p) -> p (a m)", p=128)).then_inc(loaded[j], 16)
                        if gate is not None:
                            row = one(gate)
                            sp.dma_start(g_sb[j][:, :], bass.AP(row.tensor, row.offset, [[0, 128], [1, NC]])).then_inc(loaded[j], 16)

            @block.tensor
            def _(pe):
                pe.sem_inc(down_done, 4)
                def body(j, c, n, r):
                    pe.wait_ge(loaded[j], (r + 1) * 16 * n_loads)

                    def up(m):
                        pe.wait_ge(h_done, n * MH + m + 1)
                        for k in range(kc):
                            mm = pe.matmul(G.PS[:, m % 4, 0:CW], W1[j][:, k, ts(m, 128)], src[:, k, ts(c, CW)],
                                           start=(k == 0), stop=(k == kc - 1))
                        mm.then_inc(up_done, 1)

                    def down(m):
                        pe.wait_ge(h_done, 4 + n * MH + m + 1)
                        if m == 0:
                            pe.wait_ge(y_done, n + 1)
                        for o in range(KD):
                            mm = pe.matmul(G.PS[:, 4 + o, 0:CW], W2[j][:, m, ts(o, 128)], H[:, m % 4, :],
                                           start=(m == 0), stop=(m == MH - 1))
                        mm.then_inc(down_done, 1)

                    up(0)
                    for m in range(1, MH):
                        up(m)
                        down(m - 1)
                    down(MH - 1)
                rounds(pe, body)

            @block.scalar
            def _(act):
                act.sem_inc(h_done, 4)
                def body(j, c, n, r):
                    act.wait_ge(loaded[j], (r + 1) * 16 * n_loads)
                    for m in range(MH):
                        act.wait_ge(up_done, n * MH + m + 1)
                        act.wait_ge(down_done, n * MH + m + 1)
                        act.activation(H[:, m % 4, :], G.PS[:, m % 4, 0:CW], func, bias=B1[j][:, m:m + 1]).then_inc(h_done, 1)
                rounds(act, body)

            @block.vector
            def _(v):
                v.sem_inc(y_done, 1)
                def body(j, c, n, r):
                    v.wait_ge(loaded[j], (r + 1) * 16 * n_loads)
                    v.wait_ge(down_done, 4 + (n + 1) * MH)
                    for o in range(KD):
                        if gate is not None:
                            ins = v.scalar_tensor_tensor(out=Y[:, o, :], in0=G.PS[:, 4 + o, 0:CW], scalar=B2[j][:, o:o + 1],
                                                         in1=g_sb[j][:, ts(c, CW)], op0=ALU.add, op1=ALU.mult)
                        else:
                            ins = v.tensor_scalar(Y[:, o, :], G.PS[:, 4 + o, 0:CW], B2[j][:, o:o + 1], None, ALU.add)
                    ins.then_inc(y_done, 1)
                    v.wait_ge(y_done, n + 2)
                    v.tensor_tensor(out[:, :, ts(c, CW)], out[:, :, ts(c, CW)], Y[:, :, :], ALU.add).then_inc(out_done, 1)
                    v.wait_ge(out_done, n + 1)
                with v.Fori(0, n_exp // NP) as r:
                    for j in range(NP):
                        with v.Fori(0, NCH) as c:
                            body(j, c, (r * NP + j) * NCH + c, r)
                        v.sem_inc(exp_done, 1)


def setup(nc, G, x):
    with Stage(nc) as s:
        rows = s.sb("rows", [P, T, D])
        made, loaded = s.sem("made"), s.sem("loaded")
        with nc.Block() as block:
            @block.gpsimd
            def _(pool):
                c = Chain(pool, made)
                c(pool.memset(G.ident[:, :], 0.0))
                c(pool.affine_select(out=G.ident[:, :], in_=G.ident[:, :], compare_op=ALU.not_equal, fill=1.0, base=0,
                                     pattern=[[-1, 128]], channel_multiplier=1))
                c(pool.memset(G.blockmask[:, :], 1.0))
                g4 = G.blockmask[:, :].rearrange("p (g n) -> p g n", g=4)
                c(pool.affine_select(out=g4, in_=g4, compare_op=ALU.is_ge, fill=0.0, base=0,
                                     pattern=[[-32, 4], [0, 32]], channel_multiplier=1))
                c(pool.affine_select(out=g4, in_=g4, compare_op=ALU.is_ge, fill=0.0, base=31,
                                     pattern=[[32, 4], [0, 32]], channel_multiplier=-1))
                c(pool.memset(G.before[:, :], 1.0))
                c(pool.affine_select(out=G.before[:, :], in_=G.before[:, :], compare_op=ALU.is_gt, fill=0.0, base=0,
                                     pattern=[[1, P]], channel_multiplier=-1))
                c(pool.memset(G.after[:, :], 1.0))
                c(pool.affine_select(out=G.after[:, :], in_=G.after[:, :], compare_op=ALU.is_gt, fill=0.0, base=0,
                                     pattern=[[-1, P]], channel_multiplier=1))
                c(pool.memset(G.upto[:, :], 1.0))
                c(pool.affine_select(out=G.upto[:, :], in_=G.upto[:, :], compare_op=ALU.is_ge, fill=0.0, base=0,
                                     pattern=[[1, P]], channel_multiplier=-1))
                c(pool.memset(G.ones[:, :], 1.0))
                c(pool.memset(G.mean[:, :], 1.0 / D))
                c(pool.memset(G.eps[:, :], 1e-5))
                c(pool.iota(G.iota_i[:, :], pattern=[[1, P]], base=0, channel_multiplier=0))
                c(pool.tensor_copy(G.iota[:, :], G.iota_i[:, :]))
                c(pool.memset(G.xT[:, :, N:NC], 0.0))

            @block.sync
            def _(sp):
                sp.dma_start(rows[:, :, :], x.rearrange("(t p) d -> p t d", p=P)).then_inc(loaded, 16)
                sp.wait_ge(loaded, 16)
        rows_to_cols(nc, G, rows, D, G.xT)


def finish(nc, G, out):
    with Stage(nc) as s:
        rows = s.sb("rows", [P, T, D])
        stored = s.sem("stored")
        cols_to_rows(nc, G, G.xT, rows)
        with nc.Block() as block:
            @block.sync
            def _(sp):
                sp.dma_start(out.rearrange("(t p) d -> p t d", p=P), rows[:, :, :]).then_inc(stored, 16)
                sp.wait_ge(stored, 16)


def cols_to_rows(nc, G, src, rows, kb=KD):
    with Stage(nc) as s:
        X = s.sb("X", [128, U, kb, P])
        copied, turned, out_done = [s.sem(x) for x in ("copied", "turned", "out")]
        with nc.Block() as block:
            @block.scalar
            def _(act):
                act.sem_inc(turned, U)
                with act.Fori(0, T // U) as i:
                    for u in range(U):
                        act.wait_ge(turned, i * U + u + 1)
                        act.activation(X[:, u, :, :], src[:, :, ts(i * U + u, P)], ACT.Copy).then_inc(copied, 1)

            @block.tensor
            def _(pe):
                with pe.Fori(0, T // U) as i:
                    for u in range(U):
                        pe.wait_ge(copied, i * U + u + 1)
                        pe.wait_ge(out_done, i * U + u + 1)
                        for m in range(kb):
                            mm = pe.transpose(G.PS[0:P, u, ts(m, 128)], X[:, u, m, :], G.ident[:, :])
                        mm.then_inc(turned, 1)

            @block.vector
            def _(v):
                v.sem_inc(out_done, U)
                with v.Fori(0, T // U) as i:
                    for u in range(U):
                        t = i * U + u
                        v.wait_ge(turned, U + t + 1)
                        v.tensor_copy(rows[:, ts(t, 1), :].rearrange("p a m -> p (a m)"),
                                      G.PS[0:P, u, 0:kb * 128]).then_inc(out_done, 1)


def softmax_gates(nc, G, L, n, top=None):
    with Stage(nc) as s:
        m, z = s.sb("m", [P, T]), s.sb("z", [P, T])
        m2, eq = s.sb("m2", [P, T]), s.sb("eq", [P, T, n])
        fresh, seen, pre, work = s.sb("fresh", [P, T]), s.sb("seen", [P, T]), s.sb("pre", [P, T, n]), s.sb("work", [P, T, n])
        steps, ready, exp_done, mm_done = [s.sem(x) for x in ("steps", "ready", "exp", "mm")]
        bc = lambda a: a[:, :].unsqueeze(2).to_broadcast([P, T, n])

        def first_of(c, v, val, src):
            c(v.tensor_tensor(eq[:, :, :], src, bc(val), ALU.is_equal))
            c(v.memset(seen[:, :], 1.0))
            for e in range(n):
                c(v.tensor_tensor(eq[:, :, e], eq[:, :, e], seen[:, :], ALU.mult))
                c(v.tensor_tensor(seen[:, :], seen[:, :], eq[:, :, e], ALU.subtract))

        with nc.Block() as block:
            @block.vector
            def _(v):
                c = Chain(v, steps)
                c(v.tensor_reduce(m[:, :], L[:, :, :], AX.X, ALU.max))
                v.tensor_tensor(L[:, :, :], L[:, :, :], bc(m), ALU.subtract).then_inc(ready, 1)
                v.wait_ge(exp_done, 1)
                c(v.tensor_reduce(z[:, :], L[:, :, :], AX.X, ALU.add))
                c(v.reciprocal(z[:, :], z[:, :]))
                c(v.tensor_tensor(L[:, :, :], L[:, :, :], bc(z), ALU.mult))
                if top is not None:
                    c(v.tensor_reduce(m[:, :], L[:, :, :], AX.X, ALU.max))
                    first_of(c, v, m, L[:, :, :])
                if top == 2:
                    c(v.tensor_copy(pre[:, :, :], eq[:, :, :]))
                    c(v.scalar_tensor_tensor(out=work[:, :, :], in0=eq[:, :, :], scalar=-4.0, in1=L[:, :, :], op0=ALU.mult, op1=ALU.add))
                    c(v.tensor_reduce(m2[:, :], work[:, :, :], AX.X, ALU.max))
                    first_of(c, v, m2, work[:, :, :])
                    c(v.tensor_tensor(eq[:, :, :], eq[:, :, :], pre[:, :, :], ALU.add))
                    c(v.tensor_tensor(z[:, :], m[:, :], m2[:, :], ALU.add))
                    c(v.reciprocal(z[:, :], z[:, :]))
                    c(v.tensor_tensor(L[:, :, :], L[:, :, :], eq[:, :, :], ALU.mult))
                    c(v.tensor_tensor(L[:, :, :], L[:, :, :], bc(z), ALU.mult))
                if top == 1:
                    room = float(-(-5 * N // (4 * n)))
                    v.sem_inc(ready, 1)
                    v.wait_ge(mm_done, 2)
                    c(v.tensor_copy(work[:, :, :], G.PS[0:P, 1, 0:T * n].rearrange("p (t e) -> p t e", e=n)))
                    for e in range(n):
                        c(v.tensor_tensor_scan(pre[:, :, e], work[:, :, e], G.zero[0:P, 0:T], 0.0, ALU.add, ALU.add))
                    c(v.tensor_tensor(pre[:, :, :], pre[:, :, :], work[:, :, :], ALU.subtract))
                    c(v.tensor_tensor(pre[:, :, :], pre[:, :, :], G.PS[0:P, 0, 0:T * n].rearrange("p (t e) -> p t e", e=n), ALU.add))
                    c(v.tensor_scalar(pre[:, :, :], pre[:, :, :], room, None, ALU.is_le))
                    c(v.tensor_tensor(eq[:, :, :], eq[:, :, :], pre[:, :, :], ALU.mult))
                    c(v.tensor_tensor(L[:, :, :], L[:, :, :], eq[:, :, :], ALU.mult))

            @block.scalar
            def _(act):
                act.wait_ge(ready, 1)
                act.activation(L[:, :, :], L[:, :, :], ACT.Exp).then_inc(exp_done, 1)

            if top == 1:
                @block.tensor
                def _(pe):
                    pe.wait_ge(ready, 2)
                    e_flat = eq[:, :, :].rearrange("p t e -> p (t e)")
                    pe.matmul(G.PS[0:P, 0, 0:T * n], G.upto[:, :], e_flat, start=True, stop=True).then_inc(mm_done, 1)
                    pe.matmul(G.PS[0:P, 1, 0:T * n], G.ones[0:P, 0:P], e_flat, start=True, stop=True).then_inc(mm_done, 1)


def routed_ffn(nc, G, I, wr, br, experts, n, top, func):
    w1, b1, w2, b2, F = experts
    with Stage(nc) as s:
        L = s.sb("L", [P, T, n])
        norm_cols(nc, G, G.xT, G.xn)
        project_rows(nc, G, G.xn, KD, [(wr, 0)], n, L, [(br, 0)] if br is not None else [])
        softmax_gates(nc, G, L, n, top)
        spread_gate(nc, G, L, n, G.gate)
    ffn(nc, G, G.xn, KD, w1, b1, w2, b2, F, func, G.xT, n, G.gate)


def bn_ffn(nc, G, I, out, n_exp=8):
    names = ["W1", "W2", "Wo"]
    vecs = ["b1", "g1", "be1", "m1", "v1", "b2", "g2", "be2", "m2", "v2", "bo"]
    w = [I["L0_ffn_" + x] for x in names]
    with Stage(nc) as s:
        W = [[s.sb(f"W{j}{l}", [128, KD, D]) for l in range(3)] for j in range(2)]
        V = s.sb("V", [128, len(vecs), n_exp * KD])
        SC = s.sb("SC", [128, 2, n_exp * KD])
        SH = s.sb("SH", [128, 2, n_exp * KD])
        eps = s.sb("eps", [128, 1])
        cur = s.sb("cur", [128, 2, 5, KD])
        g_sb = [s.sb(f"g{j}", [128, NC]) for j in range(2)]
        H = [s.sb(f"H{l}", [128, KD, CW]) for l in range(2)]
        Y = s.sb("Y", [128, KD, CW])
        vload, steps, ready, root = [s.sem(x) for x in ("vload", "steps", "ready", "root")]
        loaded = [s.sem(f"loaded{j}") for j in range(2)]
        up_done, h_done, y_mm, y_done, out_done, exp_done, cur_done = [
            s.sem(x) for x in ("up", "h", "ymm", "y", "out", "expert", "cur")]
        at = vecs.index
        with nc.Block() as block:
            @block.sync
            def _(sp):
                for j, name in enumerate(vecs):
                    sp.dma_start(V[:, j, :], I["L0_ffn_" + name].rearrange("e (k p) -> p (e k)", p=128)).then_inc(vload, 16)

            @block.scalar
            def _(act):
                act.wait_ge(ready, 1)
                act.wait_ge(vload, 16 * len(vecs))
                for l in range(2):
                    act.activation(SC[:, l, :], V[:, at(f"v{l + 1}"), :], ACT.Sqrt, bias=eps[:, 0:1]).then_inc(root, 1)

            @block.vector
            def _(v):
                c = Chain(v, steps)
                v.memset(eps[:, :], 0.001).then_inc(ready, 1)
                v.wait_ge(vload, 16 * len(vecs))
                v.wait_ge(root, 2)
                c(v.reciprocal(SC[:, :, :], SC[:, :, :]))
                for l in range(2):
                    a = lambda x: V[:, at(f"{x}{l + 1}"), :]
                    c(v.tensor_tensor(SC[:, l, :], SC[:, l, :], a("g"), ALU.mult))
                    c(v.tensor_tensor(SH[:, l, :], a("b"), a("m"), ALU.subtract))
                    c(v.tensor_tensor(SH[:, l, :], SH[:, l, :], SC[:, l, :], ALU.mult))
                    c(v.tensor_tensor(SH[:, l, :], SH[:, l, :], a("be"), ALU.add))
        with nc.Block() as block:
            @block.sync
            def _(sp):
                sp.sem_inc(exp_done, 2)
                with sp.Fori(0, n_exp // 2) as r:
                    for j in range(2):
                        e = r * 2 + j
                        sp.wait_ge(exp_done, e + 1)
                        for l in range(3):
                            sp.dma_start(W[j][l][:, :, :], w[l][ts(e, 1)].rearrange("a (k p) f -> p (a k) f", p=128)).then_inc(loaded[j], 16)
                        row = G.gate[ts(e, 1)]
                        sp.dma_start(g_sb[j][:, :], bass.AP(row.tensor, row.offset, [[0, 128], [1, NC]])).then_inc(loaded[j], 16)

            @block.tensor
            def _(pe):
                with pe.Fori(0, n_exp // 2) as r:
                    for j in range(2):
                        with pe.Fori(0, NCH) as c:
                            n = (r * 2 + j) * NCH + c
                            pe.wait_ge(loaded[j], (r + 1) * 64)
                            for l in range(3):
                                if l == 0:
                                    pe.wait_ge(h_done, n * 4 + 2)
                                elif l == 1:
                                    pe.wait_ge(h_done, n * 4 + 4)
                                else:
                                    pe.wait_ge(y_done, n + 1)
                                for k in range(KD):
                                    if l:
                                        pe.wait_ge(h_done, 4 + n * 4 + 2 * (l - 1) + k + 1)
                                    rhs = H[l - 1][:, k, :] if l else G.xn[:, k, ts(c, CW)]
                                    for m in range(KD):
                                        mm = pe.matmul(G.PS[:, 2 * l + m, 0:CW], W[j][l][:, k, ts(m, 128)], rhs,
                                                       start=(k == 0), stop=(k == KD - 1))
                                        if k == KD - 1:
                                            mm.then_inc(up_done if l < 2 else y_mm, 1)

            @block.scalar
            def _(act):
                act.sem_inc(h_done, 4)
                with act.Fori(0, n_exp // 2) as r:
                    for j in range(2):
                        with act.Fori(0, NCH) as c:
                            n = (r * 2 + j) * NCH + c
                            act.wait_ge(cur_done, r * 2 + j + 1)
                            for l in range(2):
                                for m in range(KD):
                                    act.wait_ge(up_done, n * 4 + 2 * l + m + 1)
                                    if l == 0:
                                        act.wait_ge(up_done, n * 4 + 1)
                                    act.activation(H[l][:, m, :], G.PS[:, 2 * l + m, 0:CW], ACT.Relu,
                                                   scale=cur[:, j, l, m:m + 1], bias=cur[:, j, 2 + l, m:m + 1]).then_inc(h_done, 1)

            @block.vector
            def _(v):
                v.sem_inc(y_done, 1)
                with v.Fori(0, n_exp // 2) as r:
                    for j in range(2):
                        e = r * 2 + j
                        for l in range(2):
                            v.tensor_copy(cur[:, j, l, :], SC[:, l, ts(e, KD)])
                            v.tensor_copy(cur[:, j, 2 + l, :], SH[:, l, ts(e, KD)])
                        v.tensor_copy(cur[:, j, 4, :], V[:, at("bo"), ts(e, KD)]).then_inc(cur_done, 1)
                        with v.Fori(0, NCH) as c:
                            n = e * NCH + c
                            v.wait_ge(cur_done, e + 1)
                            v.wait_ge(loaded[j], (r + 1) * 64)
                            v.wait_ge(y_mm, (n + 1) * 2)
                            for o in range(KD):
                                ins = v.scalar_tensor_tensor(out=Y[:, o, :], in0=G.PS[:, 4 + o, 0:CW], scalar=cur[:, j, 4, o:o + 1],
                                                             in1=g_sb[j][:, ts(c, CW)], op0=ALU.add, op1=ALU.mult)
                            ins.then_inc(y_done, 1)
                            v.wait_ge(y_done, n + 2)
                            v.tensor_tensor(out[:, :, ts(c, CW)], out[:, :, ts(c, CW)], Y[:, :, :], ALU.add).then_inc(out_done, 1)
                            v.wait_ge(out_done, n + 1)
                        v.sem_inc(exp_done, 1)


def rank(nc, G, key, key_row, dst):
    with Stage(nc) as s:
        row, junk = s.sb("row", [P, N]), s.sb("junk", [P, N])
        part = s.sb("part", [P, 4, T])
        stored, loaded, steps, done = [s.sem(x) for x in ("stored", "loaded", "steps", "done")]
        turned = s.sem("turned")
        kr = s.sb("kr", [T, P])
        with nc.Block() as block:
            @block.tensor
            def _(pe):
                pe.transpose(G.PS[0:T, 0, 0:P], key[:, :], G.ident[0:P, 0:P]).then_inc(turned, 1)

            @block.sync
            def _(sp):
                sp.wait_ge(steps, 1)
                sp.dma_start(key_row.rearrange("(t p) -> t p", p=P), kr[:, :]).then_inc(stored, 16)
                sp.wait_ge(stored, 16)
                sp.dma_start(row[:, :], over(key_row, P)).then_inc(loaded, 16)

            @block.vector
            def _(v):
                v.wait_ge(turned, 1)
                v.tensor_copy(kr[:, :], G.PS[0:T, 0, 0:P]).then_inc(steps, 1)
                v.memset(part[:, :, :], 0.0).then_inc(steps, 1)
                v.wait_ge(steps, 2)
                v.wait_ge(loaded, 16)
                c = Chain(v, done)
                for t in range(T):
                    k = key[:, t:t + 1]
                    a, b = t * P, (t + 1) * P
                    if t > 0:
                        c(v.tensor_scalar(junk[:, 0:a], row[:, 0:a], k, 0.0, ALU.is_le, ALU.add, accum_out=part[:, 0, t:t + 1]))
                    if t < T - 1:
                        c(v.tensor_scalar(junk[:, b:N], row[:, b:N], k, 0.0, ALU.is_lt, ALU.add, accum_out=part[:, 1, t:t + 1]))
                    c(v.tensor_scalar(junk[:, a:b], row[:, a:b], k, 0.0, ALU.is_lt, ALU.add, accum_out=part[:, 2, t:t + 1]))
                    c(v.scalar_tensor_tensor(out=junk[:, a:b], in0=row[:, a:b], scalar=k, in1=G.after[:, :],
                                             op0=ALU.is_equal, op1=ALU.mult, accum_out=part[:, 3, t:t + 1]))
                c(v.tensor_tensor(part[:, 0:2, :], part[:, 0:2, :], part[:, 2:4, :], ALU.add))
                c(v.tensor_tensor(dst[:, :], part[:, 0, :], part[:, 1, :], ALU.add))


def vec_steps(nc, fn):
    with Stage(nc) as s:
        steps = s.sem("steps")
        with nc.Block() as block:
            @block.vector
            def _(v):
                fn(Chain(v, steps), v)


def top_k_ffn(nc, G, I):
    kept = N // 2 - 1
    with Stage(nc) as s:
        L, R = s.sb("L", [P, T, 1]), s.sb("R", [P, T])
        flat = L[:, :, :].rearrange("p t a -> p (t a)")
        neg = s.sb("neg", [P, T])
        norm_cols(nc, G, G.xT, G.xn)
        project_rows(nc, G, G.xn, KD, [(I["L2_ffn_wr"], 0)], 1, L, [(I["L2_ffn_br"], 0)])
        vec_steps(nc, lambda c, v: c(v.tensor_scalar(neg[:, :], flat, -1.0, None, ALU.mult)))
        rank(nc, G, neg, G.key_row, R)

        def steps(c, v):
            c(v.tensor_scalar(R[:, :], R[:, :], float(kept), None, ALU.is_lt))
            c(v.tensor_tensor(flat, flat, R[:, :], ALU.mult))
        vec_steps(nc, steps)
        spread_gate(nc, G, L, 1, G.gate)
    one = lambda a: I["L2_ffn_" + a].rearrange("(a k) f -> a k f" if a[0] == "w" else "(a f) -> a f", a=1)
    ffn(nc, G, G.xn, KD, one("w1"), one("b1"), one("w2"), one("b2"), 1024, ACT.Gelu_apprx_tanh, G.xT, 1, G.gate)
    add_cols(nc, flat3(G.xT), flat3(G.xn))


def elu_like(nc, x, n, plus_one):
    p = x.shape[0]
    with Stage(nc) as s:
        m = s.sb("m", [p, n])
        low, e = s.sem("low"), s.sem("exp")
        steps = s.sem("steps")
        with nc.Block() as block:
            @block.vector
            def _(v):
                v.tensor_scalar(m[:, :], x, 0.0, None, ALU.min).then_inc(low, 1)
                v.wait_ge(e, 1)
                if plus_one:
                    v.scalar_tensor_tensor(out=x, in0=x, scalar=0.0, in1=m[:, :], op0=ALU.max, op1=ALU.add).then_inc(steps, 1)
                else:
                    v.tensor_scalar(m[:, :], m[:, :], -1.0, None, ALU.add).then_inc(steps, 1)
                    v.wait_ge(steps, 1)
                    v.scalar_tensor_tensor(out=x, in0=x, scalar=0.0, in1=m[:, :], op0=ALU.max, op1=ALU.add).then_inc(steps, 1)

            @block.scalar
            def _(act):
                act.wait_ge(low, 1)
                act.activation(m[:, :], m[:, :], ACT.Exp).then_inc(e, 1)


def outer_sums(nc, G, Kr, Vr, dst, ksum=None, kb=KD, extra=None, scale=1.0):
    with Stage(nc) as s:
        X = s.sb("X", [P, U, kb * 128])
        Z = s.sb("Z", [P, 128])
        S = s.sb("S", [128, kb])
        zeroed, copied, mm_done, all_done, steps = [s.sem(x) for x in ("zeroed", "copied", "mm", "all", "steps")]
        with nc.Block() as block:
            @block.gpsimd
            def _(pool):
                pool.memset(Z[:, :], 0.0).then_inc(zeroed, 1)

            @block.scalar
            def _(act):
                act.sem_inc(mm_done, U)
                with act.Fori(0, T // U) as i:
                    for u in range(U):
                        act.wait_ge(mm_done, i * U + u + 1)
                        act.activation(X[:, u, :], Kr[:, ts(i * U + u, 1), :].rearrange("p a m -> p (a m)"), ACT.Copy).then_inc(copied, 1)

            @block.tensor
            def _(pe):
                pe.wait_ge(zeroed, 1)
                for b in range(kb):
                    pe.matmul(G.PS[:, b, 0:128], Z[:, :], Z[:, :], start=True, stop=False, skip_group_check=True)
                    pe.matmul(G.PS[:, 2 + b, 0:1], Z[:, :], Z[:, 0:1], start=True, stop=False, skip_group_check=True)
                with pe.Fori(0, T // U) as i:
                    for u in range(U):
                        pe.wait_ge(copied, i * U + u + 1)
                        for b in range(kb):
                            pe.matmul(G.PS[:, b, 0:128], X[:, u, ts(b, 128)],
                                      Vr[:, ts(i * U + u, 1), ts(b, 128)].rearrange("p a m -> p (a m)"),
                                      start=False, stop=False, skip_group_check=True)
                            mm = pe.matmul(G.PS[:, 2 + b, 0:1], X[:, u, ts(b, 128)], G.ones[0:P, 0:1],
                                           start=False, stop=False, skip_group_check=True)
                        mm.then_inc(mm_done, 1)
                if extra is not None:
                    K2, V2 = extra
                    n = K2.shape[0]
                    for b in range(kb):
                        pe.matmul(G.PS[:, b, 0:128], K2[:, ts(b, 128)], V2[:, ts(b, 128)], start=False, stop=False, skip_group_check=True)
                        pe.matmul(G.PS[:, 2 + b, 0:1], K2[:, ts(b, 128)], G.ones[0:n, 0:1], start=False, stop=False, skip_group_check=True)
                for b in range(kb):
                    pe.matmul(G.PS[:, b, 0:128], Z[:, :], Z[:, :], start=False, stop=True, skip_group_check=True)
                    mm = pe.matmul(G.PS[:, 2 + b, 0:1], Z[:, :], Z[:, 0:1], start=False, stop=True, skip_group_check=True)
                mm.then_inc(all_done, 1)

            @block.vector
            def _(v):
                v.wait_ge(all_done, 1)
                c = Chain(v, steps)
                for b in range(kb):
                    c(v.scalar_tensor_tensor(out=dst[:, b, :], in0=G.PS[:, b, 0:128], scalar=scale, in1=G.blockmask[:, :],
                                             op0=ALU.mult, op1=ALU.mult))
                    if ksum is not None:
                        c(v.tensor_copy(S[:, b:b + 1], G.PS[:, 2 + b, 0:1]))
                        c(v.tensor_scalar(ksum[:, b, :], G.blockmask[:, :], S[:, b:b + 1], None, ALU.mult))


def attend_cols(nc, G, q, kv, ksum, out, kb=KD):
    with Stage(nc) as s:
        den = s.sb("den", [128, kb, CW])
        num_done, steps, out_done = [s.sem(x) for x in ("num", "steps", "out")]
        with nc.Block() as block:
            @block.tensor
            def _(pe):
                with pe.Fori(0, NCH) as i:
                    pe.wait_ge(out_done, i + 1)
                    for b in range(kb):
                        mm = pe.matmul(G.PS[:, b, 0:CW], kv[:, b, :], q[:, b, ts(i, CW)], start=True, stop=True)
                        if ksum is not None:
                            mm = pe.matmul(G.PS[:, 2 + b, 0:CW], ksum[:, b, :], q[:, b, ts(i, CW)], start=True, stop=True)
                    mm.then_inc(num_done, 1)

            @block.vector
            def _(v):
                v.sem_inc(out_done, 1)
                with v.Fori(0, NCH) as i:
                    v.wait_ge(num_done, i + 1)
                    if ksum is not None:
                        c = Chain(v, steps, i * 2)
                        c(v.tensor_scalar(den[:, :, :], G.PS[:, 2:2 + kb, 0:CW], 1e-6, None, ALU.add))
                        c(v.reciprocal(den[:, :, :], den[:, :, :]))
                        v.tensor_tensor(out[:, :, ts(i, CW)], G.PS[:, 0:kb, 0:CW], den[:, :, :], ALU.mult).then_inc(out_done, 1)
                    else:
                        v.tensor_copy(out[:, :, ts(i, CW)], G.PS[:, 0:kb, 0:CW]).then_inc(out_done, 1)


flat3 = lambda a: a[:, :, :].rearrange("p a b -> p (a b)")


def copy_cols(nc, dst, src):
    vec_steps(nc, lambda c, v: c(v.tensor_copy(dst, src)))


def add_cols(nc, dst, src):
    vec_steps(nc, lambda c, v: c(v.tensor_tensor(dst, dst, src, ALU.add)))


def linear_attention(nc, G, wq, wk, wv, bq, bk, bv, q):
    dense_cols(nc, G, G.xn, KD, wq, KD, q, bias=bq)
    elu_like(nc, flat3(q), KD * NC, True)
    with Stage(nc) as s:
        kv, ks = s.sb("kv", [128, KD, 128]), s.sb("ks", [128, KD, 128])
        with Stage(nc) as s2:
            Kr, Vr = s2.sb("Kr", [P, T, D]), s2.sb("Vr", [P, T, D])
            project_rows(nc, G, G.xn, KD, [(wk, 0)], D, Kr, [(bk, 0)] if bk is not None else [])
            project_rows(nc, G, G.xn, KD, [(wv, 0)], D, Vr, [(bv, 0)] if bv is not None else [])
            elu_like(nc, flat3(Kr), T * D, True)
            outer_sums(nc, G, Kr, Vr, kv, ks)
        attend_cols(nc, G, q, kv, ks, q)


def mask_stage(nc, G):
    with Stage(nc) as s:
        ix = s.sb("ix", [128, CHAINS, 4], I32)
        copied, rounds, scattered = [s.sem(x) for x in ("copied", "rounds", "scattered")]
        with nc.Block() as block:
            @block.gpsimd
            def _(pool):
                edge_mask(pool, G, ix, copied, rounds, scattered)


def mask_keys(nc, G):
    with Stage(nc) as s:
        key, spare, none = [s.sb(x, [128, ET]) for x in ("key", "spare", "none")]
        ed, spare_i = s.sb("ed", [128, 2, ET]), s.sb("spare_i", [128, ET], I32)
        made, steps = s.sem("made"), s.sem("steps")
        with nc.Block() as block:
            @block.gpsimd
            def _(pool):
                pool.iota(spare_i[:, :], pattern=[[128, CHAINS], [0, ET // CHAINS]], base=N * N, channel_multiplier=1).then_inc(made, 1)

            @block.vector
            def _(v):
                c = Chain(v, steps)
                v.wait_ge(made, 1)
                c(v.tensor_copy(spare[:, :], spare_i[:, :]))
                for j in range(2):
                    c(v.tensor_copy(ed[:, j, :], G.edges[:, :, j]))
                c(v.scalar_tensor_tensor(out=key[:, :], in0=ed[:, 1, :], scalar=float(N), in1=ed[:, 0, :], op0=ALU.mult, op1=ALU.add))
                c(v.tensor_scalar(none[:, :], G.edges[:, :, 2:3].bitcast(F32).rearrange("p j a -> p (j a)"), 0.0, None, ALU.is_lt))
                c(v.tensor_tensor(spare[:, :], spare[:, :], none[:, :], ALU.mult))
                c(v.tensor_tensor(key[:, :], key[:, :], spare[:, :], ALU.add))
                c(v.tensor_copy(G.keys[:, :], key[:, :]))


def fill_mask(nc, G):
    with Stage(nc) as s:
        low = s.sb("low", [P, N], BF16)
        made, stored = s.sem("made"), s.sem("stored")
        with nc.Block() as block:
            @block.gpsimd
            def _(pool):
                pool.memset(low[:, :], NEG).then_inc(made, 1)

            @block.sync
            def _(sp):
                sp.wait_ge(made, 1)
                mask = G.mask[0:N * N].rearrange("(n m) a -> n (m a)", m=N)
                with sp.Fori(0, T) as t:
                    sp.dma_start(mask[ts(t, P), :], low[:, :]).then_inc(stored, 16)
                sp.wait_ge(stored, 16 * T)


def one_ffn(nc, G, src, kc, w1, b1, w2, b2, F, func, out):
    a3 = lambda a: a.rearrange("(a k) f -> a k f", a=1)
    a2 = lambda a: a.rearrange("(a f) -> a f", a=1)
    ffn(nc, G, src, kc, a3(w1), a2(b1), a3(w2), a2(b2), F, func, out, 1, None)


def mix0(nc, G, I):
    p = lambda n: I["L0_mix_" + n]
    with Stage(nc) as s:
        a, b = s.sb("a", [128, KD, NC]), s.sb("b", [128, KD, NC])
        linear_attention(nc, G, p("Wq"), p("Wk"), p("Wv"), p("bq"), p("bk"), p("bv"), a)
        copy_cols(nc, flat3(b), flat3(G.xn))
        dense_cols(nc, G, a, KD, p("Wo"), KD, b, bias=p("bo"), add=True)
        norm_cols(nc, G, b, b, gain=p("ln1_g"), shift=p("ln1_b"))
        copy_cols(nc, flat3(a), flat3(b))
        one_ffn(nc, G, b, KD, p("W1"), p("b1"), p("W2"), p("b2"), 1024, ACT.Relu, a)
        norm_cols(nc, G, a, G.xT, gain=p("ln2_g"), shift=p("ln2_b"), add=G.xT)


def mix1(nc, G, I):
    p = lambda n: I["L1_mix_" + n].rearrange("h a c -> (h a c)")
    HG = T * 8
    with Stage(nc) as s:
        kv, o = s.sb("kv", [128, KD, 128]), s.sb("o", [128, KD, NC])
        with Stage(nc) as s2:
            R, sq = s2.sb("R", [P, T, D]), s2.sb("sq", [P, T, D])
            wb = s2.sb("wb", [P, 4, D])
            st = s2.sb("st", [P, HG])
            loaded, steps, ready, root = [s2.sem(x) for x in ("loaded", "steps", "ready", "root")]
            cols_to_rows(nc, G, G.xn, R)
            g3 = lambda a: a[:, :, :].rearrange("p t (h c) -> p (t h) c", c=32)
            bc = st[:, :].unsqueeze(2).to_broadcast([P, HG, 32])
            row = lambda j: wb[:, j:j + 1, :].to_broadcast([P, T, D])
            with nc.Block() as block:
                @block.sync
                def _(sp):
                    for j, name in enumerate(("kln_weight", "kln_bias", "vln_weight", "vln_bias")):
                        sp.dma_start(wb[:, j, :], over(p(name), P)).then_inc(loaded, 16)

                @block.vector
                def _(v):
                    c = Chain(v, steps)
                    c(v.tensor_reduce(st[:, :], g3(R), AX.X, ALU.add))
                    c(v.tensor_scalar(st[:, :], st[:, :], 1.0 / 32, None, ALU.mult))
                    c(v.tensor_tensor(g3(R), g3(R), bc, ALU.subtract))
                    c(v.tensor_tensor(sq[:, :, :], R[:, :, :], R[:, :, :], ALU.mult))
                    v.tensor_reduce(st[:, :], g3(sq), AX.X, ALU.add).then_inc(ready, 1)
                    v.wait_ge(root, 1)
                    c(v.tensor_scalar(st[:, :], st[:, :], 1e-5, None, ALU.add))
                    c(v.reciprocal(st[:, :], st[:, :]))
                    c(v.tensor_tensor(g3(R), g3(R), bc, ALU.mult))
                    v.wait_ge(loaded, 64)
                    c(v.tensor_tensor(sq[:, :, :], R[:, :, :], row(2), ALU.mult))
                    c(v.tensor_tensor(sq[:, :, :], sq[:, :, :], row(3), ALU.add))
                    c(v.tensor_tensor(R[:, :, :], R[:, :, :], row(0), ALU.mult))
                    c(v.tensor_tensor(R[:, :, :], R[:, :, :], row(1), ALU.add))

                @block.scalar
                def _(act):
                    act.wait_ge(ready, 1)
                    act.activation(st[:, :], st[:, :], ACT.Sqrt, scale=1.0 / 31).then_inc(root, 1)
            outer_sums(nc, G, R, sq, kv, scale=1.0 / N)
        attend_cols(nc, G, G.xn, kv, None, o)
        add_cols(nc, flat3(o), flat3(G.xn))
        add_cols(nc, flat3(G.xT), flat3(o))


def mix2(nc, G, I):
    p = lambda n: I["L2_mix_" + n]
    HID = 128
    with Stage(nc) as s:
        q = s.sb("q", [128, 1, NC])
        ctxm = s.sb("ctxm", [128, 1, 128])
        xr = s.sb("xr", [128, KD, NC])
        norm_cols(nc, G, G.xn, xr, gain=p("g_pre"), rms=True)
        with Stage(nc) as s2:
            R = s2.sb("R", [P, T, 3 * HID])
            sums = s2.sb("sums", [128, 1, 128])
            top, part, wide = s2.sb("top", [P, HID]), s2.sb("part", [128, 1]), s2.sb("wide", [P, HID])
            mem = s2.sb("mem", [4, 2, HID])
            topc, tr = s2.sb("topc", [HID, 1]), s2.sb("tr", [HID, HID])
            hm = s2.sb("hm", [P, T * 4])
            loaded, steps, turned, exp_done, ready, spread = [
                s2.sem(x) for x in ("loaded", "steps", "turned", "exp", "ready", "spread")]
            project_rows(nc, G, xr, KD, [(p("w_qkv"), 0)], 3 * HID, R)
            qv = R[:, :, 0:HID].rearrange("p t (h c) -> p t h c", c=32)
            kv_, K = R[:, :, HID:2 * HID], R[:, :, HID:2 * HID]
            hm4 = hm[:, :].rearrange("p (t h) -> p t h", h=4)
            with nc.Block() as block:
                @block.sync
                def _(sp):
                    for j in range(2):
                        sp.dma_start(mem[:, j, :], p("mem_kv")[j].rearrange("h d n -> n (h d)")).then_inc(loaded, 16)

                @block.vector
                def _(v):
                    c = Chain(v, steps)
                    c(v.tensor_reduce(hm4, qv, AX.X, ALU.max))
                    for h in range(4):
                        c(v.tensor_tensor(qv[:, :, h, :], qv[:, :, h, :], hm4[:, :, h:h + 1].to_broadcast([P, T, 32]), ALU.subtract))
                    c(v.tensor_reduce(top[:, :], K.rearrange("p t c -> p c t"), AX.X, ALU.max))
                    v.wait_ge(loaded, 32)
                    c(v.tensor_tensor(top[0:4, :], top[0:4, :], mem[:, 0, :], ALU.max))
                    v.sem_inc(ready, 1)
                    v.wait_ge(turned, 1)
                    c(v.tensor_reduce(topc[:, :], G.PS[:, 0, 0:P], AX.X, ALU.max))
                    c(v.tensor_scalar(tr[:, :], G.ident[:, :], topc[:, 0:1], None, ALU.mult))
                    v.sem_inc(ready, 1)
                    v.wait_ge(turned, 2)
                    c(v.tensor_copy(wide[:, :], G.PS[0:P, 1, 0:HID]))
                    c(v.tensor_tensor(K, K, wide[:, :].unsqueeze(1).to_broadcast([P, T, HID]), ALU.subtract))
                    c(v.tensor_tensor(mem[:, 0, :], mem[:, 0, :], wide[0:4, :], ALU.subtract))
                    v.sem_inc(ready, 1)
                    v.wait_ge(exp_done, 3)
                    c(v.tensor_reduce(hm4, qv, AX.X, ALU.add))
                    c(v.reciprocal(hm[:, :], hm[:, :]))
                    c(v.tensor_scalar(hm[:, :], hm[:, :], 32.0 ** -0.5, None, ALU.mult))
                    for h in range(4):
                        c(v.tensor_tensor(qv[:, :, h, :], qv[:, :, h, :], hm4[:, :, h:h + 1].to_broadcast([P, T, 32]), ALU.mult))

                @block.tensor
                def _(pe):
                    pe.wait_ge(ready, 1)
                    pe.transpose(G.PS[:, 0, 0:P], top[:, :], G.ident[0:P, 0:P]).then_inc(turned, 1)
                    pe.wait_ge(ready, 2)
                    pe.matmul(G.PS[:, 1, 0:HID], G.ones[:, :], tr[:, :], start=True, stop=True).then_inc(turned, 1)

                @block.scalar
                def _(act):
                    act.wait_ge(ready, 3)
                    act.activation(R[:, :, 0:HID], R[:, :, 0:HID], ACT.Exp).then_inc(exp_done, 1)
                    act.activation(K, K, ACT.Exp).then_inc(exp_done, 1)
                    act.activation(mem[:, 0, :], mem[:, 0, :], ACT.Exp).then_inc(exp_done, 1)
            outer_sums(nc, G, R[:, :, HID:2 * HID], R[:, :, 2 * HID:3 * HID], ctxm, sums, kb=1,
                       extra=(mem[:, 0, :], mem[:, 1, :]))

            def divide(c, v):
                c(v.tensor_reduce(part[:, :], sums[:, 0, :], AX.X, ALU.max))
                c(v.reciprocal(part[:, :], part[:, :]))
                c(v.tensor_scalar(ctxm[:, 0, :], ctxm[:, 0, :], part[:, 0:1], None, ALU.mult))
                c(v.memset(q[:, :, N:NC], 0.0))
            vec_steps(nc, divide)
            rows_to_cols(nc, G, R[:, :, 0:HID], HID, q)
        attend_cols(nc, G, q, ctxm, None, q, kb=1)
        y = xr
        dense_cols(nc, G, q, 1, p("w_out"), KD, y, bias=p("b_out"))
        norm_cols(nc, G, y, y, gain=p("g_out"), rms=True)
        add_cols(nc, flat3(G.xT), flat3(y))
        add_cols(nc, flat3(G.xT), flat3(G.xn))


def mix3(nc, G, I):
    p = lambda n: I["L3_mix_" + n]
    with Stage(nc) as s:
        q = s.sb("q", [128, KD, NC])
        linear_attention(nc, G, p("Wq"), p("Wk"), p("Wv"), None, None, None, q)
        cat = s.sb("cat", [128, 4, NC])
        msg = cat[:, 2:4, :]
        dense_cols(nc, G, q, KD, p("Wm"), KD, msg)
        norm_cols(nc, G, msg, msg, gain=p("g1"), shift=p("b1"))
        copy_cols(nc, cat[:, 0:2, :], G.xn[:, :, :])
        def clear(c, v):
            c(v.memset(q[:, :, :], 0.0))
            c(v.memset(zb[:, :], 0.0))
        zb = s.sb("zb", [1, 512])
        vec_steps(nc, clear)
        with Stage(nc) as s2:
            done = s2.sem("done")
            with nc.Block() as block:
                @block.sync
                def _(sp):
                    sp.dma_start(G.zeros_row.rearrange("(a n) -> a n", a=1), zb[:, :]).then_inc(done, 16)
                    sp.wait_ge(done, 16)
        one_ffn(nc, G, cat, 4, p("W1"), G.zeros_row, p("W2"), G.zeros_row[0:D], 512, ACT.Relu, q)
        norm_cols(nc, G, q, G.xT, gain=p("g2"), shift=p("b2"), add=G.xT)
        add_cols(nc, flat3(G.xT), flat3(G.xn))


def sort_edges(nc, G, I):
    with Stage(nc) as s:
        raw = s.sb("raw", [P, 2, EF], I32)
        val, hi, lo = s.sb("val", [P, 2, EF]), s.sb("hi", [P, 2, EF]), s.sb("lo", [P, 2, EF])
        rows = s.sb("rows", [P, EF, 4], I32)
        mask, scan, place = s.sb("mask", [P, EF]), s.sb("scan", [P, EF]), s.sb("place", [P, EF])
        zero = s.sb("zero", [P, EF])
        cnt, base = s.sb("cnt", [P, T]), s.sb("base", [P, T])
        tot, tot_i = s.sb("tot", [P, T]), s.sb("tot_i", [P, T], I32)
        ends = s.sb("ends", [P, T])
        place_i, low_i = s.sb("place_i", [P, EF], I32), s.sb("low_i", [P, EF], I32)
        tile_no, tile_i = s.sb("tile_no", [1, ET]), s.sb("tile_i", [1, ET], I32)
        bucket_f = s.sb("bucket_f", [1, ET])
        fill = s.sb("fill", [128, ET, 4], I32)
        loaded, steps, counted, base_done, made, filled, rank_steps, first = [
            s.sem(x) for x in ("loaded", "steps", "counted", "base", "made", "filled", "rank_steps", "first")]
        last_steps, order = s.sem("last_steps"), s.sem("order")
        with nc.Block() as block:
            @block.sync
            def _(sp):
                for j, name in enumerate(("src", "dst")):
                    sp.dma_start(raw[:, j, :], I[name].rearrange("(p f) -> p f", p=P)).then_inc(loaded, 16)
                sp.wait_ge(made, 4)
                sp.dma_start(G.sorted.rearrange("(p j) w -> p j w", p=128), fill[:, :, :]).then_inc(filled, 16)
                sp.wait_ge(filled, 16)

            @block.gpsimd
            def _(pool):
                pool.memset(fill[:, :, :], 0).then_inc(made, 1)
                pool.wait_ge(made, 1)
                pool.memset(fill[:, :, 2:3].bitcast(F32), -1.0).then_inc(made, 1)
                pool.iota(tile_i[:, :], pattern=[[1, ET]], base=0, channel_multiplier=0).then_inc(made, 1)
                pool.wait_ge(made, 3)
                pool.tensor_copy(tile_no[:, :], tile_i[:, :]).then_inc(made, 1)

            @block.vector
            def _(v):
                c = Chain(v, steps)
                c(v.memset(hi[:, :, :], 0.0))
                c(v.memset(zero[:, :], 0.0))
                v.wait_ge(loaded, 32)
                c(v.tensor_copy(val[:, :, :], raw[:, :, :]))
                for b in range(1, T):
                    c(v.scalar_tensor_tensor(out=hi[:, :, :], in0=val[:, :, :], scalar=float(P * b), in1=hi[:, :, :],
                                             op0=ALU.is_ge, op1=ALU.add))
                c(v.scalar_tensor_tensor(out=lo[:, :, :], in0=hi[:, :, :], scalar=-float(P), in1=val[:, :, :],
                                         op0=ALU.mult, op1=ALU.add))
                c(v.memset(rows[:, :, :], 0))
                for j in range(2):
                    c(v.tensor_copy(rows[:, :, j], raw[:, j, :]))
                c(v.tensor_copy(rows[:, :, 2:3].bitcast(F32).rearrange("p f a -> p (f a)"), lo[:, 1, :]))
                c(v.memset(place[:, :], 0.0))
        with nc.Block() as block:
            @block.vector
            def _(v):
                with v.Fori(0, T) as b:
                    c = Chain(v, rank_steps, b * 5)
                    c(v.tensor_scalar(mask[:, :], hi[:, 1, :], G.iota[0:P, ts(b, 1)], None, ALU.is_equal))
                    c(v.tensor_tensor_scan(scan[:, :], mask[:, :], zero[:, :], 0.0, ALU.add, ALU.add))
                    c(v.tensor_copy(cnt[:, ts(b, 1)], scan[:, EF - 1:EF]))
                    c(v.tensor_tensor(scan[:, :], scan[:, :], mask[:, :], ALU.mult))
                    c(v.tensor_tensor(place[:, :], place[:, :], scan[:, :], ALU.add))
                v.sem_inc(counted, 1)
                v.wait_ge(base_done, 2)
                c = Chain(v, first)
                c(v.tensor_scalar(tot[:, :], G.PS[0:P, 1, 0:T], 127.0, None, ALU.add))
                c(v.tensor_copy(tot_i[:, :], tot[:, :]))
                c(v.tensor_scalar(tot_i[:, :], tot_i[:, :], 7, None, ALU.arith_shift_right))
                c(v.tensor_copy(tot[:, :], tot_i[:, :]))
                c(v.tensor_tensor_scan(ends[:, :], tot[:, :], zero[:, 0:T], 0.0, ALU.add, ALU.add))
                c(v.tensor_tensor(base[:, :], ends[:, :], tot[:, :], ALU.subtract))
                c(v.tensor_scalar(base[:, :], base[:, :], 128.0, -1.0, ALU.mult, ALU.add))
                c(v.tensor_tensor(base[:, :], base[:, :], G.PS[0:P, 0, 0:T], ALU.add))
                c(v.memset(bucket_f[:, :], 0.0))
                for b in range(T - 1):
                    c(v.scalar_tensor_tensor(out=bucket_f[:, :], in0=tile_no[:, :], scalar=ends[0:1, b:b + 1], in1=bucket_f[:, :],
                                             op0=ALU.is_ge, op1=ALU.add))
                c(v.tensor_copy(G.bucket[:, :], bucket_f[:, :]))
                with v.Fori(0, T) as b:
                    c = Chain(v, last_steps, b * 2)
                    c(v.tensor_scalar(mask[:, :], hi[:, 1, :], G.iota[0:P, ts(b, 1)], base[:, ts(b, 1)], ALU.is_equal, ALU.mult))
                    c(v.tensor_tensor(place[:, :], place[:, :], mask[:, :], ALU.add))
                c = Chain(v, order)
                c(v.tensor_copy(place_i[:, :], place[:, :]))
                c(v.tensor_scalar(low_i[:, :], place_i[:, :], 127, None, ALU.bitwise_and))
                c(v.tensor_scalar(place_i[:, :], place_i[:, :], 7, None, ALU.arith_shift_right))
                c(v.tensor_copy(mask[:, :], low_i[:, :]))
                c(v.tensor_copy(scan[:, :], place_i[:, :]))
                c(v.scalar_tensor_tensor(out=place[:, :], in0=mask[:, :], scalar=float(ET), in1=scan[:, :], op0=ALU.mult, op1=ALU.add))
                c(v.tensor_copy(place_i[:, :], place[:, :]))

            @block.tensor
            def _(pe):
                pe.wait_ge(counted, 1)
                pe.matmul(G.PS[0:P, 0, 0:T], G.before[:, :], cnt[:, :], start=True, stop=True).then_inc(base_done, 1)
                pe.matmul(G.PS[0:P, 1, 0:T], G.ones[0:P, 0:P], cnt[:, :], start=True, stop=True).then_inc(base_done, 1)
        SB = 10
        with Stage(nc) as s2:
            ix = [s2.sb(f"ix{j}", [P, SB], I32) for j in range(2)]
            row = [s2.sb(f"row{j}", [P, SB, 4], I32) for j in range(2)]
            rounds = s2.sem("rounds")
            copied, scattered, fetched = s2.sem("copied"), [s2.sem("scattered0"), s2.sem("scattered1")], s2.sem("fetched")
            oh_lo = [s2.sb(f"oh_lo{j}", [P, 2, 8, P], BF16) for j in range(2)]
            oh_hi = [s2.sb(f"oh_hi{j}", [P, 2, 8, T], BF16) for j in range(2)]
            Z = s2.sb("Z", [P, P], BF16)
            zeroed, hot, counted2, deg_done, deg_out = [s2.sem(x) for x in ("zeroed", "hot", "counted2", "deg", "degout")]
            with nc.Block() as block:
                @block.gpsimd
                def _(pool):
                    with pool.Fori(0, EF // (2 * SB)) as i:
                        for j in range(2):
                            g = i * 2 + j
                            pool.tensor_copy(ix[j][:, :], place_i[:, ts(g, SB)]).then_inc(copied, 1)
                            pool.tensor_copy(row[j][:, :, :], rows[:, ts(g, SB), :]).then_inc(copied, 1)
                            pool.wait_ge(copied, g * 2 + 2)
                            pool.sem_inc(rounds, 1)
                            for f in range(SB):
                                pool.indirect_dma_start(G.sorted[:, :], bass.IndirectOffsetOnAxis(ap=ix[j][:, f:f + 1], axis=0),
                                                        row[j][:, f, :], None).then_inc(scattered[j], 16)
                        for j in range(2):
                            pool.wait_ge(scattered[j], (i + 1) * 16 * SB)
                    pool.dma_start(G.edges[:, :, :], G.sorted.rearrange("(p j) w -> p j w", p=128)).then_inc(fetched, 16)
                    pool.wait_ge(fetched, 16)

                @block.vector
                def _(v):
                    v.memset(Z[:, :], 0.0).then_inc(zeroed, 1)
                    v.sem_inc(counted2, 2)
                    with v.Fori(0, EF // 16) as i:
                        for j in range(2):
                            g = i * 2 + j
                            v.wait_ge(counted2, g + 1)
                            for e in range(2):
                                part = lambda x: x[:, e, ts(g, 8)].unsqueeze(2)
                                v.tensor_tensor(oh_lo[j][:, e, :, :], G.iota[0:P, :].unsqueeze(1).to_broadcast([P, 8, P]),
                                                part(lo).to_broadcast([P, 8, P]), ALU.is_equal)
                                ins = v.tensor_tensor(oh_hi[j][:, e, :, :], G.iota[0:P, 0:T].unsqueeze(1).to_broadcast([P, 8, T]),
                                                      part(hi).to_broadcast([P, 8, T]), ALU.is_equal)
                            ins.then_inc(hot, 1)
                    v.wait_ge(deg_done, 1)
                    v.tensor_copy(G.out_deg[:, :], G.PS[0:P, 2, 0:T]).then_inc(deg_out, 1)
                    v.tensor_copy(G.in_deg[:, :], G.PS[0:P, 3, 0:T]).then_inc(deg_out, 1)

                @block.tensor
                def _(pe):
                    pe.wait_ge(zeroed, 1)
                    mm = lambda e, a, b, **k: pe.matmul(G.PS[0:P, 2 + e, 0:T], a, b, skip_group_check=True, **k)
                    for e in range(2):
                        mm(e, Z[:, :], Z[:, 0:T], start=True, stop=False)
                    with pe.Fori(0, EF // 16) as i:
                        for j in range(2):
                            pe.wait_ge(hot, i * 2 + j + 1)
                            for e in range(2):
                                for f in range(8):
                                    last = mm(e, oh_lo[j][:, e, f, :], oh_hi[j][:, e, f, :], start=False, stop=False)
                            last.then_inc(counted2, 1)
                    for e in range(2):
                        last = mm(e, Z[:, :], Z[:, 0:T], start=False, stop=True)
                    last.then_inc(deg_done, 1)


def edge_mask(pool, G, ix, copied, rounds, scattered):
    n = ET // CHAINS
    by_chain = G.keys[:, :].rearrange("p (c j) -> p c j", c=CHAINS)
    with pool.Fori(0, n // 4) as i:
        pool.tensor_copy(ix[:, :, :], by_chain[:, :, ts(i, 4)]).then_inc(copied, 1)
        pool.wait_ge(copied, i + 1)
        for j in range(4):
            pool.sem_inc(rounds, 1)
            for c in range(CHAINS):
                pool.indirect_dma_start(G.mask[:, :], bass.IndirectOffsetOnAxis(ap=ix[:, c, j:j + 1], axis=0),
                                        G.zero_b[:, 0:1], None).then_inc(scattered, 16)
            pool.wait_ge(scattered, (i * 4 + j + 1) * 16 * CHAINS)


def segment_max(nc, G, rows, H, M):
    HALVES = ((0, 1563), (1563, N))
    W = HALVES[0][1]
    ring = 5
    with Stage(nc) as s:
        A = s.sb("A", [P, H, N])
        K = [s.sb(f"K{j}", [P, W], BF16) for j in range(ring)]
        junk = [s.sb(f"junk{j}", [P, W], BF16) for j in range(2)]
        red = s.sb("red", [P, U, H, 2])
        aload, read, reduced, turns, reduce_done = [s.sem(x) for x in ("aload", "read", "reduced", "turns", "reduce_done")]
        got = [s.sem(f"got{j}") for j in range(ring)]
        mask = G.mask[0:N * N].rearrange("(n m) a -> n (m a)", m=N)
        units = [(u, a) for u in range(U) for a in range(2)]
        with nc.Block() as block:
            @block.sync
            def _(sp):
                for h in range(H):
                    sp.dma_start(A[:, h, :], over(rows[h, 0:N], P)).then_inc(aload, 16)
                with sp.Fori(0, T // U) as i:
                    for n, (u, a) in enumerate(units):
                        lo, hi = HALVES[a]
                        sp.wait_ge(read, i * len(units) + n + 1)
                        sp.dma_start(K[n % ring][:, 0:hi - lo], mask[ts(i * U + u, P), lo:hi]).then_inc(got[n % ring], 16)

            @block.vector
            def _(v):
                v.sem_inc(read, ring)
                v.sem_inc(reduce_done, 2)
                v.wait_ge(aload, 16 * H)
                with v.Fori(0, T // U) as i:
                    for n, (u, a) in enumerate(units):
                        lo, hi = HALVES[a]
                        v.wait_ge(got[n % ring], (i * 2 + n // ring + 1) * 16)
                        for h in range(H):
                            m = n * H + h
                            v.wait_ge(reduce_done, i * len(units) * H + m + 1)
                            v.sem_inc(turns, 1)
                            v.tensor_tensor_reduce(junk[m % 2][:, 0:hi - lo], K[n % ring][:, 0:hi - lo], A[:, h, lo:hi], 1.0, NEG * 2,
                                                         ALU.add, ALU.max, red[:, u, h, a:a + 1]).then_inc(reduce_done, 1)
                        v.wait_ge(reduce_done, 2 + i * len(units) * H + (n + 1) * H)
                        v.sem_inc(read, 1)
                    v.tensor_reduce(M[:, ts(i, U), :], red[:, :, :, :], AX.X, ALU.max).then_inc(reduced, 1)
                    v.wait_ge(reduced, i + 1)


def aggregate(nc, G, table, W, H, DM, acc):
    NI = ET // (2 * EB)
    WH = W + H
    wide = WH > 512
    NB = 2 if wide else 4
    with Stage(nc) as s:
        ix = [s.sb(f"ix{j}", [128, EB, 4], I32) for j in range(2)]
        R = [s.sb(f"R{j}", [128, EB, WH]) for j in range(2)]
        hot = [s.sb(f"hot{j}", [128, EB, P]) for j in range(2)]
        z = [s.sb(f"z{j}", [128, EB, H]) for j in range(2)] if H else None
        hotT = s.sb("hotT", [P, EB, 128]) if H else None
        copied, freed, scores, exp_done, prep, mm_done, steps, put, hot_done, turned, turn_out, d_done, d_free = [
            s.sem(x) for x in ("copied", "freed", "scores", "exp", "prep", "mm", "steps", "put", "hot", "turned", "turn_out",
                               "d", "d_free")]
        got = [s.sem("got0"), s.sem("got1")]
        rounds = s.sem("rounds")
        DB = lambda j: G.PS[:, 6 + j, 0:EB * 2 * H].rearrange("p (f h) -> p f h", h=2 * H)
        with nc.Block() as block:
            @block.gpsimd
            def _(pool):
                pool.sem_inc(freed, 2)
                with pool.Fori(0, NI) as i:
                    for j in range(2):
                        g = i * 2 + j
                        pool.wait_ge(freed, g + 1)
                        pool.tensor_copy(ix[j][:, :, :], G.edges[:, ts(g, EB), :]).then_inc(copied, 1)
                        pool.wait_ge(copied, g + 1)
                        pool.sem_inc(rounds, 1)
                        for f in range(EB):
                            pool.indirect_dma_start(R[j][:, f, :], None, table[:, :],
                                                    bass.IndirectOffsetOnAxis(ap=ix[j][:, f, 0:1], axis=0)).then_inc(got[j], 16)

            @block.scalar
            def _(act):
                if H:
                    act.sem_inc(d_done, 1)
                    with act.Fori(0, NI) as i:
                        for j in range(2):
                            g = i * 2 + j
                            act.wait_ge(turned, g + 1)
                            act.wait_ge(d_done, g + 1)
                            act.activation(hotT[:, :, :].rearrange("p f e -> p (f e)"),
                                           G.PS[0:P, 4:6, :].rearrange("p a e -> p (a e)"), ACT.Copy).then_inc(turn_out, 1)
                        for j in range(2):
                            act.wait_ge(scores, i * 2 + j + 1)
                            act.activation(R[j][:, :, W:WH], z[j][:, :, :], ACT.Exp).then_inc(exp_done, 1)

            @block.vector
            def _(v):
                v.sem_inc(put, NB)
                v.sem_inc(d_free, 2)
                with v.Fori(0, NI) as i:
                    for j in range(2):
                        v.tensor_tensor(hot[j][:, :, :], G.iota[:, :].unsqueeze(1).to_broadcast([128, EB, P]),
                                        G.edges[:, ts(i * 2 + j, EB), 2:3].bitcast(F32).to_broadcast([128, EB, P]),
                                        ALU.is_equal).then_inc(hot_done, 1)
                    for j in range(2):
                        g = i * 2 + j
                        if not H:
                            v.wait_ge(got[j], (i + 1) * 16 * EB)
                            v.wait_ge(hot_done, g + 1)
                            v.sem_inc(prep, 1)
                            continue
                        v.wait_ge(d_done, 1 + g + 1)
                        v.wait_ge(got[j], (i + 1) * 16 * EB)
                        c = Chain(v, steps, g * 3)
                        c(v.tensor_tensor(z[j][:, :, :], R[j][:, :, W:WH], DB(j)[:, :, 0:H], ALU.add))
                        c(v.scalar_tensor_tensor(out=z[j][:, :, :], in0=z[j][:, :, :], scalar=0.2, in1=z[j][:, :, :], op0=ALU.mult, op1=ALU.max))
                        c(v.tensor_tensor(z[j][:, :, :], z[j][:, :, :], DB(j)[:, :, H:2 * H], ALU.subtract))
                        v.sem_inc(d_free, 1)
                        v.tensor_scalar(z[j][:, :, :], z[j][:, :, :], 0.0, None, ALU.min).then_inc(scores, 1)
                    for j in range(2):
                        if H:
                            g = i * 2 + j
                            v.wait_ge(exp_done, g + 1)
                            r = R[j][:, :, 0:W].rearrange("p f (h c) -> p f h c", h=H)
                            v.tensor_tensor(r, r, R[j][:, :, W:WH].unsqueeze(3).to_broadcast([128, EB, H, W // H]), ALU.mult).then_inc(prep, 1)
                    for j in range(2):
                        for f in range(EB):
                            n = (i * 2 + j) * EB + f
                            b = v.value_load(G.bucket[0:1, ts(n, 1)], min_val=0, max_val=T - 1)
                            k = (j * EB + f) % NB
                            v.wait_ge(mm_done, n + 1)
                            v.wait_ge(put, n + NB)
                            to = acc[:, ts(b, 1), 0:WH].rearrange("p a w -> p (a w)")
                            if wide:
                                v.tensor_tensor(to.rearrange("p (a w) -> p a w", a=2), to.rearrange("p (a w) -> p a w", a=2),
                                                G.PS[0:P, 2 * k:2 * k + 2, 0:WH // 2], ALU.add).then_inc(put, 1)
                            else:
                                v.tensor_tensor(to, to, G.PS[0:P, k, 0:WH], ALU.add).then_inc(put, 1)

            @block.tensor
            def _(pe):
                with pe.Fori(0, NI) as i:
                    for j in range(2):
                        if not H:
                            continue
                        g = i * 2 + j
                        pe.wait_ge(hot_done, g + 1)
                        for f in range(EB):
                            mm = pe.transpose(G.PS[0:P, 4 + f // 4, ts(f % 4, 128)], hot[j][:, f, :], G.ident[:, :])
                        mm.then_inc(turned, 1)
                        pe.wait_ge(turn_out, g + 1)
                        pe.wait_ge(d_free, g + 1)
                        for f in range(EB):
                            b = pe.value_load(G.bucket[0:1, ts(g * EB + f, 1)], min_val=0, max_val=T - 1)
                            mm = pe.matmul(DB(j)[:, f, :], hotT[:, f, :], DM[:, ts(b, 1), :].rearrange("p a h -> p (a h)"),
                                           start=True, stop=True)
                        mm.then_inc(d_done, 1)
                    for j in range(2):
                        pe.wait_ge(prep, i * 2 + j + 1)
                        for f in range(EB):
                            n = (i * 2 + j) * EB + f
                            k = (j * EB + f) % NB
                            pe.wait_ge(put, n + 1)
                            if wide:
                                for a in range(2):
                                    mm = pe.matmul(G.PS[0:P, 2 * k + a, 0:WH // 2], hot[j][:, f, :],
                                                   R[j][:, f, a * (WH // 2):(a + 1) * (WH // 2)], start=True, stop=True)
                            else:
                                mm = pe.matmul(G.PS[0:P, k, 0:WH], hot[j][:, f, :], R[j][:, f, :], start=True, stop=True)
                            mm.then_inc(mm_done, 1)
                            if f == EB - 1:
                                pe.wait_ge(mm_done, n + 1)
                                pe.sem_inc(freed, 1)


def store_rows(nc, pairs):
    with Stage(nc) as s:
        stored = s.sem("stored")
        with nc.Block() as block:
            @block.sync
            def _(sp):
                for to, a in pairs:
                    sp.dma_start(to.rearrange("(t p) d -> p t d", p=P), a).then_inc(stored, 16)
                sp.wait_ge(stored, 16 * len(pairs))


def score_weights(nc, G, wt, kc, W, H, a_src, a_dst, wa):
    C, wc, K = W // H, W // 128, kc * 128
    with Stage(nc) as s:
        A, Wt = s.sb("A", [128, wc, 2 * H]), s.sb("Wt", [128, wc, K])
        O = s.sb("O", [128, kc, 2 * H])
        zeroed, loaded, mm_done, copied, stored = [s.sem(x) for x in ("zeroed", "loaded", "mm", "copied", "stored")]
        with nc.Block() as block:
            @block.gpsimd
            def _(pool):
                pool.memset(A[:, :, :], 0.0).then_inc(zeroed, 1)

            @block.sync
            def _(sp):
                sp.dma_start(Wt[:, :, :], wt.rearrange("(c p) k -> p c k", p=128)).then_inc(loaded, 16)
                sp.wait_ge(zeroed, 1)
                n = 16
                for j, a in enumerate((a_src, a_dst)):
                    for r in range(0, W, min(C, 128)):
                        h, p0, m = r // C, r % 128, min(C, 128)
                        sp.dma_start(A[p0:p0 + m, r // 128, j * H + h:j * H + h + 1],
                                     a[r:r + m].rearrange("(p a) -> p a", a=1)).then_inc(loaded, 16)
                        n += 16
                s.n_loaded = n
                sp.wait_ge(copied, 1)
                sp.dma_start(wa[0:K, 0:2 * H].rearrange("(k p) h -> p k h", p=128), O[:, :, :]).then_inc(stored, 16)
                sp.wait_ge(stored, 16)

            @block.tensor
            def _(pe):
                pe.wait_ge(loaded, 16 + 16 * 2 * (W // min(C, 128)))
                for k in range(kc):
                    for c in range(wc):
                        mm = pe.matmul(G.PS[:, k, 0:2 * H], Wt[:, c, ts(k, 128)], A[:, c, :], start=(c == 0), stop=(c == wc - 1))
                mm.then_inc(mm_done, 1)

            @block.vector
            def _(v):
                v.wait_ge(mm_done, 1)
                v.tensor_copy(O[:, :, :], G.PS[:, 0:kc, 0:2 * H]).then_inc(copied, 1)


def gat(nc, G, src, kc, w, wt, a_src, a_dst, W, H, bias, acc, loops=False, eps=0.0, everywhere=False):
    C = W // H
    table = G.table[0:N * (W + H)].rearrange("(n w) -> n w", w=W + H)
    wa = G.wa[0:kc * 128 * 2 * H].rearrange("(k h) -> k h", h=2 * H)
    with Stage(nc) as s:
        AL, M = s.sb("AL", [P, T, 2 * H]), s.sb("M", [P, T, H])
        DM = s.sb("DM", [P, T, 2 * H])
        one, row, wide = s.sb("one", [P, 1]), s.sb("row", [1, 2]), s.sb("wide", [P, 1])
        wself = s.sb("wself", [P, T, H])
        Bw = s.sb("Bw", [P, W])
        score_weights(nc, G, wt, kc, W, H, a_src, a_dst, wa)
        project_rows(nc, G, src, kc, [(wa, 0)], 2 * H, AL)
        project_rows(nc, G, src, kc, [(w, 0)], W, acc[:, :, 0:W])
        store_rows(nc, [(table[:, 0:W], acc[:, :, 0:W]), (table[:, W:W + H], AL[:, :, 0:H])])
        vec_steps(nc, lambda c, v: c(v.tensor_copy(wself[:, :, :], AL[:, :, 0:H])))
        spread_gate(nc, G, wself, H, G.arows)
        segment_max(nc, G, G.arows, H, M)
        a_s, a_d = AL[:, :, 0:H], AL[:, :, H:2 * H]
        steps, ready, turned, exp_done = [s.sem(x) for x in ("steps", "ready", "turned", "exp")]
        with nc.Block() as block:
            @block.vector
            def _(v):
                c = Chain(v, steps)
                leaky = lambda x: v.scalar_tensor_tensor(out=x, in0=x, scalar=0.2, in1=x, op0=ALU.mult, op1=ALU.max)
                m = DM[:, :, H:2 * H]
                if loops:
                    c(v.tensor_tensor(M[:, :, :], M[:, :, :], a_s, ALU.max))
                c(v.tensor_copy(DM[:, :, 0:H], a_d))
                c(v.tensor_tensor(m, M[:, :, :], a_d, ALU.add))
                c(leaky(m))
                if everywhere:
                    c(v.tensor_reduce(one[:, :], m, AX.XY, ALU.max))
                    v.sem_inc(ready, 1)
                    v.wait_ge(turned, 1)
                    c(v.tensor_reduce(row[:, 0:1], G.PS[0:1, 0, 0:P], AX.X, ALU.max))
                    v.sem_inc(ready, 1)
                    v.wait_ge(turned, 2)
                    c(v.tensor_copy(wide[:, :], G.PS[0:P, 1, 0:1]))
                    c(v.tensor_copy(m, wide[:, :].unsqueeze(2).to_broadcast([P, T, H])))
                if loops:
                    c(v.tensor_tensor(wself[:, :, :], a_s, a_d, ALU.add))
                    c(leaky(wself[:, :, :]))
                    c(v.tensor_tensor(wself[:, :, :], wself[:, :, :], m, ALU.subtract))
                    v.sem_inc(ready, 1)
                    v.wait_ge(exp_done, 1)
                    for h in range(H):
                        r = acc[:, :, h * C:(h + 1) * C]
                        c(v.tensor_tensor(r, r, wself[:, :, h:h + 1].to_broadcast([P, T, C]), ALU.mult))
                    c(v.tensor_copy(acc[:, :, W:W + H], wself[:, :, :]))
                else:
                    c(v.memset(acc[:, :, :], 0.0))

            if everywhere:
                @block.tensor
                def _(pe):
                    pe.wait_ge(ready, 1)
                    pe.transpose(G.PS[0:1, 0, 0:P], one[:, :], G.ident[0:P, 0:P]).then_inc(turned, 1)
                    pe.wait_ge(ready, 2)
                    pe.matmul(G.PS[0:P, 1, 0:1], G.ones[0:1, 0:P], row[:, 0:1], start=True, stop=True).then_inc(turned, 1)
            if loops:
                @block.scalar
                def _(act):
                    act.wait_ge(ready, 1)
                    act.activation(wself[:, :, :], wself[:, :, :], ACT.Exp).then_inc(exp_done, 1)
        aggregate(nc, G, table, W, H, DM, acc)
        loaded, last = s.sem("loaded"), s.sem("last")
        with nc.Block() as block:
            @block.sync
            def _(sp):
                sp.dma_start(Bw[:, :], over(bias, P)).then_inc(loaded, 16)

            @block.vector
            def _(v):
                c = Chain(v, last)
                if eps:
                    c(v.tensor_scalar(acc[:, :, W:W + H], acc[:, :, W:W + H], eps, None, ALU.add))
                c(v.tensor_copy(M[:, :, :], acc[:, :, W:W + H]))
                c(v.reciprocal(M[:, :, :], M[:, :, :]))
                for h in range(H):
                    r = acc[:, :, h * C:(h + 1) * C]
                    c(v.tensor_tensor(r, r, M[:, :, h:h + 1].to_broadcast([P, T, C]), ALU.mult))
                v.wait_ge(loaded, 16)
                c(v.tensor_tensor(acc[:, :, 0:W], acc[:, :, 0:W], Bw[:, :].unsqueeze(1).to_broadcast([P, T, W]), ALU.add))


def gnn0(nc, G, I):
    table = G.table[0:N * D].rearrange("(n w) -> n w", w=D)
    with Stage(nc) as s:
        acc = s.sb("acc", [P, T, D])
        dg = s.sb("dg", [P, 2, T])
        Bw = s.sb("Bw", [P, D])
        steps, root = s.sem("steps"), s.sem("root")
        with nc.Block() as block:
            @block.vector
            def _(v):
                v.tensor_scalar(dg[:, 0, :], G.out_deg[:, :], 1.0, None, ALU.max).then_inc(steps, 1)
                v.tensor_scalar(dg[:, 1, :], G.in_deg[:, :], 1.0, None, ALU.max).then_inc(steps, 1)
                v.wait_ge(root, 1)
                v.reciprocal(dg[:, :, :], dg[:, :, :]).then_inc(steps, 1)

            @block.scalar
            def _(act):
                act.wait_ge(steps, 2)
                act.activation(dg[:, :, :], dg[:, :, :], ACT.Sqrt).then_inc(root, 1)
        project_rows(nc, G, G.xn, KD, [(I["L0_gnn_weight"], 0)], D, acc, mul=dg[:, 0, :])
        store_rows(nc, [(table, acc[:, :, :])])
        vec_steps(nc, lambda c, v: c(v.memset(acc[:, :, :], 0.0)))
        aggregate(nc, G, table, D, 0, None, acc)
        loaded, last = s.sem("loaded"), s.sem("last")
        with nc.Block() as block:
            @block.sync
            def _(sp):
                sp.dma_start(Bw[:, :], over(I["L0_gnn_bias"], P)).then_inc(loaded, 16)

            @block.vector
            def _(v):
                c = Chain(v, last)
                c(v.tensor_tensor(acc[:, :, :], acc[:, :, :], dg[:, 1, :].unsqueeze(2).to_broadcast([P, T, D]), ALU.mult))
                v.wait_ge(loaded, 16)
                c(v.tensor_tensor(acc[:, :, :], acc[:, :, :], Bw[:, :].unsqueeze(1).to_broadcast([P, T, D]), ALU.add))
        rows_to_cols(nc, G, acc, D, G.xT, add=True)


def gnn1(nc, G, I):
    p = lambda n: I["L1_gnn_" + n]
    flat = lambda n: p(n).rearrange("a h c -> (a h c)")
    with Stage(nc) as s:
        acc = s.sb("acc", [P, T, 516])
        gat(nc, G, G.xn, KD, p("W1_T"), p("W1"), flat("a_src1"), flat("a_dst1"), 512, 4, p("b1"), acc, eps=1e-16)
        elu_like(nc, flat3(acc), T * 516, False)
        h = s.sb("h", [128, 4, NC])
        rows_to_cols(nc, G, acc[:, :, 0:512], 512, h)
        acc = acc[:, :, 0:D + 1]
        gat(nc, G, h, 4, p("W2_T"), p("W2"), flat("a_src2"), flat("a_dst2"), D, 1, p("b2"), acc, eps=1e-16)
        rows_to_cols(nc, G, acc[:, :, 0:D], D, G.xT, add=True)


def gnn2(nc, G, I):
    p = lambda n: I["L2_gnn_" + n]
    flat = lambda n: p(n).rearrange("h c -> (h c)")
    with Stage(nc) as s:
        h = s.sb("h", [128, KD, NC])
        with Stage(nc) as s2:
            acc = s2.sb("acc", [P, T, D + 4])
            gat(nc, G, G.xn, KD, p("W1"), p("W1_T"), flat("a_src1"), flat("a_dst1"), D, 4, p("b1"), acc, loops=True)
            rows_to_cols(nc, G, acc[:, :, 0:D], D, h)
        elu_like(nc, flat3(h), KD * NC, False)
        acc = s.sb("acc2", [P, T, D + 1])
        gat(nc, G, h, KD, p("W2"), p("W2_T"), flat("a_src2"), flat("a_dst2"), D, 1, p("b2"), acc, loops=True)
        rows_to_cols(nc, G, acc[:, :, 0:D], D, G.xT, add=True)


def move_rows(nc, kind, far, index, near):
    with Stage(nc) as s:
        moved = s.sem("moved")
        with nc.Block() as block:
            @block.gpsimd
            def _(pool):
                for t in range(T):
                    at = bass.IndirectOffsetOnAxis(ap=index[:, t:t + 1], axis=0)
                    if kind == "scatter":
                        pool.indirect_dma_start(far[:, :], at, near[:, t, :], None).then_inc(moved, 16)
                    else:
                        pool.indirect_dma_start(near[:, t, :], None, far[:, :], at).then_inc(moved, 16)
                pool.wait_ge(moved, 16 * T)


def dma(nc, to, of):
    with Stage(nc) as s:
        done = s.sem("done")
        with nc.Block() as block:
            @block.sync
            def _(sp):
                sp.dma_start(to, of).then_inc(done, 16)
                sp.wait_ge(done, 16)


def load_rows(nc, far, near):
    with Stage(nc) as s:
        loaded = s.sem("loaded")
        with nc.Block() as block:
            @block.sync
            def _(sp):
                sp.dma_start(near, far.rearrange("(t p) d -> p t d", p=P)).then_inc(loaded, 16)
                sp.wait_ge(loaded, 16)


def act_cols(nc, x, func):
    with Stage(nc) as s:
        done = s.sem("done")
        with nc.Block() as block:
            @block.scalar
            def _(act):
                act.activation(x, x, func).then_inc(done, 1)


def conv(nc, G, src, w, b, out):
    taps = 4
    with Stage(nc) as s:
        Wc, Bc = s.sb("Wc", [128, KD, taps]), s.sb("Bc", [128, KD])
        loaded, steps = s.sem("loaded"), s.sem("steps")
        with nc.Block() as block:
            @block.sync
            def _(sp):
                sp.dma_start(Wc[:, :, :], w.rearrange("(k p) j -> p k j", p=128)).then_inc(loaded, 16)
                sp.dma_start(Bc[:, :], blocks(b)).then_inc(loaded, 16)

            @block.vector
            def _(v):
                v.wait_ge(loaded, 32)
                c = Chain(v, steps)
                for k in range(KD):
                    c(v.tensor_scalar(out[:, k, :], src[:, k, :], Wc[:, k, taps - 1:taps], Bc[:, k:k + 1], ALU.mult, ALU.add))
                    for j in range(taps - 1):
                        d = taps - 1 - j
                        c(v.scalar_tensor_tensor(out=out[:, k, d:NC], in0=src[:, k, 0:NC - d], scalar=Wc[:, k, j:j + 1],
                                                 in1=out[:, k, d:NC], op0=ALU.mult, op1=ALU.add))
        act_cols(nc, out[:, :, :], ACT.Silu)


def softplus_cols(nc, G, x):
    with Stage(nc) as s:
        y, w, l = s.sb("y", [128, KD, CW]), s.sb("w", [128, KD, CW]), s.sb("l", [128, KD, CW])
        d = s.sb("d", [128, KD, CW])
        steps, neg, exp_done, one, ln_done = [s.sem(x) for x in ("steps", "neg", "exp", "one", "ln")]
        a = lambda t: t[:, :, :]
        with nc.Block() as block:
            @block.vector
            def _(v):
                with v.Fori(0, NCH) as i:
                    xs = x[:, :, ts(i, CW)]
                    c = Chain(v, steps, i * 12)
                    c(v.tensor_scalar(a(y), xs, -1.0, None, ALU.mult))
                    v.tensor_tensor(a(y), a(y), xs, ALU.min).then_inc(neg, 1)
                    v.wait_ge(exp_done, i + 1)
                    c(v.tensor_scalar(a(w), a(y), 1.0, None, ALU.add))
                    v.sem_inc(one, 1)
                    c(v.tensor_scalar(a(d), a(y), -0.25, 1.0 / 3, ALU.mult, ALU.add))
                    c(v.tensor_tensor(a(d), a(d), a(y), ALU.mult))
                    c(v.scalar_tensor_tensor(out=a(d), in0=a(d), scalar=-0.5, in1=a(y), op0=ALU.add, op1=ALU.mult))
                    c(v.scalar_tensor_tensor(out=a(d), in0=a(d), scalar=1.0, in1=a(y), op0=ALU.add, op1=ALU.mult))
                    v.wait_ge(ln_done, i + 1)
                    c(v.tensor_scalar(a(w), a(y), 1.0 / 64, None, ALU.is_ge))
                    c(v.tensor_scalar(a(y), a(y), 1.0 / 64, None, ALU.is_lt))
                    c(v.tensor_tensor(a(l), a(l), a(w), ALU.mult))
                    c(v.tensor_tensor(a(d), a(d), a(y), ALU.mult))
                    c(v.tensor_tensor(a(l), a(l), a(d), ALU.add))
                    c(v.scalar_tensor_tensor(out=xs, in0=xs, scalar=0.0, in1=a(l), op0=ALU.max, op1=ALU.add))
                    assert c.n == 12

            @block.scalar
            def _(act):
                with act.Fori(0, NCH) as i:
                    act.wait_ge(neg, i + 1)
                    act.activation(a(y), a(y), ACT.Exp).then_inc(exp_done, 1)
                    act.wait_ge(one, i + 1)
                    act.activation(a(l), a(w), ACT.Ln).then_inc(ln_done, 1)


def state_scan(nc, G, xc, dt, BC, z, A_log, D_param, S, y):
    with Stage(nc) as s:
        A, Dp = s.sb("A", [128, KD, S]), s.sb("Dp", [128, KD])
        sel = s.sb("sel", [S, S, 128])
        last = s.sb("last", [128, KD, S])
        u = s.sb("u", [128, KD, CW])
        dA = [s.sb(f"dA{k}", [128, CW]) for k in range(2)]
        ex, dts = [s.sb(f"ex{k}", [128, CW]) for k in range(2)], s.sb("dts", [128, KD, CW])
        dB = s.sb("dB", [128, CW])
        h = s.sb("h", [128, CW])
        hc = [s.sb(f"hc{k}", [128, CW]) for k in range(2)]
        loaded, made, a_done, steps, spread, hc_done, dA_done, dA_used, summed, out_done, scan_done = [
            s.sem(x) for x in ("loaded", "made", "a", "steps", "spread", "hc", "dA", "dA_used", "summed", "out", "scan")]
        spread_free, y_steps, pe_turns = [s.sem(x) for x in ("spread_free", "y_steps", "pe_turns")]
        dt_copied, ex_done, pool_turns = [s.sem(x) for x in ("dt_copied", "ex", "pool_turns")]
        with nc.Block() as block:
            @block.sync
            def _(sp):
                sp.dma_start(A[:, :, :], A_log.rearrange("(k p) s -> p k s", p=128)).then_inc(loaded, 16)
                sp.dma_start(Dp[:, :], blocks(D_param)).then_inc(loaded, 16)

            @block.gpsimd
            def _(pool):
                pool.memset(sel[:, :, :], 0.0).then_inc(made, 1)
                pool.wait_ge(made, 1)
                pool.affine_select(out=sel[:, :, :], in_=sel[:, :, :], compare_op=ALU.not_equal, fill=1.0, base=0,
                                   pattern=[[-1, S], [0, 128]], channel_multiplier=1).then_inc(made, 1)
                pool.wait_ge(a_done, 2)
                with pool.Fori(0, NCH) as i:
                    pool.tensor_copy(dts[:, :, :], dt[:, :, ts(i, CW)]).then_inc(dt_copied, 1)
                    pool.wait_ge(dt_copied, i + 1)
                    for t in range(S):
                        for k in range(KD):
                            n = i * S * KD + t * KD + k
                            pool.wait_ge(dA_done, n + 1)
                            pool.sem_inc(pool_turns, 1)
                            pool.tensor_scalar(ex[k][:, :], dts[:, k, :], A[:, k, t:t + 1], -1e3, ALU.mult, ALU.max).then_inc(ex_done, 1)
                    pool.wait_ge(ex_done, (i + 1) * S * KD)

            @block.scalar
            def _(act):
                act.wait_ge(loaded, 32)
                act.activation(A[:, :, :], A[:, :, :], ACT.Exp).then_inc(a_done, 1)
                act.sem_inc(dA_done, 2)
                with act.Fori(0, NCH) as i:
                    for t in range(S):
                        for k in range(KD):
                            n = i * S * KD + t * KD + k
                            act.wait_ge(ex_done, n + 1)
                            act.wait_ge(dA_used, n + 1)
                            act.activation(dA[k][:, :], ex[k][:, :], ACT.Exp).then_inc(dA_done, 1)

            @block.tensor
            def _(pe):
                pe.wait_ge(made, 2)
                def add_up(i, t):
                    for k in range(KD):
                        pe.wait_ge(hc_done, i * S * KD + t * KD + k + 1)
                        pe.matmul(G.PS[:, 4 + k, 0:CW], G.ident[:, :], hc[k][:, :], start=(t == 0), stop=(t == S - 1)).then_inc(summed, 1)
                with pe.Fori(0, NCH) as i:
                    for t in range(S):
                        pe.wait_ge(spread_free, i * S + t + 1)
                        pe.sem_inc(pe_turns, 1)
                        for j in range(2):
                            mm = pe.matmul(G.PS[:, 2 * (t % 2) + j, 0:CW], sel[:, t, :], BC[j][:, 0, ts(i, CW)], start=True, stop=True)
                        mm.then_inc(spread, 1)
                        if t == 1:
                            pe.wait_ge(out_done, i + 1)
                        if t:
                            add_up(i, t - 1)
                    add_up(i, S - 1)

            @block.vector
            def _(v):
                v.sem_inc(spread_free, 2)
                v.sem_inc(out_done, 1)
                v.sem_inc(dA_used, 2)
                v.sem_inc(summed, 2)
                v.wait_ge(a_done, 1)
                v.tensor_scalar(A[:, :, :], A[:, :, :], -1.0, None, ALU.mult).then_inc(a_done, 1)
                v.memset(last[:, :, :], 0.0).then_inc(scan_done, 1)
                v.wait_ge(scan_done, 1)
                with v.Fori(0, NCH) as i:
                    c = Chain(v, steps, i * (1 + 3 * S * KD))
                    c(v.tensor_tensor(u[:, :, :], dt[:, :, ts(i, CW)], xc[:, :, ts(i, CW)], ALU.mult))
                    for t in range(S):
                        v.wait_ge(spread, i * S + t + 1)
                        for k in range(KD):
                            n = i * S * KD + t * KD + k
                            c(v.tensor_tensor(dB[:, :], u[:, k, :], G.PS[:, 2 * (t % 2), 0:CW], ALU.mult))
                            v.wait_ge(dA_done, 2 + n + 1)
                            c(v.tensor_tensor_scan(h[:, :], dA[k][:, :], dB[:, :], last[:, k, t:t + 1], ALU.mult, ALU.add))
                            v.sem_inc(dA_used, 1)
                            c(v.tensor_copy(last[:, k, t:t + 1], h[:, CW - 1:CW]))
                            v.wait_ge(summed, n + 1)
                            v.tensor_tensor(hc[k][:, :], h[:, :], G.PS[:, 2 * (t % 2) + 1, 0:CW], ALU.mult).then_inc(hc_done, 1)
                            v.wait_ge(hc_done, n + 1)
                            if k == KD - 1:
                                v.sem_inc(spread_free, 1)
                    v.wait_ge(summed, 2 + (i + 1) * S * KD)
                    for k in range(KD):
                        v.scalar_tensor_tensor(out=y[:, k, ts(i, CW)], in0=xc[:, k, ts(i, CW)], scalar=Dp[:, k:k + 1],
                                               in1=G.PS[:, 4 + k, 0:CW], op0=ALU.mult, op1=ALU.add).then_inc(y_steps, 1)
                    v.wait_ge(y_steps, (i + 1) * 2)
                    v.tensor_tensor(y[:, :, ts(i, CW)], y[:, :, ts(i, CW)], z[:, :, ts(i, CW)], ALU.mult).then_inc(out_done, 1)


def gnn3(nc, G, I):
    p = lambda n: I["L3_gnn_" + n]
    S, R = 16, 16
    far = G.table[0:N * D].rearrange("(n w) -> n w", w=D)
    with Stage(nc) as s:
        place, place_i, key = s.sb("place", [P, T]), s.sb("place_i", [P, T], I32), s.sb("key", [P, T])
        noise = s.sb("noise", [P, T])
        load_rows(nc, I["node_vec"].rearrange("(n a) -> n a", a=1), noise[:, :].unsqueeze(2))
        vec_steps(nc, lambda c, v: c(v.tensor_tensor(key[:, :], G.out_deg[:, :], noise[:, :], ALU.add)))
        rank(nc, G, key, G.key_row, place)
        vec_steps(nc, lambda c, v: c(v.tensor_copy(place_i[:, :], place[:, :])))
        with Stage(nc) as s2:
            xc, z = s2.sb("xc", [128, KD, NC]), s2.sb("z", [128, KD, NC])
            with Stage(nc) as s3:
                xp = s3.sb("xp", [128, KD, NC])
                with Stage(nc) as s4:
                    rows = s4.sb("rows", [P, T, D])
                    cols_to_rows(nc, G, G.xn, rows)
                    move_rows(nc, "scatter", far, place_i, rows)
                    load_rows(nc, far, rows[:, :, :])
                    rows_to_cols(nc, G, rows, D, xp)
                raw = s3.sb("raw", [128, KD, NC])
                w = p("in_proj_w_T")
                dense_cols(nc, G, xp, KD, w[:, 0:D], KD, raw)
                dense_cols(nc, G, xp, KD, w[:, D:2 * D], KD, z)
                act_cols(nc, z[:, :, :], ACT.Silu)
                conv(nc, G, raw, p("conv_w"), p("conv_b"), xc)
            dt = s2.sb("dt", [128, KD, NC])
            w = p("x_proj_w_T")
            with Stage(nc) as s3:
                low = s3.sb("low", [R, 1, NC])
                dense_cols(nc, G, xc, KD, w[:, 0:R], 1, low, mp=R)
                dense_cols(nc, G, low, 1, p("dt_proj_w_T"), KD, dt, bias=p("dt_proj_b"), kp=R)
            softplus_cols(nc, G, dt)
            BC = [s2.sb(f"BC{j}", [S, 1, NC]) for j in range(2)]
            for j in range(2):
                dense_cols(nc, G, xc, KD, w[:, R + j * S:R + (j + 1) * S], 1, BC[j], mp=S)
            state_scan(nc, G, xc, dt, BC, z, p("A_log"), p("D_param"), S, xc)
            dense_cols(nc, G, xc, KD, p("out_proj_w_T"), KD, z)
            rows = s2.sb("rows", [P, T, D])
            cols_to_rows(nc, G, z, rows)
            store_rows(nc, [(far, rows[:, :, :])])
        with Stage(nc) as s2:
            ha = s2.sb("ha", [128, KD, NC])
            copy_cols(nc, flat3(ha), flat3(G.xn))
            with Stage(nc) as s3:
                rows = s3.sb("rows", [P, T, D])
                move_rows(nc, "gather", far, place_i, rows)
                rows_to_cols(nc, G, rows, D, ha, add=True)
            norm_cols(nc, G, ha, ha, gain=p("ln_global_g"), shift=p("ln_global_b"))
            dma(nc, G.aside, flat3(ha))
        hl = s.sb("hl", [128, KD, NC])
        with Stage(nc) as s2:
            acc = s2.sb("acc", [P, T, D + 4])
            flat = lambda n: p(n).rearrange("h c -> (h c)")
            gat(nc, G, G.xn, KD, p("gat_w_T"), p("gat_w"), flat("gat_a_src"), flat("gat_a_tgt"), D, 4, p("gat_b"), acc,
                eps=1e-16, everywhere=True)
            rows_to_cols(nc, G, acc[:, :, 0:D], D, hl)
        ha, g = s.sb("ha", [128, KD, NC]), s.sb("g", [128, KD, NC])
        dma(nc, flat3(ha), G.aside)
        add_cols(nc, flat3(hl), flat3(G.xn))
        elu_like(nc, flat3(hl), KD * NC, False)
        norm_cols(nc, G, hl, hl, gain=p("ln_local_g"), shift=p("ln_local_b"))
        dense_cols(nc, G, hl, KD, p("wl_T"), KD, g)
        dense_cols(nc, G, ha, KD, p("wg_T"), KD, g, add=True)
        act_cols(nc, g[:, :, :], ACT.Sigmoid)

        def blend(c, v):
            c(v.tensor_tensor(flat3(hl), flat3(hl), flat3(ha), ALU.subtract))
            c(v.tensor_tensor(flat3(hl), flat3(hl), flat3(g), ALU.mult))
            c(v.tensor_tensor(flat3(hl), flat3(hl), flat3(ha), ALU.add))
            c(v.tensor_copy(flat3(g), flat3(hl)))
        vec_steps(nc, blend)
        one_ffn(nc, G, hl, KD, p("ff1_w_T"), p("ff1_b"), p("ff2_w_T"), p("ff2_b"), 512, ACT.Relu, g)
        norm_cols(nc, G, g, G.xT, gain=p("ln2_g"), shift=p("ln2_b"), add=G.xT)


GNN = {0: gnn0, 2: gnn1, 4: gnn2, 6: gnn3}
MIX = {0: mix0, 2: mix1, 4: mix2, 6: mix3}


def build(nc, I, out):
    class G:
        pass
    with ExitStack() as mem:
        mem.enter_context(nc.allow_non_contiguous_dma(reason="biases, a feature to a partition"))
        sb = lambda name, shape, dt=F32: mem.enter_context(nc.sbuf_tensor(name, shape, dt))
        G.xT, G.xn = sb("xT", [128, KD, NC]), sb("xn", [128, KD, NC])
        G.ident, G.ones, G.mean = sb("ident", [128, 128]), sb("ones", [128, 128]), sb("mean", [128, 128])
        G.blockmask, G.before, G.upto = sb("blockmask", [128, 128]), sb("before", [P, P]), sb("upto", [P, P])
        G.after = sb("after", [P, P])
        G.iota, G.iota_i, G.eps = sb("iota", [128, P]), sb("iota_i", [128, P], I32), sb("eps", [128, 1])
        G.zero = sb("zero", [128, CW])
        G.PS = mem.enter_context(nc.psum_tensor("PS", [128, 8, 512], F32))
        dram = lambda name, shape, dt=F32: nc.dram_tensor(name, shape, dt, kind="Internal").ap()
        G.gate = dram("gate_rows", (8, NC))
        G.key_row, G.zeros_row = dram("key_row", (N,)), dram("zeros_row", (512,))
        G.edges, G.bucket = sb("edges", [128, ET, 4], I32), sb("bucket", [1, ET], I32)
        G.out_deg, G.in_deg = sb("out_deg", [P, T]), sb("in_deg", [P, T])
        G.sorted = dram("sorted_edges", (ET * 128, 4), I32)
        G.table, G.wa = dram("table", (N * 516,)), dram("wa", (512 * 8,))
        G.aside = dram("aside", (128, KD * NC))
        G.arows, G.mask = dram("arows", (4, NC)), dram("mask", (N * N + CHAINS * 128, 1), BF16)
        G.zero_b, G.keys = sb("zero_b", [128, 1], BF16), sb("keys", [128, ET], I32)
        setup(nc, G, I["x"])
        with Stage(nc) as s:
            done = s.sem("done")
            with nc.Block() as block:
                @block.vector
                def _(v):
                    v.memset(G.zero_b[:, :], 0.0)
                    v.memset(G.zero[:, :], 0.0).then_inc(done, 1)

                @block.sync
                def _(sp):
                    sp.wait_ge(done, 1)
                    sp.dma_start(G.gate[0:8, N:NC], G.zero[0:8, 0:NC - N]).then_inc(done, 16)
                    sp.wait_ge(done, 17)
        p = lambda name: I[name]
        for k in range(BLOCKS):
            if k == 0:
                sort_edges(nc, G, I)
                mask_keys(nc, G)
                fill_mask(nc, G)
                mask_stage(nc, G)
            if k in MIX:
                norm_cols(nc, G, G.xT, G.xn)
                GNN[k](nc, G, I)
                MIX[k](nc, G, I)
            if k == 1:
                with Stage(nc) as s:
                    L = s.sb("L", [P, T, 8])
                    norm_cols(nc, G, G.xT, G.xn)
                    project_rows(nc, G, G.xn, KD, [(p("L0_ffn_Wr"), 0)], 8, L, [(p("L0_ffn_br"), 0)])
                    softmax_gates(nc, G, L, 8)
                    spread_gate(nc, G, L, 8, G.gate)
                bn_ffn(nc, G, I, G.xT)
            if k == 5:
                top_k_ffn(nc, G, I)
            if k == 3:
                shared = [p("L1_ffn_" + a).rearrange("(a k) f -> a k f" if a[0] == "W" else "(a f) -> a f", a=1)
                          for a in ("W1s", "b1s", "W2s", "b2s")]
                routed_ffn(nc, G, I, p("L1_ffn_Wr"), None, [p("L1_ffn_W1p"), p("L1_ffn_b1p"), p("L1_ffn_W2p"), p("L1_ffn_b2p"), 1024],
                           8, 2, ACT.Gelu)
                ffn(nc, G, G.xn, KD, *shared, 1024, ACT.Gelu, G.xT, 1, None)
            if k == 7:
                routed_ffn(nc, G, I, p("L3_ffn_gate_w"), p("L3_ffn_gate_b"),
                           [p("L3_ffn_w1"), p("L3_ffn_b1"), p("L3_ffn_w2"), p("L3_ffn_b2"), 1024], 8, 1, ACT.Relu)
        finish(nc, G, out)


def kernel(**inputs):
    import numpy as np
    import concourse.bacc as bacc
    from concourse.bass_utils import run_bass_kernel_spmd

    nc = bacc.Bacc("TRN2", target_bir_lowering=False, num_devices=1)
    turned = ["L1_gnn_W1", "L1_gnn_W2", "L2_gnn_W1", "L2_gnn_W2", "L3_gnn_gat_w", "L3_gnn_in_proj_w", "L3_gnn_x_proj_w",
              "L3_gnn_dt_proj_w", "L3_gnn_out_proj_w", "L3_gnn_wl", "L3_gnn_wg", "L3_gnn_ff1_w", "L3_gnn_ff2_w"]
    arrays, aps = {}, {}
    for name, a in list(inputs.items()) + [(n + "_T", np.asarray(inputs[n]).T) for n in turned]:
        if name in ("edge_weight", "L2_mix_t", "L2_ffn_attention_mask"):
            continue
        a = np.ascontiguousarray(a)
        arrays["in_" + name] = a
        aps[name] = nc.dram_tensor("in_" + name, a.shape, mybir.dt.from_np(a.dtype), kind="ExternalInput").ap()
    out = nc.dram_tensor("out_x", (N, D), F32, kind="ExternalOutput").ap()
    build(nc, aps, out)
    return run_bass_kernel_spmd(nc, [arrays], core_ids=[0]).results[0]["out_x"]
```

```python
from contextlib import ExitStack

import concourse.bass as bass
from concourse import mybir
from concourse.alu_op_type import AluOpType as ALU

F32 = mybir.dt.float32
BF16 = mybir.dt.bfloat16
I32 = mybir.dt.int32
ACT = mybir.ActivationFunctionType
AX = mybir.AxisListType
ts = bass.ts

N = 3125
E = 50000
D = 256
KD = D // 128
P = 125
T = N // P
U = 5
CW = 448
NCH = 7
NC = NCH * CW
EF = E // P
EB = 4
RING = 4
NG = -(-((E + T * (EB * 128 - 1)) // (EB * 128)) // RING) * RING
ET = NG * EB
CHAINS = 4
MASK_STEPS = ET // (4 * CHAINS)
MASK_EARLY = MASK_STEPS // 4
NEG = -1e30
BLOCKS = 8


class Stage:

    count = 0

    def __init__(self, nc):
        self.nc = nc
        self.mem = ExitStack()
        self.sems = []
        Stage.count += 1
        self.n = Stage.count

    def sb(self, name, shape, dt=F32):
        return self.mem.enter_context(self.nc.sbuf_tensor(f"{name}_{self.n}", shape, dt))

    def sem(self, name):
        s = self.nc.alloc_semaphore(f"{name}_{self.n}")
        self.sems.append(s)
        return s

    def __enter__(self):
        return self

    def __exit__(self, *exc):
        if exc[0] is None and self.sems:
            self.nc.clear_and_free_semaphores(self.sems)
            self.nc.all_engine_barrier()
        self.mem.close()


class Chain:

    def __init__(self, eng, sem, base=0):
        self.eng, self.sem, self.base, self.n = eng, sem, base, 0

    def __call__(self, ins):
        self.n += 1
        ins.then_inc(self.sem, 1)
        self.eng.wait_ge(self.sem, self.base + self.n)


def blocks(v, n=128):
    return v.rearrange("(m p) -> p m", p=n)


def over(ap, n):
    return bass.AP(ap.tensor, ap.offset, [[0, n]] + [list(d) for d in ap.ap])


def norm_cols(nc, G, src, dst, eps=1e-5, gain=None, shift=None, add=None, rms=False):
    with Stage(nc) as s:
        cen, sq, rstd = [[s.sb(f"{x}{j}", [128, KD, CW] if x != "rstd" else [128, CW]) for j in range(2)]
                         for x in ("cen", "sq", "rstd")]
        gs = s.sb("gs", [128, 2, KD])
        loaded, mean_done, cen_done, sq_done, var_done, root_done, steps, out_done = [
            s.sem(x) for x in ("loaded", "mean", "cen", "sq", "var", "root", "steps", "out")]
        n_loads = (gain is not None) + (shift is not None)
        PS = G.PS

        def chunks(eng, first, second):
            first(0, 0)
            with eng.Fori(0, NCH // 2) as r:
                first(r * 2 + 1, 1)
                second(r * 2, 0)
                first(r * 2 + 2, 0)
                second(r * 2 + 1, 1)
            second(NCH - 1, 0)

        with nc.Block() as block:
            @block.sync
            def _(sp):
                if gain is not None:
                    sp.dma_start(gs[:, 0, :], blocks(gain)).then_inc(loaded, 16)
                if shift is not None:
                    sp.dma_start(gs[:, 1, :], blocks(shift)).then_inc(loaded, 16)

            @block.tensor
            def _(pe):
                def mean(i, j):
                    if rms:
                        return
                    pe.wait_ge(cen_done, i + 1)
                    for k in range(KD):
                        mm = pe.matmul(PS[:, j, 0:CW], G.mean[:, :], src[:, k, ts(i, CW)], start=(k == 0), stop=(k == KD - 1))
                    mm.then_inc(mean_done, 1)

                def squares(i, j):
                    pe.wait_ge(sq_done, i + 3)
                    pe.wait_ge(root_done, i + 1)
                    for k in range(KD):
                        mm = pe.matmul(PS[:, 2 + j, 0:CW], (G.ones if rms else G.mean)[:, :], sq[j][:, k, :],
                                       start=(k == 0), stop=(k == KD - 1))
                    mm.then_inc(var_done, 1)
                pe.sem_inc(var_done, 2)
                chunks(pe, mean, squares)

            @block.scalar
            def _(act):
                def square(i, j):
                    act.wait_ge(var_done, i + 1)
                    if rms:
                        act.activation(sq[j][:, :, :], src[:, :, ts(i, CW)], ACT.Square).then_inc(sq_done, 1)
                    else:
                        act.wait_ge(cen_done, i + 3)
                        act.activation(sq[j][:, :, :], cen[j][:, :, :], ACT.Square).then_inc(sq_done, 1)

                def root(i, j):
                    act.wait_ge(var_done, i + 3)
                    act.wait_ge(out_done, i + 1)
                    if rms:
                        act.activation(rstd[j][:, :], PS[:, 2 + j, 0:CW], ACT.Sqrt).then_inc(root_done, 1)
                    else:
                        act.activation(rstd[j][:, :], PS[:, 2 + j, 0:CW], ACT.Sqrt, bias=G.eps[:, 0:1]).then_inc(root_done, 1)
                act.sem_inc(sq_done, 2)
                act.sem_inc(root_done, 2)
                chunks(act, square, root)

            @block.vector
            def _(v):
                K = (2 if rms else 1) + KD * ((gain is not None or shift is not None) + (add is not None))

                def center(i, j):
                    if rms:
                        return
                    v.wait_ge(mean_done, i + 1)
                    v.wait_ge(sq_done, i + 1)
                    v.wait_ge(out_done, i + 1)
                    for k in range(KD):
                        ins = v.tensor_tensor(cen[j][:, k, :], src[:, k, ts(i, CW)], PS[:, j, 0:CW], ALU.subtract)
                    ins.then_inc(cen_done, 1)

                def scale(i, j):
                    c = Chain(v, steps, i * K)
                    v.wait_ge(root_done, i + 3)
                    if rms:
                        c(v.tensor_scalar(rstd[j][:, :], rstd[j][:, :], 1e-12, float(D) ** -0.5, ALU.max, ALU.mult))
                        cs = src[:, :, ts(i, CW)]
                    else:
                        v.wait_ge(cen_done, i + 3)
                        cs = cen[j][:, :, :]
                    c(v.reciprocal(rstd[j][:, :], rstd[j][:, :]))
                    for k in range(KD):
                        to = cen[j][:, k, :] if add is not None else dst[:, k, ts(i, CW)]
                        ins = v.tensor_tensor(to, cs[:, k, :], rstd[j][:, :], ALU.mult)
                        if gain is not None or shift is not None:
                            c(ins)
                            g = gs[:, 0, k:k + 1] if gain is not None else 1.0
                            b = gs[:, 1, k:k + 1] if shift is not None else 0.0
                            ins = v.tensor_scalar(to, to, g, b, ALU.mult, ALU.add)
                        if add is not None:
                            c(ins)
                            ins = v.tensor_tensor(dst[:, k, ts(i, CW)], add[:, k, ts(i, CW)], to, ALU.add)
                    assert c.n == K
                    ins.then_inc(out_done, 1)
                v.sem_inc(cen_done, 2)
                v.sem_inc(out_done, 2)
                if n_loads:
                    v.wait_ge(loaded, 16 * n_loads)
                chunks(v, center, scale)


def dense_cols(nc, G, src, kc, w, mo, out, bias=None, func=ACT.Identity, add=False, kp=128, mp=128):
    NB = min(mo, 4)
    with Stage(nc) as s:
        W, B = s.sb("W", [kp, kc, mo * mp]), s.sb("B", [mp, mo])
        loaded, mm_done, out_done, zeroed, turns = [s.sem(x) for x in ("loaded", "mm", "out", "zeroed", "turns")]
        with nc.Block() as block:
            @block.sync
            def _(sp):
                sp.dma_start(W[:, :, :], w.rearrange("(k p) m -> p k m", p=kp)).then_inc(loaded, 16)
                if bias is not None:
                    sp.dma_start(B[:, :], blocks(bias, mp)).then_inc(loaded, 16)
            n_loads = 16 * (1 + (bias is not None))

            @block.tensor
            def _(pe):
                pe.wait_ge(loaded, n_loads)
                with pe.Fori(0, NCH) as i:
                    for m in range(mo):
                        pe.wait_ge(out_done, i * mo + m + 1)
                        if kp < 128:
                            pe.sem_inc(turns, 1)
                        for k in range(kc):
                            mm = pe.matmul(G.PS[0:mp, m % NB, 0:CW], W[:, k, ts(m, mp)], src[:, k, ts(i, CW)],
                                           start=(k == 0), stop=(k == kc - 1))
                        mm.then_inc(mm_done, 1)

            def evacuate(eng, one):
                eng.sem_inc(out_done, NB)
                if bias is None:
                    eng.memzero(B[:, :]).then_inc(zeroed, 1)
                    eng.wait_ge(zeroed, 1)
                else:
                    eng.wait_ge(loaded, n_loads)
                with eng.Fori(0, NCH) as i:
                    for m in range(mo):
                        eng.wait_ge(mm_done, i * mo + m + 1)
                        one(i, m).then_inc(out_done, 1)

            if add:
                @block.vector
                def _(v):
                    evacuate(v, lambda i, m: v.scalar_tensor_tensor(
                        out=out[:, m, ts(i, CW)], in0=G.PS[0:mp, m % NB, 0:CW], scalar=B[:, m:m + 1],
                        in1=out[:, m, ts(i, CW)], op0=ALU.add, op1=ALU.add))
            else:
                @block.scalar
                def _(act):
                    evacuate(act, lambda i, m: act.activation(
                        out[:, m, ts(i, CW)], G.PS[0:mp, m % NB, 0:CW], func, bias=B[:, m:m + 1]))


def project_rows(nc, G, src, kc, parts, M, dst, bias=(), kp=128, mul=None):
    with Stage(nc) as s:
        W = s.sb("W", [kp, kc, M])
        B = s.sb("B", [P, M]) if bias else None
        X = s.sb("X", [kp, U, kc, P])
        loaded, copied, mm_done, out_done = [s.sem(x) for x in ("loaded", "copied", "mm", "out")]
        n_loads = 16 * (len(parts) + len(bias))
        with nc.Block() as block:
            @block.sync
            def _(sp):
                for w, c in parts:
                    sp.dma_start(W[:, :, c:c + w.shape[1]], w.rearrange("(k p) m -> p k m", p=kp)).then_inc(loaded, 16)
                for b, c in bias:
                    sp.dma_start(B[:, c:c + b.shape[0]], over(b, P)).then_inc(loaded, 16)

            @block.scalar
            def _(act):
                act.sem_inc(mm_done, U)
                with act.Fori(0, T // U) as i:
                    for u in range(U):
                        act.wait_ge(mm_done, i * U + u + 1)
                        act.activation(X[:, u, :, :], src[:, :, ts(i * U + u, P)], ACT.Copy).then_inc(copied, 1)

            @block.tensor
            def _(pe):
                pe.wait_ge(loaded, n_loads)
                with pe.Fori(0, T // U) as i:
                    for u in range(U):
                        pe.wait_ge(copied, i * U + u + 1)
                        pe.wait_ge(out_done, i * U + u + 1)
                        for k in range(kc):
                            mm = pe.matmul(G.PS[0:P, u, 0:M], X[:, u, k, :], W[:, k, :],
                                           start=(k == 0), stop=(k == kc - 1))
                        mm.then_inc(mm_done, 1)

            @block.vector
            def _(v):
                v.sem_inc(out_done, U)
                v.wait_ge(loaded, n_loads)
                with v.Fori(0, T // U) as i:
                    for u in range(U):
                        t = i * U + u
                        v.wait_ge(mm_done, U + t + 1)
                        to = dst[:, ts(t, 1), :].rearrange("p a m -> p (a m)")
                        if bias:
                            ins = v.tensor_tensor(to, G.PS[0:P, u, 0:M], B[:, :], ALU.add)
                        elif mul is not None:
                            ins = v.tensor_scalar(to, G.PS[0:P, u, 0:M], mul[:, ts(t, 1)], None, ALU.mult)
                        else:
                            ins = v.tensor_copy(to, G.PS[0:P, u, 0:M])
                        ins.then_inc(out_done, 1)


def rows_to_cols(nc, G, rows, M, dst, add=False):
    mo = M // 128
    with Stage(nc) as s:
        X = s.sb("X", [P, U, M])
        copied, turned, out_done = [s.sem(x) for x in ("copied", "turned", "out")]
        with nc.Block() as block:
            @block.scalar
            def _(act):
                act.sem_inc(turned, U)
                with act.Fori(0, T // U) as i:
                    for u in range(U):
                        act.wait_ge(turned, i * U + u + 1)
                        act.activation(X[:, u, :], rows[:, ts(i * U + u, 1), :].rearrange("p a m -> p (a m)"),
                                       ACT.Copy).then_inc(copied, 1)

            @block.tensor
            def _(pe):
                with pe.Fori(0, T // U) as i:
                    for u in range(U):
                        pe.wait_ge(copied, i * U + u + 1)
                        pe.wait_ge(out_done, i * U + u + 1)
                        for m in range(mo):
                            mm = pe.transpose(G.PS[:, u, m * P:(m + 1) * P], X[:, u, ts(m, 128)], G.ident[0:P, 0:P])
                        mm.then_inc(turned, 1)

            @block.vector
            def _(v):
                v.sem_inc(out_done, U)
                if not add:
                    v.memset(dst[:, :, N:NC], 0.0)
                with v.Fori(0, T // U) as i:
                    for u in range(U):
                        t = i * U + u
                        v.wait_ge(turned, U + t + 1)
                        ps = G.PS[:, u, 0:mo * P].rearrange("p (m n) -> p m n", m=mo)
                        if add:
                            ins = v.tensor_tensor(dst[:, :, ts(t, P)], dst[:, :, ts(t, P)], ps, ALU.add)
                        else:
                            ins = v.tensor_copy(dst[:, :, ts(t, P)], ps)
                        ins.then_inc(out_done, 1)


def spread_gate(nc, G, gates, n, dram):
    W = T * n
    turns = [(a, min(120, W - a)) for a in range(0, W, 120)]
    with Stage(nc) as s:
        R = s.sb("R", [128, len(turns), P])
        turned, copied, stored = [s.sem(x) for x in ("turned", "copied", "stored")]
        flat = gates.rearrange("p t e -> p (t e)")
        with nc.Block() as block:
            @block.tensor
            def _(pe):
                for j, (a, w) in enumerate(turns):
                    pe.transpose(G.PS[0:w, j, 0:P], flat[:, a:a + w], G.ident[0:P, 0:P]).then_inc(turned, 1)

            @block.vector
            def _(v):
                for j, (a, w) in enumerate(turns):
                    v.wait_ge(turned, j + 1)
                    v.tensor_copy(R[0:w, j, :], G.PS[0:w, j, 0:P]).then_inc(copied, 1)

            @block.sync
            def _(sp):
                sp.wait_ge(copied, len(turns))
                done = 0
                for j, (a, w) in enumerate(turns):
                    for t in range(a // n, (a + w) // n):
                        sp.dma_start(dram[0:n, t * P:(t + 1) * P], R[t * n - a:t * n - a + n, j, :]).then_inc(stored, 16)
                        done += 1
                sp.wait_ge(stored, 16 * done)


def ffn(nc, G, src, kc, w1, b1, w2, b2, F, func, out, n_exp, gate, mask_steps=None):
    MH = F // 128
    NP = min(2, n_exp)
    with Stage(nc) as s:
        W1 = [s.sb(f"W1{j}", [128, kc, F]) for j in range(NP)]
        W2 = [s.sb(f"W2{j}", [128, MH, D]) for j in range(NP)]
        B1 = [s.sb(f"B1{j}", [128, MH]) for j in range(NP)]
        B2 = [s.sb(f"B2{j}", [128, KD]) for j in range(NP)]
        g_sb = [s.sb(f"g{j}", [128, NC]) for j in range(NP)] if gate is not None else None
        H = s.sb("H", [128, 4, CW])
        Y = s.sb("Y", [128, KD, CW])
        n_loads = 5 if gate is not None else 4
        loaded = [s.sem(f"loaded{j}") for j in range(NP)]
        up_done, h_done, down_done, y_done, out_done, exp_done = [
            s.sem(x) for x in ("up", "h", "down", "y", "out", "expert")]

        def rounds(eng, body):
            with eng.Fori(0, n_exp // NP) as r:
                for j in range(NP):
                    with eng.Fori(0, NCH) as c:
                        body(j, c, (r * NP + j) * NCH + c, r)

        own = mask_buffers(s) if mask_steps else None
        with nc.Block() as block:
            if mask_steps:
                @block.gpsimd
                def _(pool):
                    edge_mask(pool, G, own, *mask_steps)

            @block.sync
            def _(sp):
                sp.sem_inc(exp_done, NP)
                with sp.Fori(0, n_exp // NP) as r:
                    for j in range(NP):
                        e = r * NP + j
                        sp.wait_ge(exp_done, e + 1)
                        one = lambda ap: ap[ts(e, 1)]
                        sp.dma_start(W1[j][:, :, :], one(w1).rearrange("a (k p) f -> p (a k) f", p=128)).then_inc(loaded[j], 16)
                        sp.dma_start(W2[j][:, :, :], one(w2).rearrange("a (m p) d -> p (a m) d", p=128)).then_inc(loaded[j], 16)
                        sp.dma_start(B1[j][:, :], one(b1).rearrange("a (m p) -> p (a m)", p=128)).then_inc(loaded[j], 16)
                        sp.dma_start(B2[j][:, :], one(b2).rearrange("a (m p) -> p (a m)", p=128)).then_inc(loaded[j], 16)
                        if gate is not None:
                            row = one(gate)
                            sp.dma_start(g_sb[j][:, :], bass.AP(row.tensor, row.offset, [[0, 128], [1, NC]])).then_inc(loaded[j], 16)

            @block.tensor
            def _(pe):
                pe.sem_inc(down_done, 4)
                def body(j, c, n, r):
                    pe.wait_ge(loaded[j], (r + 1) * 16 * n_loads)

                    def up(m):
                        pe.wait_ge(h_done, n * MH + m + 1)
                        for k in range(kc):
                            mm = pe.matmul(G.PS[:, m % 4, 0:CW], W1[j][:, k, ts(m, 128)], src[:, k, ts(c, CW)],
                                           start=(k == 0), stop=(k == kc - 1))
                        mm.then_inc(up_done, 1)

                    def down(m):
                        pe.wait_ge(h_done, 4 + n * MH + m + 1)
                        if m == 0:
                            pe.wait_ge(y_done, n + 1)
                        for o in range(KD):
                            mm = pe.matmul(G.PS[:, 4 + o, 0:CW], W2[j][:, m, ts(o, 128)], H[:, m % 4, :],
                                           start=(m == 0), stop=(m == MH - 1))
                        mm.then_inc(down_done, 1)

                    up(0)
                    for m in range(1, MH):
                        up(m)
                        down(m - 1)
                    down(MH - 1)
                rounds(pe, body)

            @block.scalar
            def _(act):
                act.sem_inc(h_done, 4)
                def body(j, c, n, r):
                    act.wait_ge(loaded[j], (r + 1) * 16 * n_loads)
                    for m in range(MH):
                        act.wait_ge(up_done, n * MH + m + 1)
                        act.wait_ge(down_done, n * MH + m + 1)
                        act.activation(H[:, m % 4, :], G.PS[:, m % 4, 0:CW], func, bias=B1[j][:, m:m + 1]).then_inc(h_done, 1)
                rounds(act, body)

            @block.vector
            def _(v):
                v.sem_inc(y_done, 1)
                def body(j, c, n, r):
                    v.wait_ge(loaded[j], (r + 1) * 16 * n_loads)
                    v.wait_ge(down_done, 4 + (n + 1) * MH)
                    for o in range(KD):
                        if gate is not None:
                            ins = v.scalar_tensor_tensor(out=Y[:, o, :], in0=G.PS[:, 4 + o, 0:CW], scalar=B2[j][:, o:o + 1],
                                                         in1=g_sb[j][:, ts(c, CW)], op0=ALU.add, op1=ALU.mult)
                        else:
                            ins = v.tensor_scalar(Y[:, o, :], G.PS[:, 4 + o, 0:CW], B2[j][:, o:o + 1], None, ALU.add)
                    ins.then_inc(y_done, 1)
                    v.wait_ge(y_done, n + 2)
                    v.tensor_tensor(out[:, :, ts(c, CW)], out[:, :, ts(c, CW)], Y[:, :, :], ALU.add).then_inc(out_done, 1)
                    v.wait_ge(out_done, n + 1)
                with v.Fori(0, n_exp // NP) as r:
                    for j in range(NP):
                        with v.Fori(0, NCH) as c:
                            body(j, c, (r * NP + j) * NCH + c, r)
                        v.sem_inc(exp_done, 1)


def setup(nc, G, x):
    with Stage(nc) as s:
        rows = s.sb("rows", [P, T, D])
        made, loaded = s.sem("made"), s.sem("loaded")
        with nc.Block() as block:
            @block.gpsimd
            def _(pool):
                c = Chain(pool, made)
                c(pool.memset(G.ident[:, :], 0.0))
                c(pool.affine_select(out=G.ident[:, :], in_=G.ident[:, :], compare_op=ALU.not_equal, fill=1.0, base=0,
                                     pattern=[[-1, 128]], channel_multiplier=1))
                c(pool.memset(G.blockmask[:, :], 1.0))
                g4 = G.blockmask[:, :].rearrange("p (g n) -> p g n", g=4)
                c(pool.affine_select(out=g4, in_=g4, compare_op=ALU.is_ge, fill=0.0, base=0,
                                     pattern=[[-32, 4], [0, 32]], channel_multiplier=1))
                c(pool.affine_select(out=g4, in_=g4, compare_op=ALU.is_ge, fill=0.0, base=31,
                                     pattern=[[32, 4], [0, 32]], channel_multiplier=-1))
                c(pool.memset(G.before[:, :], 1.0))
                c(pool.affine_select(out=G.before[:, :], in_=G.before[:, :], compare_op=ALU.is_gt, fill=0.0, base=0,
                                     pattern=[[1, P]], channel_multiplier=-1))
                c(pool.memset(G.after[:, :], 1.0))
                c(pool.affine_select(out=G.after[:, :], in_=G.after[:, :], compare_op=ALU.is_gt, fill=0.0, base=0,
                                     pattern=[[-1, P]], channel_multiplier=1))
                c(pool.memset(G.upto[:, :], 1.0))
                c(pool.affine_select(out=G.upto[:, :], in_=G.upto[:, :], compare_op=ALU.is_ge, fill=0.0, base=0,
                                     pattern=[[1, P]], channel_multiplier=-1))
                c(pool.memset(G.ones[:, :], 1.0))
                c(pool.memset(G.mean[:, :], 1.0 / D))
                c(pool.memset(G.eps[:, :], 1e-5))
                c(pool.iota(G.iota_i[:, :], pattern=[[1, P]], base=0, channel_multiplier=0))
                c(pool.tensor_copy(G.iota[:, :], G.iota_i[:, :]))
                c(pool.memset(G.xT[:, :, N:NC], 0.0))

            @block.sync
            def _(sp):
                sp.dma_start(rows[:, :, :], x.rearrange("(t p) d -> p t d", p=P)).then_inc(loaded, 16)
                sp.wait_ge(loaded, 16)
        rows_to_cols(nc, G, rows, D, G.xT)


def finish(nc, G, out):
    with Stage(nc) as s:
        rows = s.sb("rows", [P, T, D])
        stored = s.sem("stored")
        cols_to_rows(nc, G, G.xT, rows)
        with nc.Block() as block:
            @block.sync
            def _(sp):
                sp.dma_start(out.rearrange("(t p) d -> p t d", p=P), rows[:, :, :]).then_inc(stored, 16)
                sp.wait_ge(stored, 16)


def cols_to_rows(nc, G, src, rows, kb=KD):
    with Stage(nc) as s:
        X = s.sb("X", [128, U, kb, P])
        copied, turned, out_done = [s.sem(x) for x in ("copied", "turned", "out")]
        with nc.Block() as block:
            @block.scalar
            def _(act):
                act.sem_inc(turned, U)
                with act.Fori(0, T // U) as i:
                    for u in range(U):
                        act.wait_ge(turned, i * U + u + 1)
                        act.activation(X[:, u, :, :], src[:, :, ts(i * U + u, P)], ACT.Copy).then_inc(copied, 1)

            @block.tensor
            def _(pe):
                with pe.Fori(0, T // U) as i:
                    for u in range(U):
                        pe.wait_ge(copied, i * U + u + 1)
                        pe.wait_ge(out_done, i * U + u + 1)
                        for m in range(kb):
                            mm = pe.transpose(G.PS[0:P, u, ts(m, 128)], X[:, u, m, :], G.ident[:, :])
                        mm.then_inc(turned, 1)

            @block.vector
            def _(v):
                v.sem_inc(out_done, U)
                with v.Fori(0, T // U) as i:
                    for u in range(U):
                        t = i * U + u
                        v.wait_ge(turned, U + t + 1)
                        v.tensor_copy(rows[:, ts(t, 1), :].rearrange("p a m -> p (a m)"),
                                      G.PS[0:P, u, 0:kb * 128]).then_inc(out_done, 1)


def softmax_gates(nc, G, L, n):
    with Stage(nc) as s:
        m, z = s.sb("m", [P, T]), s.sb("z", [P, T])
        steps, ready, exp_done = [s.sem(x) for x in ("steps", "ready", "exp")]
        bc = lambda a: a[:, :].unsqueeze(2).to_broadcast([P, T, n])
        with nc.Block() as block:
            @block.vector
            def _(v):
                c = Chain(v, steps)
                c(v.tensor_reduce(m[:, :], L[:, :, :], AX.X, ALU.max))
                v.tensor_tensor(L[:, :, :], L[:, :, :], bc(m), ALU.subtract).then_inc(ready, 1)
                v.wait_ge(exp_done, 1)
                c(v.tensor_reduce(z[:, :], L[:, :, :], AX.X, ALU.add))
                c(v.reciprocal(z[:, :], z[:, :]))
                c(v.tensor_tensor(L[:, :, :], L[:, :, :], bc(z), ALU.mult))

            @block.scalar
            def _(act):
                act.wait_ge(ready, 1)
                act.activation(L[:, :, :], L[:, :, :], ACT.Exp).then_inc(exp_done, 1)


def route(nc, G, L, n, top, S, put, take, gate, tile_expert):
    with Stage(nc) as s:
        eq, work, pre = s.sb("eq", [P, top, T, n]), s.sb("work", [P, T, n]), s.sb("pre", [P, T, n])
        sel, keep, prod = s.sb("sel", [P, T, n]), s.sb("keep", [P, T, n]), s.sb("prod", [P, T, n])
        m, seen, spare = s.sb("m", [P, top, T]), s.sb("seen", [P, T]), s.sb("spare", [P, T])
        base, tiles, ends = s.sb("base", [P, n]), s.sb("tiles", [P, n]), s.sb("ends", [P, n])
        spare_i, kept = s.sb("spare_i", [P, T], I32), s.sb("kept", [P, T])
        NT = tile_expert.shape[1] if tile_expert is not None else n
        tile_no, tile_i, owner = s.sb("tile_no", [1, NT]), s.sb("tile_i", [1, NT], I32), s.sb("owner", [1, NT])
        steps, ready, mm_done, made = [s.sem(x) for x in ("steps", "ready", "mm", "made")]
        bc = lambda a: a.unsqueeze(2).to_broadcast([P, T, n])
        with nc.Block() as block:
            @block.gpsimd
            def _(pool):
                pool.iota(spare_i[:, :], pattern=[[P, T]], base=NT * S, channel_multiplier=1).then_inc(made, 1)
                pool.iota(tile_i[:, :], pattern=[[1, NT]], base=0, channel_multiplier=0).then_inc(made, 1)

            @block.vector
            def _(v):
                c = Chain(v, steps)
                src = L[:, :, :]
                for a in range(top):
                    c(v.tensor_reduce(m[:, a, :], src, AX.X, ALU.max))
                    c(v.tensor_tensor(eq[:, a, :, :], src, bc(m[:, a, :]), ALU.is_equal))
                    c(v.memset(seen[:, :], 1.0))
                    for e in range(n):
                        c(v.tensor_tensor(eq[:, a, :, e], eq[:, a, :, e], seen[:, :], ALU.mult))
                        c(v.tensor_tensor(seen[:, :], seen[:, :], eq[:, a, :, e], ALU.subtract))
                    if a + 1 < top:
                        c(v.scalar_tensor_tensor(out=work[:, :, :], in0=eq[:, a, :, :], scalar=-4.0, in1=src, op0=ALU.mult, op1=ALU.add))
                        src = work[:, :, :]
                c(v.tensor_copy(sel[:, :, :], eq[:, 0, :, :]))
                for a in range(1, top):
                    c(v.tensor_tensor(sel[:, :, :], sel[:, :, :], eq[:, a, :, :], ALU.add))
                v.sem_inc(ready, 1)
                v.wait_ge(mm_done, 2)
                c(v.tensor_copy(work[:, :, :], G.PS[0:P, 1, 0:T * n].rearrange("p (t e) -> p t e", e=n)))
                for e in range(n):
                    c(v.tensor_tensor_scan(pre[:, :, e], work[:, :, e], G.zero[0:P, 0:T], 0.0, ALU.add, ALU.add))
                c(v.tensor_copy(ends[:, :], pre[:, T - 1, :]))
                c(v.tensor_tensor(pre[:, :, :], pre[:, :, :], work[:, :, :], ALU.subtract))
                c(v.tensor_tensor(pre[:, :, :], pre[:, :, :], G.PS[0:P, 0, 0:T * n].rearrange("p (t e) -> p t e", e=n), ALU.add))
                v.wait_ge(made, 2)
                if top == 1:
                    room = float(-(-5 * N // (4 * n)))
                    c(v.tensor_scalar(keep[:, :, :], pre[:, :, :], room, None, ALU.is_le))
                    c(v.tensor_tensor(prod[:, :, :], eq[:, 0, :, :], keep[:, :, :], ALU.mult))
                    c(v.tensor_reduce(kept[:, :], prod[:, :, :], AX.X, ALU.add))
                    for e in range(n):
                        c(v.memset(base[:, e:e + 1], float(e * S - 1)))
                else:
                    c(v.memset(tiles[:, :], 0.0))
                    for k in range(-(-N // S)):
                        c(v.scalar_tensor_tensor(out=tiles[:, :], in0=ends[:, :], scalar=float(k * S), in1=tiles[:, :],
                                                 op0=ALU.is_gt, op1=ALU.add))
                    c(v.tensor_tensor_scan(ends[:, :], tiles[:, :], G.zero[0:P, 0:n], 0.0, ALU.add, ALU.add))
                    c(v.tensor_tensor(base[:, :], ends[:, :], tiles[:, :], ALU.subtract))
                    c(v.tensor_scalar(base[:, :], base[:, :], float(S), -1.0, ALU.mult, ALU.add))
                    c(v.tensor_copy(tile_no[:, :], tile_i[:, :]))
                    c(v.memset(owner[:, :], 0.0))
                    for e in range(n - 1):
                        c(v.scalar_tensor_tensor(out=owner[:, :], in0=tile_no[:, :], scalar=ends[0:1, e:e + 1], in1=owner[:, :],
                                                 op0=ALU.is_ge, op1=ALU.add))
                    c(v.tensor_copy(tile_expert[:, :], owner[:, :]))
                c(v.tensor_tensor(pre[:, :, :], pre[:, :, :], base[:, :].unsqueeze(1).to_broadcast([P, T, n]), ALU.add))
                for a in range(top):
                    c(v.tensor_tensor(prod[:, :, :], eq[:, a, :, :], pre[:, :, :], ALU.mult))
                    c(v.tensor_reduce(seen[:, :], prod[:, :, :], AX.X, ALU.add))
                    if top == 1:
                        c(v.tensor_tensor(gate[:, :, 0], m[:, 0, :], kept[:, :], ALU.mult))
                        c(v.tensor_tensor(seen[:, :], seen[:, :], kept[:, :], ALU.mult))
                        c(v.tensor_copy(take[:, :, 0], seen[:, :]))
                        c(v.tensor_scalar(kept[:, :], kept[:, :], -1.0, 1.0, ALU.mult, ALU.add))
                        c(v.tensor_copy(spare[:, :], spare_i[:, :]))
                        c(v.tensor_tensor(spare[:, :], spare[:, :], kept[:, :], ALU.mult))
                        c(v.tensor_tensor(seen[:, :], seen[:, :], spare[:, :], ALU.add))
                    else:
                        c(v.tensor_copy(take[:, :, a], seen[:, :]))
                    c(v.tensor_copy(put[:, :, a], seen[:, :]))
                if top == 2:
                    c(v.tensor_tensor(seen[:, :], m[:, 0, :], m[:, 1, :], ALU.add))
                    c(v.reciprocal(seen[:, :], seen[:, :]))
                    for a in range(2):
                        c(v.tensor_tensor(gate[:, :, a], m[:, a, :], seen[:, :], ALU.mult))

            @block.tensor
            def _(pe):
                pe.wait_ge(ready, 1)
                flat = sel[:, :, :].rearrange("p t e -> p (t e)")
                pe.matmul(G.PS[0:P, 0, 0:T * n], G.upto[:, :], flat, start=True, stop=True).then_inc(mm_done, 1)
                pe.matmul(G.PS[0:P, 1, 0:T * n], G.ones[0:P, 0:P], flat, start=True, stop=True).then_inc(mm_done, 1)


def spread_tokens(nc, G, put, top, rows_in_tiles):
    with Stage(nc) as s:
        rows, none = s.sb("rows", [P, T, D]), s.sb("none", [128, D * 4])
        made, filled, moved = s.sem("made"), s.sem("filled"), s.sem("moved")
        cols_to_rows(nc, G, G.xn, rows)
        with nc.Block() as block:
            @block.vector
            def _(v):
                v.memset(none[:, :], 0.0).then_inc(made, 1)

            @block.sync
            def _(sp):
                sp.wait_ge(made, 1)
                for r in range(0, rows_in_tiles, 512):
                    sp.dma_start(G.slots[r:r + 512, :].rearrange("(p a) d -> p (a d)", p=128), none[:, :]).then_inc(filled, 16)

            @block.gpsimd
            def _(pool):
                pool.wait_ge(filled, 16 * (rows_in_tiles // 512))
                pool.sem_inc(made, 1)
                for a in range(top):
                    for t in range(T):
                        pool.indirect_dma_start(G.slots[:, :], bass.IndirectOffsetOnAxis(ap=put[:, t, a:a + 1], axis=0),
                                                rows[:, t, :], None).then_inc(moved, 16)
                pool.wait_ge(moved, 16 * T * top)


def experts_ffn(nc, G, w1, b1, w2, b2, F, func, n, S, NT, tile_expert):
    MH, RB = F // 128, S // 128
    with Stage(nc) as s:
        W1, W2 = [s.sb(f"W1{j}", [128, KD, F]) for j in range(2)], [s.sb(f"W2{j}", [128, MH, D]) for j in range(2)]
        B1, B2 = s.sb("B1", [128, n, MH]), s.sb("B2", [128, n, D])
        X, XT = [s.sb(f"X{j}", [128, RB, D]) for j in range(2)], s.sb("XT", [128, KD, S])
        H, Y = s.sb("H", [128, MH, S]), [s.sb(f"Y{j}", [128, RB, D]) for j in range(2)]
        bias = s.sb("bias", [128, 2, MH])
        loaded, stored = [s.sem(f"loaded{j}") for j in range(2)], [s.sem(f"stored{j}") for j in range(2)]
        bload, freed, turned, x_done, up_done, h_done, down_done, y_done, sent = [
            s.sem(x) for x in ("bload", "freed", "turned", "x", "up", "h", "down", "y", "sent")]
        rows = lambda of, t: of[ts(t, S), :].rearrange("(a p) d -> p a d", p=128)
        expert = lambda eng, t: t if tile_expert is None else eng.value_load(tile_expert[0:1, ts(t, 1)], min_val=0, max_val=n - 1)

        with nc.Block() as block:
            @block.sync
            def _(sp):
                sp.dma_start(B1[:, :, :], b1.rearrange("e (m p) -> p e m", p=128)).then_inc(bload, 16)
                sp.dma_start(B2[:, :, :], bass.AP(b2.tensor, b2.offset, [[0, 128], [D, n], [1, D]])).then_inc(bload, 16)
                sp.sem_inc(freed, 2)
                with sp.Fori(0, NT // 2) as i:
                    for j in range(2):
                        t = i * 2 + j
                        e = expert(sp, t)
                        sp.wait_ge(freed, t + 1)
                        sp.dma_start(X[j][:, :, :], rows(G.slots, t)).then_inc(loaded[j], 16)
                        sp.dma_start(W1[j][:, :, :], w1[ts(e, 1)].rearrange("a (k p) f -> p (a k) f", p=128)).then_inc(loaded[j], 16)
                        sp.dma_start(W2[j][:, :, :], w2[ts(e, 1)].rearrange("a (m p) d -> p (a m) d", p=128)).then_inc(loaded[j], 16)

            @block.tensor
            def _(pe):
                pe.sem_inc(down_done, 1)
                with pe.Fori(0, NT // 2) as i:
                    for j in range(2):
                        t = i * 2 + j
                        pe.wait_ge(loaded[j], (i + 1) * 48)
                        for k in range(KD):
                            for r in range(RB):
                                mm = pe.transpose(G.PS[:, k, ts(r, 128)], X[j][:, r, ts(k, 128)], G.ident[:, :])
                        mm.then_inc(turned, 1)
                        pe.wait_ge(x_done, t + 1)
                        for m in range(MH):
                            pe.wait_ge(h_done, t * MH + m + 1)
                            for k in range(KD):
                                mm = pe.matmul(G.PS[:, 2 + m % 4, 0:S], W1[j][:, k, ts(m, 128)], XT[:, k, :],
                                               start=(k == 0), stop=(k == KD - 1))
                            mm.then_inc(up_done, 1)
                        for r in range(RB):
                            pe.wait_ge(y_done, t * RB + r + 1)
                            for m in range(MH):
                                if r == 0:
                                    pe.wait_ge(h_done, 4 + t * MH + m + 1)
                                mm = pe.matmul(G.PS[:, 6 + r % 2, 0:D], H[:, m, ts(r, 128)], W2[j][:, m, :],
                                               start=(m == 0), stop=(m == MH - 1))
                            mm.then_inc(down_done, 1)
                        pe.wait_ge(down_done, 1 + (t + 1) * RB)
                        pe.sem_inc(freed, 1)

            @block.scalar
            def _(act):
                act.sem_inc(h_done, 4)
                with act.Fori(0, NT // 2) as i:
                    for j in range(2):
                        t = i * 2 + j
                        act.wait_ge(x_done, t + 1)
                        act.wait_ge(down_done, 1 + t * RB)
                        for m in range(MH):
                            act.wait_ge(up_done, t * MH + m + 1)
                            act.activation(H[:, m, :], G.PS[:, 2 + m % 4, 0:S], func, bias=bias[:, j, m:m + 1]).then_inc(h_done, 1)

            @block.vector
            def _(v):
                v.sem_inc(y_done, 2)
                v.wait_ge(bload, 32)
                v.sem_inc(sent, 1)
                with v.Fori(0, NT // 2) as i:
                    for j in range(2):
                        t = i * 2 + j
                        e = expert(v, t)
                        v.wait_ge(h_done, 4 + t * MH)
                        v.tensor_copy(bias[:, j, :], B1[:, ts(e, 1), :].rearrange("p a m -> p (a m)"))
                        v.wait_ge(turned, t + 1)
                        v.tensor_copy(XT[:, :, :], G.PS[:, 0:KD, 0:S]).then_inc(x_done, 1)
                        for r in range(RB):
                            v.wait_ge(down_done, 1 + t * RB + r + 1)
                            if r == 0:
                                v.wait_ge(stored[j], i * 16)
                            v.tensor_tensor(Y[j][:, r, :], G.PS[:, 6 + r % 2, 0:D], B2[:, ts(e, 1), :].rearrange("p a d -> p (a d)"),
                                            ALU.add).then_inc(y_done, 1)

            @block.gpsimd
            def _(pool):
                with pool.Fori(0, NT // 2) as i:
                    for j in range(2):
                        t = i * 2 + j
                        pool.wait_ge(y_done, 2 + (t + 1) * RB)
                        pool.dma_start(rows(G.results, t), Y[j][:, :, :]).then_inc(stored[j], 16)
                for j in range(2):
                    pool.wait_ge(stored[j], 16 * (NT // 2))


def sum_results(nc, G, take, gate, top, n_rows):
    with Stage(nc) as s:
        Y = [s.sb(f"Y{a}", [P, T, D]) for a in range(top)]
        moved, steps = [s.sem(f"moved{i}") for i in range(T // U)], s.sem("steps")
        with nc.Block() as block:
            @block.gpsimd
            def _(pool):
                for t in range(T):
                    for a in range(top):
                        pool.indirect_dma_start(Y[a][:, t, :], None, G.results[0:n_rows, :],
                                                bass.IndirectOffsetOnAxis(ap=take[:, t, a:a + 1], axis=0)).then_inc(moved[t // U], 16)

            @block.vector
            def _(v):
                c = Chain(v, steps)
                for a in range(0, T, U):
                    v.wait_ge(moved[a // U], 16 * top * U)
                    for b in range(top):
                        y = Y[b][:, a:a + U, :]
                        c(v.tensor_tensor(y, y, gate[:, a:a + U, b:b + 1].to_broadcast([P, U, D]), ALU.mult))
                    if top == 2:
                        c(v.tensor_tensor(Y[0][:, a:a + U, :], Y[0][:, a:a + U, :], Y[1][:, a:a + U, :], ALU.add))
        rows_to_cols(nc, G, Y[0], D, G.xT, add=True)


def routed_ffn(nc, G, I, wr, br, experts, n, top, func, S):
    w1, b1, w2, b2, F = experts
    NT = n if top == 1 else -(-((top * N + n * (S - 1)) // S) // 2) * 2
    with Stage(nc) as s:
        put, take = s.sb("put", [P, T, top], I32), s.sb("take", [P, T, top], I32)
        gate = s.sb("gate", [P, T, top])
        tile_expert = s.sb("tile_expert", [1, NT], I32) if top > 1 else None
        norm_cols(nc, G, G.xT, G.xn)
        with Stage(nc) as s2:
            L = s2.sb("L", [P, T, n])
            project_rows(nc, G, G.xn, KD, [(wr, 0)], n, L, [(br, 0)] if br is not None else [])
            softmax_gates(nc, G, L, n)
            route(nc, G, L, n, top, S, put, take, gate, tile_expert)
        spread_tokens(nc, G, put, top, NT * S)
        experts_ffn(nc, G, w1, b1, w2, b2, F, func, n, S, NT, tile_expert)
        sum_results(nc, G, take, gate, top, NT * S)


def bn_ffn(nc, G, I, out, n_exp=8):
    names = ["W1", "W2", "Wo"]
    vecs = ["b1", "g1", "be1", "m1", "v1", "b2", "g2", "be2", "m2", "v2", "bo"]
    w = [I["L0_ffn_" + x] for x in names]
    with Stage(nc) as s:
        W = [[s.sb(f"W{j}{l}", [128, KD, D]) for l in range(3)] for j in range(2)]
        V = s.sb("V", [128, len(vecs), n_exp * KD])
        SC = s.sb("SC", [128, 2, n_exp * KD])
        SH = s.sb("SH", [128, 2, n_exp * KD])
        eps = s.sb("eps", [128, 1])
        cur = s.sb("cur", [128, 2, 5, KD])
        g_sb = [s.sb(f"g{j}", [128, NC]) for j in range(2)]
        H = [s.sb(f"H{l}", [128, KD, CW]) for l in range(2)]
        Y = s.sb("Y", [128, KD, CW])
        vload, steps, ready, root = [s.sem(x) for x in ("vload", "steps", "ready", "root")]
        loaded = [s.sem(f"loaded{j}") for j in range(2)]
        up_done, h_done, y_mm, y_done, out_done, exp_done, cur_done = [
            s.sem(x) for x in ("up", "h", "ymm", "y", "out", "expert", "cur")]
        at = vecs.index
        with nc.Block() as block:
            @block.sync
            def _(sp):
                for j, name in enumerate(vecs):
                    sp.dma_start(V[:, j, :], I["L0_ffn_" + name].rearrange("e (k p) -> p (e k)", p=128)).then_inc(vload, 16)

            @block.scalar
            def _(act):
                act.wait_ge(ready, 1)
                act.wait_ge(vload, 16 * len(vecs))
                for l in range(2):
                    act.activation(SC[:, l, :], V[:, at(f"v{l + 1}"), :], ACT.Sqrt, bias=eps[:, 0:1]).then_inc(root, 1)

            @block.vector
            def _(v):
                c = Chain(v, steps)
                v.memset(eps[:, :], 0.001).then_inc(ready, 1)
                v.wait_ge(vload, 16 * len(vecs))
                v.wait_ge(root, 2)
                c(v.reciprocal(SC[:, :, :], SC[:, :, :]))
                for l in range(2):
                    a = lambda x: V[:, at(f"{x}{l + 1}"), :]
                    c(v.tensor_tensor(SC[:, l, :], SC[:, l, :], a("g"), ALU.mult))
                    c(v.tensor_tensor(SH[:, l, :], a("b"), a("m"), ALU.subtract))
                    c(v.tensor_tensor(SH[:, l, :], SH[:, l, :], SC[:, l, :], ALU.mult))
                    c(v.tensor_tensor(SH[:, l, :], SH[:, l, :], a("be"), ALU.add))
        own = mask_buffers(s)
        with nc.Block() as block:
            @block.gpsimd
            def _(pool):
                edge_mask(pool, G, own, MASK_EARLY, MASK_STEPS)

            @block.sync
            def _(sp):
                sp.sem_inc(exp_done, 2)
                with sp.Fori(0, n_exp // 2) as r:
                    for j in range(2):
                        e = r * 2 + j
                        sp.wait_ge(exp_done, e + 1)
                        for l in range(3):
                            sp.dma_start(W[j][l][:, :, :], w[l][ts(e, 1)].rearrange("a (k p) f -> p (a k) f", p=128)).then_inc(loaded[j], 16)
                        row = G.gate[ts(e, 1)]
                        sp.dma_start(g_sb[j][:, :], bass.AP(row.tensor, row.offset, [[0, 128], [1, NC]])).then_inc(loaded[j], 16)

            @block.tensor
            def _(pe):
                with pe.Fori(0, n_exp // 2) as r:
                    for j in range(2):
                        with pe.Fori(0, NCH) as c:
                            n = (r * 2 + j) * NCH + c
                            pe.wait_ge(loaded[j], (r + 1) * 64)
                            for l in range(3):
                                if l == 0:
                                    pe.wait_ge(h_done, n * 4 + 2)
                                elif l == 1:
                                    pe.wait_ge(h_done, n * 4 + 4)
                                else:
                                    pe.wait_ge(y_done, n + 1)
                                for k in range(KD):
                                    if l:
                                        pe.wait_ge(h_done, 4 + n * 4 + 2 * (l - 1) + k + 1)
                                    rhs = H[l - 1][:, k, :] if l else G.xn[:, k, ts(c, CW)]
                                    for m in range(KD):
                                        mm = pe.matmul(G.PS[:, 2 * l + m, 0:CW], W[j][l][:, k, ts(m, 128)], rhs,
                                                       start=(k == 0), stop=(k == KD - 1))
                                        if k == KD - 1:
                                            mm.then_inc(up_done if l < 2 else y_mm, 1)

            @block.scalar
            def _(act):
                act.sem_inc(h_done, 4)
                with act.Fori(0, n_exp // 2) as r:
                    for j in range(2):
                        with act.Fori(0, NCH) as c:
                            n = (r * 2 + j) * NCH + c
                            act.wait_ge(cur_done, r * 2 + j + 1)
                            for l in range(2):
                                for m in range(KD):
                                    act.wait_ge(up_done, n * 4 + 2 * l + m + 1)
                                    if l == 0:
                                        act.wait_ge(up_done, n * 4 + 1)
                                    act.activation(H[l][:, m, :], G.PS[:, 2 * l + m, 0:CW], ACT.Relu,
                                                   scale=cur[:, j, l, m:m + 1], bias=cur[:, j, 2 + l, m:m + 1]).then_inc(h_done, 1)

            @block.vector
            def _(v):
                v.sem_inc(y_done, 1)
                with v.Fori(0, n_exp // 2) as r:
                    for j in range(2):
                        e = r * 2 + j
                        for l in range(2):
                            v.tensor_copy(cur[:, j, l, :], SC[:, l, ts(e, KD)])
                            v.tensor_copy(cur[:, j, 2 + l, :], SH[:, l, ts(e, KD)])
                        v.tensor_copy(cur[:, j, 4, :], V[:, at("bo"), ts(e, KD)]).then_inc(cur_done, 1)
                        with v.Fori(0, NCH) as c:
                            n = e * NCH + c
                            v.wait_ge(cur_done, e + 1)
                            v.wait_ge(loaded[j], (r + 1) * 64)
                            v.wait_ge(y_mm, (n + 1) * 2)
                            for o in range(KD):
                                ins = v.scalar_tensor_tensor(out=Y[:, o, :], in0=G.PS[:, 4 + o, 0:CW], scalar=cur[:, j, 4, o:o + 1],
                                                             in1=g_sb[j][:, ts(c, CW)], op0=ALU.add, op1=ALU.mult)
                            ins.then_inc(y_done, 1)
                            v.wait_ge(y_done, n + 2)
                            v.tensor_tensor(out[:, :, ts(c, CW)], out[:, :, ts(c, CW)], Y[:, :, :], ALU.add).then_inc(out_done, 1)
                            v.wait_ge(out_done, n + 1)
                        v.sem_inc(exp_done, 1)


def rank(nc, G, key, key_row, dst):
    with Stage(nc) as s:
        row, junk = s.sb("row", [P, N]), s.sb("junk", [P, N])
        part = s.sb("part", [P, 4, T])
        stored, loaded, steps, done = [s.sem(x) for x in ("stored", "loaded", "steps", "done")]
        turned = s.sem("turned")
        kr = s.sb("kr", [T, P])
        with nc.Block() as block:
            @block.tensor
            def _(pe):
                pe.transpose(G.PS[0:T, 0, 0:P], key[:, :], G.ident[0:P, 0:P]).then_inc(turned, 1)

            @block.sync
            def _(sp):
                sp.wait_ge(steps, 1)
                sp.dma_start(key_row.rearrange("(t p) -> t p", p=P), kr[:, :]).then_inc(stored, 16)
                sp.wait_ge(stored, 16)
                sp.dma_start(row[:, :], over(key_row, P)).then_inc(loaded, 16)

            @block.vector
            def _(v):
                v.wait_ge(turned, 1)
                v.tensor_copy(kr[:, :], G.PS[0:T, 0, 0:P]).then_inc(steps, 1)
                v.memset(part[:, :, :], 0.0).then_inc(steps, 1)
                v.wait_ge(steps, 2)
                v.wait_ge(loaded, 16)
                c = Chain(v, done)
                for t in range(T):
                    k = key[:, t:t + 1]
                    a, b = t * P, (t + 1) * P
                    if t > 0:
                        c(v.tensor_scalar(junk[:, 0:a], row[:, 0:a], k, 0.0, ALU.is_le, ALU.add, accum_out=part[:, 0, t:t + 1]))
                    if t < T - 1:
                        c(v.tensor_scalar(junk[:, b:N], row[:, b:N], k, 0.0, ALU.is_lt, ALU.add, accum_out=part[:, 1, t:t + 1]))
                    c(v.tensor_scalar(junk[:, a:b], row[:, a:b], k, 0.0, ALU.is_lt, ALU.add, accum_out=part[:, 2, t:t + 1]))
                    c(v.scalar_tensor_tensor(out=junk[:, a:b], in0=row[:, a:b], scalar=k, in1=G.after[:, :],
                                             op0=ALU.is_equal, op1=ALU.mult, accum_out=part[:, 3, t:t + 1]))
                c(v.tensor_tensor(part[:, 0:2, :], part[:, 0:2, :], part[:, 2:4, :], ALU.add))
                c(v.tensor_tensor(dst[:, :], part[:, 0, :], part[:, 1, :], ALU.add))


def vec_steps(nc, fn):
    with Stage(nc) as s:
        steps = s.sem("steps")
        with nc.Block() as block:
            @block.vector
            def _(v):
                fn(Chain(v, steps), v)


def top_k_ffn(nc, G, I):
    kept = N // 2 - 1
    with Stage(nc) as s:
        L, R = s.sb("L", [P, T, 1]), s.sb("R", [P, T])
        flat = L[:, :, :].rearrange("p t a -> p (t a)")
        neg = s.sb("neg", [P, T])
        norm_cols(nc, G, G.xT, G.xn)
        project_rows(nc, G, G.xn, KD, [(I["L2_ffn_wr"], 0)], 1, L, [(I["L2_ffn_br"], 0)])
        vec_steps(nc, lambda c, v: c(v.tensor_scalar(neg[:, :], flat, -1.0, None, ALU.mult)))
        rank(nc, G, neg, G.key_row, R)

        def steps(c, v):
            c(v.tensor_scalar(R[:, :], R[:, :], float(kept), None, ALU.is_lt))
            c(v.tensor_tensor(flat, flat, R[:, :], ALU.mult))
        vec_steps(nc, steps)
        spread_gate(nc, G, L, 1, G.gate)
    one = lambda a: I["L2_ffn_" + a].rearrange("(a k) f -> a k f" if a[0] == "w" else "(a f) -> a f", a=1)
    ffn(nc, G, G.xn, KD, one("w1"), one("b1"), one("w2"), one("b2"), 1024, ACT.Gelu_apprx_tanh, G.xT, 1, G.gate)
    add_cols(nc, flat3(G.xT), flat3(G.xn))


def elu_like(nc, x, n, plus_one):
    p = x.shape[0]
    with Stage(nc) as s:
        m = s.sb("m", [p, n])
        low, e = s.sem("low"), s.sem("exp")
        steps = s.sem("steps")
        with nc.Block() as block:
            @block.vector
            def _(v):
                v.tensor_scalar(m[:, :], x, 0.0, None, ALU.min).then_inc(low, 1)
                v.wait_ge(e, 1)
                if plus_one:
                    v.scalar_tensor_tensor(out=x, in0=x, scalar=0.0, in1=m[:, :], op0=ALU.max, op1=ALU.add).then_inc(steps, 1)
                else:
                    v.tensor_scalar(m[:, :], m[:, :], -1.0, None, ALU.add).then_inc(steps, 1)
                    v.wait_ge(steps, 1)
                    v.scalar_tensor_tensor(out=x, in0=x, scalar=0.0, in1=m[:, :], op0=ALU.max, op1=ALU.add).then_inc(steps, 1)

            @block.scalar
            def _(act):
                act.wait_ge(low, 1)
                act.activation(m[:, :], m[:, :], ACT.Exp).then_inc(e, 1)


def outer_sums(nc, G, Kr, Vr, dst, ksum=None, kb=KD, extra=None, scale=1.0):
    with Stage(nc) as s:
        X = s.sb("X", [P, U, kb * 128])
        Z = s.sb("Z", [P, 128])
        S = s.sb("S", [128, kb])
        zeroed, copied, mm_done, all_done, steps = [s.sem(x) for x in ("zeroed", "copied", "mm", "all", "steps")]
        with nc.Block() as block:
            @block.gpsimd
            def _(pool):
                pool.memset(Z[:, :], 0.0).then_inc(zeroed, 1)

            @block.scalar
            def _(act):
                act.sem_inc(mm_done, U)
                with act.Fori(0, T // U) as i:
                    for u in range(U):
                        act.wait_ge(mm_done, i * U + u + 1)
                        act.activation(X[:, u, :], Kr[:, ts(i * U + u, 1), :].rearrange("p a m -> p (a m)"), ACT.Copy).then_inc(copied, 1)

            @block.tensor
            def _(pe):
                pe.wait_ge(zeroed, 1)
                for b in range(kb):
                    pe.matmul(G.PS[:, b, 0:128], Z[:, :], Z[:, :], start=True, stop=False, skip_group_check=True)
                    pe.matmul(G.PS[:, 2 + b, 0:1], Z[:, :], Z[:, 0:1], start=True, stop=False, skip_group_check=True)
                with pe.Fori(0, T // U) as i:
                    for u in range(U):
                        pe.wait_ge(copied, i * U + u + 1)
                        for b in range(kb):
                            pe.matmul(G.PS[:, b, 0:128], X[:, u, ts(b, 128)],
                                      Vr[:, ts(i * U + u, 1), ts(b, 128)].rearrange("p a m -> p (a m)"),
                                      start=False, stop=False, skip_group_check=True)
                            mm = pe.matmul(G.PS[:, 2 + b, 0:1], X[:, u, ts(b, 128)], G.ones[0:P, 0:1],
                                           start=False, stop=False, skip_group_check=True)
                        mm.then_inc(mm_done, 1)
                if extra is not None:
                    K2, V2 = extra
                    n = K2.shape[0]
                    for b in range(kb):
                        pe.matmul(G.PS[:, b, 0:128], K2[:, ts(b, 128)], V2[:, ts(b, 128)], start=False, stop=False, skip_group_check=True)
                        pe.matmul(G.PS[:, 2 + b, 0:1], K2[:, ts(b, 128)], G.ones[0:n, 0:1], start=False, stop=False, skip_group_check=True)
                for b in range(kb):
                    pe.matmul(G.PS[:, b, 0:128], Z[:, :], Z[:, :], start=False, stop=True, skip_group_check=True)
                    mm = pe.matmul(G.PS[:, 2 + b, 0:1], Z[:, :], Z[:, 0:1], start=False, stop=True, skip_group_check=True)
                mm.then_inc(all_done, 1)

            @block.vector
            def _(v):
                v.wait_ge(all_done, 1)
                c = Chain(v, steps)
                for b in range(kb):
                    c(v.scalar_tensor_tensor(out=dst[:, b, :], in0=G.PS[:, b, 0:128], scalar=scale, in1=G.blockmask[:, :],
                                             op0=ALU.mult, op1=ALU.mult))
                    if ksum is not None:
                        c(v.tensor_copy(S[:, b:b + 1], G.PS[:, 2 + b, 0:1]))
                        c(v.tensor_scalar(ksum[:, b, :], G.blockmask[:, :], S[:, b:b + 1], None, ALU.mult))


def attend_cols(nc, G, q, kv, ksum, out, kb=KD):
    def chunks(eng, chunk):
        with eng.Fori(0, NCH // 2) as r:
            for j in range(2):
                chunk(r * 2 + j, 4 * j)
        chunk(NCH - 1, 0)

    with Stage(nc) as s:
        den = s.sb("den", [128, kb, CW])
        num_done, steps, out_done = [s.sem(x) for x in ("num", "steps", "out")]
        with nc.Block() as block:
            @block.tensor
            def _(pe):
                def chunk(i, bank):
                    pe.wait_ge(out_done, i + 1)
                    for b in range(kb):
                        mm = pe.matmul(G.PS[:, bank + b, 0:CW], kv[:, b, :], q[:, b, ts(i, CW)], start=True, stop=True)
                        if ksum is not None:
                            mm = pe.matmul(G.PS[:, bank + 2 + b, 0:CW], ksum[:, b, :], q[:, b, ts(i, CW)], start=True, stop=True)
                    mm.then_inc(num_done, 1)
                chunks(pe, chunk)

            @block.vector
            def _(v):
                def chunk(i, bank):
                    num = G.PS[:, bank:bank + kb, 0:CW]
                    v.wait_ge(num_done, i + 1)
                    if ksum is not None:
                        v.wait_ge(out_done, i + 2)
                        c = Chain(v, steps, i * 2)
                        c(v.tensor_scalar(den[:, :, :], G.PS[:, bank + 2:bank + 2 + kb, 0:CW], 1e-6, None, ALU.add))
                        c(v.reciprocal(den[:, :, :], den[:, :, :]))
                        v.tensor_tensor(out[:, :, ts(i, CW)], num, den[:, :, :], ALU.mult).then_inc(out_done, 1)
                    else:
                        v.tensor_copy(out[:, :, ts(i, CW)], num).then_inc(out_done, 1)
                v.sem_inc(out_done, 2)
                chunks(v, chunk)


flat3 = lambda a: a[:, :, :].rearrange("p a b -> p (a b)")


def copy_cols(nc, dst, src):
    vec_steps(nc, lambda c, v: c(v.tensor_copy(dst, src)))


def add_cols(nc, dst, src):
    vec_steps(nc, lambda c, v: c(v.tensor_tensor(dst, dst, src, ALU.add)))


def linear_attention(nc, G, wq, wk, wv, bq, bk, bv, q):
    dense_cols(nc, G, G.xn, KD, wq, KD, q, bias=bq)
    elu_like(nc, flat3(q), KD * NC, True)
    with Stage(nc) as s:
        kv, ks = s.sb("kv", [128, KD, 128]), s.sb("ks", [128, KD, 128])
        with Stage(nc) as s2:
            Kr, Vr = s2.sb("Kr", [P, T, D]), s2.sb("Vr", [P, T, D])
            project_rows(nc, G, G.xn, KD, [(wk, 0)], D, Kr, [(bk, 0)] if bk is not None else [])
            project_rows(nc, G, G.xn, KD, [(wv, 0)], D, Vr, [(bv, 0)] if bv is not None else [])
            elu_like(nc, flat3(Kr), T * D, True)
            outer_sums(nc, G, Kr, Vr, kv, ks)
        attend_cols(nc, G, q, kv, ks, q)


def mask_keys(nc, G):
    with Stage(nc) as s:
        key, spare, none = [s.sb(x, [128, ET]) for x in ("key", "spare", "none")]
        ed, spare_i = s.sb("ed", [128, 2, ET]), s.sb("spare_i", [128, ET], I32)
        made, steps = s.sem("made"), s.sem("steps")
        with nc.Block() as block:
            @block.gpsimd
            def _(pool):
                pool.iota(spare_i[:, :], pattern=[[128, CHAINS], [0, ET // CHAINS]], base=N * N, channel_multiplier=1).then_inc(made, 1)

            @block.vector
            def _(v):
                c = Chain(v, steps)
                v.wait_ge(made, 1)
                c(v.tensor_copy(spare[:, :], spare_i[:, :]))
                for j in range(2):
                    c(v.tensor_copy(ed[:, j, :], G.edges[:, :, j]))
                c(v.scalar_tensor_tensor(out=key[:, :], in0=ed[:, 1, :], scalar=float(N), in1=ed[:, 0, :], op0=ALU.mult, op1=ALU.add))
                c(v.tensor_scalar(none[:, :], G.edges[:, :, 2:3].bitcast(F32).rearrange("p j a -> p (j a)"), 0.0, None, ALU.is_lt))
                c(v.tensor_tensor(spare[:, :], spare[:, :], none[:, :], ALU.mult))
                c(v.tensor_tensor(key[:, :], key[:, :], spare[:, :], ALU.add))
                c(v.tensor_copy(G.keys[:, :], key[:, :]))


def one_ffn(nc, G, src, kc, w1, b1, w2, b2, F, func, out, mask_steps=None):
    a3 = lambda a: a.rearrange("(a k) f -> a k f", a=1)
    a2 = lambda a: a.rearrange("(a f) -> a f", a=1)
    ffn(nc, G, src, kc, a3(w1), a2(b1), a3(w2), a2(b2), F, func, out, 1, None, mask_steps)


def mix0(nc, G, I):
    p = lambda n: I["L0_mix_" + n]
    with Stage(nc) as s:
        a, b = s.sb("a", [128, KD, NC]), s.sb("b", [128, KD, NC])
        linear_attention(nc, G, p("Wq"), p("Wk"), p("Wv"), p("bq"), p("bk"), p("bv"), a)
        copy_cols(nc, flat3(b), flat3(G.xn))
        dense_cols(nc, G, a, KD, p("Wo"), KD, b, bias=p("bo"), add=True)
        norm_cols(nc, G, b, b, gain=p("ln1_g"), shift=p("ln1_b"))
        copy_cols(nc, flat3(a), flat3(b))
        one_ffn(nc, G, b, KD, p("W1"), p("b1"), p("W2"), p("b2"), 1024, ACT.Relu, a,
                (0, MASK_EARLY))
        norm_cols(nc, G, a, G.xT, gain=p("ln2_g"), shift=p("ln2_b"), add=G.xT)


def mix1(nc, G, I):
    p = lambda n: I["L1_mix_" + n].rearrange("h a c -> (h a c)")
    HG = T * 8
    with Stage(nc) as s:
        kv, o = s.sb("kv", [128, KD, 128]), s.sb("o", [128, KD, NC])
        with Stage(nc) as s2:
            R, sq = s2.sb("R", [P, T, D]), s2.sb("sq", [P, T, D])
            wb = s2.sb("wb", [P, 4, D])
            st = s2.sb("st", [P, HG])
            loaded, steps, ready, root = [s2.sem(x) for x in ("loaded", "steps", "ready", "root")]
            cols_to_rows(nc, G, G.xn, R)
            g3 = lambda a: a[:, :, :].rearrange("p t (h c) -> p (t h) c", c=32)
            bc = st[:, :].unsqueeze(2).to_broadcast([P, HG, 32])
            row = lambda j: wb[:, j:j + 1, :].to_broadcast([P, T, D])
            with nc.Block() as block:
                @block.sync
                def _(sp):
                    for j, name in enumerate(("kln_weight", "kln_bias", "vln_weight", "vln_bias")):
                        sp.dma_start(wb[:, j, :], over(p(name), P)).then_inc(loaded, 16)

                @block.vector
                def _(v):
                    c = Chain(v, steps)
                    c(v.tensor_reduce(st[:, :], g3(R), AX.X, ALU.add))
                    c(v.tensor_scalar(st[:, :], st[:, :], 1.0 / 32, None, ALU.mult))
                    c(v.tensor_tensor(g3(R), g3(R), bc, ALU.subtract))
                    c(v.tensor_tensor(sq[:, :, :], R[:, :, :], R[:, :, :], ALU.mult))
                    v.tensor_reduce(st[:, :], g3(sq), AX.X, ALU.add).then_inc(ready, 1)
                    v.wait_ge(root, 1)
                    c(v.tensor_scalar(st[:, :], st[:, :], 1e-5, None, ALU.add))
                    c(v.reciprocal(st[:, :], st[:, :]))
                    c(v.tensor_tensor(g3(R), g3(R), bc, ALU.mult))
                    v.wait_ge(loaded, 64)
                    c(v.tensor_tensor(sq[:, :, :], R[:, :, :], row(2), ALU.mult))
                    c(v.tensor_tensor(sq[:, :, :], sq[:, :, :], row(3), ALU.add))
                    c(v.tensor_tensor(R[:, :, :], R[:, :, :], row(0), ALU.mult))
                    c(v.tensor_tensor(R[:, :, :], R[:, :, :], row(1), ALU.add))

                @block.scalar
                def _(act):
                    act.wait_ge(ready, 1)
                    act.activation(st[:, :], st[:, :], ACT.Sqrt, scale=1.0 / 31).then_inc(root, 1)
            outer_sums(nc, G, R, sq, kv, scale=1.0 / N)
        attend_cols(nc, G, G.xn, kv, None, o)
        add_cols(nc, flat3(o), flat3(G.xn))
        add_cols(nc, flat3(G.xT), flat3(o))


def mix2(nc, G, I):
    p = lambda n: I["L2_mix_" + n]
    HID = 128
    with Stage(nc) as s:
        q = s.sb("q", [128, 1, NC])
        ctxm = s.sb("ctxm", [128, 1, 128])
        xr = s.sb("xr", [128, KD, NC])
        norm_cols(nc, G, G.xn, xr, gain=p("g_pre"), rms=True)
        with Stage(nc) as s2:
            R = s2.sb("R", [P, T, 3 * HID])
            sums = s2.sb("sums", [128, 1, 128])
            top, part, wide = s2.sb("top", [P, HID]), s2.sb("part", [128, 1]), s2.sb("wide", [P, HID])
            mem = s2.sb("mem", [4, 2, HID])
            topc, tr = s2.sb("topc", [HID, 1]), s2.sb("tr", [HID, HID])
            hm = s2.sb("hm", [P, T * 4])
            loaded, steps, turned, exp_done, ready, spread = [
                s2.sem(x) for x in ("loaded", "steps", "turned", "exp", "ready", "spread")]
            project_rows(nc, G, xr, KD, [(p("w_qkv"), 0)], 3 * HID, R)
            qv = R[:, :, 0:HID].rearrange("p t (h c) -> p t h c", c=32)
            kv_, K = R[:, :, HID:2 * HID], R[:, :, HID:2 * HID]
            hm4 = hm[:, :].rearrange("p (t h) -> p t h", h=4)
            with nc.Block() as block:
                @block.sync
                def _(sp):
                    for j in range(2):
                        sp.dma_start(mem[:, j, :], p("mem_kv")[j].rearrange("h d n -> n (h d)")).then_inc(loaded, 16)

                @block.vector
                def _(v):
                    c = Chain(v, steps)
                    c(v.tensor_reduce(hm4, qv, AX.X, ALU.max))
                    for h in range(4):
                        c(v.tensor_tensor(qv[:, :, h, :], qv[:, :, h, :], hm4[:, :, h:h + 1].to_broadcast([P, T, 32]), ALU.subtract))
                    c(v.tensor_reduce(top[:, :], K.rearrange("p t c -> p c t"), AX.X, ALU.max))
                    v.wait_ge(loaded, 32)
                    c(v.tensor_tensor(top[0:4, :], top[0:4, :], mem[:, 0, :], ALU.max))
                    v.sem_inc(ready, 1)
                    v.wait_ge(turned, 1)
                    c(v.tensor_reduce(topc[:, :], G.PS[:, 0, 0:P], AX.X, ALU.max))
                    c(v.tensor_scalar(tr[:, :], G.ident[:, :], topc[:, 0:1], None, ALU.mult))
                    v.sem_inc(ready, 1)
                    v.wait_ge(turned, 2)
                    c(v.tensor_copy(wide[:, :], G.PS[0:P, 1, 0:HID]))
                    c(v.tensor_tensor(K, K, wide[:, :].unsqueeze(1).to_broadcast([P, T, HID]), ALU.subtract))
                    c(v.tensor_tensor(mem[:, 0, :], mem[:, 0, :], wide[0:4, :], ALU.subtract))
                    v.sem_inc(ready, 1)
                    v.wait_ge(exp_done, 3)
                    c(v.tensor_reduce(hm4, qv, AX.X, ALU.add))
                    c(v.reciprocal(hm[:, :], hm[:, :]))
                    c(v.tensor_scalar(hm[:, :], hm[:, :], 32.0 ** -0.5, None, ALU.mult))
                    for h in range(4):
                        c(v.tensor_tensor(qv[:, :, h, :], qv[:, :, h, :], hm4[:, :, h:h + 1].to_broadcast([P, T, 32]), ALU.mult))

                @block.tensor
                def _(pe):
                    pe.wait_ge(ready, 1)
                    pe.transpose(G.PS[:, 0, 0:P], top[:, :], G.ident[0:P, 0:P]).then_inc(turned, 1)
                    pe.wait_ge(ready, 2)
                    pe.matmul(G.PS[:, 1, 0:HID], G.ones[:, :], tr[:, :], start=True, stop=True).then_inc(turned, 1)

                @block.scalar
                def _(act):
                    act.wait_ge(ready, 3)
                    act.activation(R[:, :, 0:HID], R[:, :, 0:HID], ACT.Exp).then_inc(exp_done, 1)
                    act.activation(K, K, ACT.Exp).then_inc(exp_done, 1)
                    act.activation(mem[:, 0, :], mem[:, 0, :], ACT.Exp).then_inc(exp_done, 1)
            outer_sums(nc, G, R[:, :, HID:2 * HID], R[:, :, 2 * HID:3 * HID], ctxm, sums, kb=1,
                       extra=(mem[:, 0, :], mem[:, 1, :]))

            def divide(c, v):
                c(v.tensor_reduce(part[:, :], sums[:, 0, :], AX.X, ALU.max))
                c(v.reciprocal(part[:, :], part[:, :]))
                c(v.tensor_scalar(ctxm[:, 0, :], ctxm[:, 0, :], part[:, 0:1], None, ALU.mult))
                c(v.memset(q[:, :, N:NC], 0.0))
            vec_steps(nc, divide)
            rows_to_cols(nc, G, R[:, :, 0:HID], HID, q)
        attend_cols(nc, G, q, ctxm, None, q, kb=1)
        y = xr
        dense_cols(nc, G, q, 1, p("w_out"), KD, y, bias=p("b_out"))
        norm_cols(nc, G, y, y, gain=p("g_out"), rms=True)
        add_cols(nc, flat3(G.xT), flat3(y))
        add_cols(nc, flat3(G.xT), flat3(G.xn))


def mix3(nc, G, I):
    p = lambda n: I["L3_mix_" + n]
    with Stage(nc) as s:
        q = s.sb("q", [128, KD, NC])
        linear_attention(nc, G, p("Wq"), p("Wk"), p("Wv"), None, None, None, q)
        cat = s.sb("cat", [128, 4, NC])
        msg = cat[:, 2:4, :]
        dense_cols(nc, G, q, KD, p("Wm"), KD, msg)
        norm_cols(nc, G, msg, msg, gain=p("g1"), shift=p("b1"))
        copy_cols(nc, cat[:, 0:2, :], G.xn[:, :, :])
        def clear(c, v):
            c(v.memset(q[:, :, :], 0.0))
            c(v.memset(zb[:, :], 0.0))
        zb = s.sb("zb", [1, 512])
        vec_steps(nc, clear)
        with Stage(nc) as s2:
            done = s2.sem("done")
            with nc.Block() as block:
                @block.sync
                def _(sp):
                    sp.dma_start(G.zeros_row.rearrange("(a n) -> a n", a=1), zb[:, :]).then_inc(done, 16)
                    sp.wait_ge(done, 16)
        one_ffn(nc, G, cat, 4, p("W1"), G.zeros_row, p("W2"), G.zeros_row[0:D], 512, ACT.Relu, q)
        norm_cols(nc, G, q, G.xT, gain=p("g2"), shift=p("b2"), add=G.xT)
        add_cols(nc, flat3(G.xT), flat3(G.xn))


def sort_edges(nc, G, I):
    with Stage(nc) as s:
        raw = s.sb("raw", [P, 2, EF], I32)
        val, hi, lo = s.sb("val", [P, 2, EF]), s.sb("hi", [P, 2, EF]), s.sb("lo", [P, 2, EF])
        rows = s.sb("rows", [P, EF, 4], I32)
        mask, scan, place = s.sb("mask", [P, EF]), s.sb("scan", [P, EF]), s.sb("place", [P, EF])
        zero = s.sb("zero", [P, EF])
        cnt, base = s.sb("cnt", [P, T]), s.sb("base", [P, T])
        tot, tot_i = s.sb("tot", [P, T]), s.sb("tot_i", [P, T], I32)
        ends = s.sb("ends", [P, T])
        place_i, low_i = s.sb("place_i", [P, EF], I32), s.sb("low_i", [P, EF], I32)
        batch_no, batch_i = s.sb("batch_no", [1, NG]), s.sb("batch_i", [1, NG], I32)
        bucket_f = s.sb("bucket_f", [1, NG])
        fill = s.sb("fill", [128, ET, 4], I32)
        loaded, steps, counted, base_done, made, filled, rank_steps, first = [
            s.sem(x) for x in ("loaded", "steps", "counted", "base", "made", "filled", "rank_steps", "first")]
        last_steps, order = s.sem("last_steps"), s.sem("order")
        with nc.Block() as block:
            @block.sync
            def _(sp):
                for j, name in enumerate(("src", "dst")):
                    sp.dma_start(raw[:, j, :], I[name].rearrange("(p f) -> p f", p=P)).then_inc(loaded, 16)
                sp.wait_ge(made, 4)
                sp.dma_start(G.sorted.rearrange("(p j) w -> p j w", p=128), fill[:, :, :]).then_inc(filled, 16)
                sp.wait_ge(filled, 16)

            @block.gpsimd
            def _(pool):
                pool.memset(fill[:, :, :], 0).then_inc(made, 1)
                pool.wait_ge(made, 1)
                pool.memset(fill[:, :, 2:3].bitcast(F32), -1.0).then_inc(made, 1)
                pool.iota(batch_i[:, :], pattern=[[1, NG]], base=0, channel_multiplier=0).then_inc(made, 1)
                pool.wait_ge(made, 3)
                pool.tensor_copy(batch_no[:, :], batch_i[:, :]).then_inc(made, 1)

            @block.vector
            def _(v):
                c = Chain(v, steps)
                c(v.memset(hi[:, :, :], 0.0))
                c(v.memset(zero[:, :], 0.0))
                v.wait_ge(loaded, 32)
                c(v.tensor_copy(val[:, :, :], raw[:, :, :]))
                for b in range(1, T):
                    c(v.scalar_tensor_tensor(out=hi[:, :, :], in0=val[:, :, :], scalar=float(P * b), in1=hi[:, :, :],
                                             op0=ALU.is_ge, op1=ALU.add))
                c(v.scalar_tensor_tensor(out=lo[:, :, :], in0=hi[:, :, :], scalar=-float(P), in1=val[:, :, :],
                                         op0=ALU.mult, op1=ALU.add))
                c(v.memset(rows[:, :, :], 0))
                for j in range(2):
                    c(v.tensor_copy(rows[:, :, j], raw[:, j, :]))
                c(v.tensor_copy(rows[:, :, 2:3].bitcast(F32).rearrange("p f a -> p (f a)"), lo[:, 1, :]))
                c(v.memset(place[:, :], 0.0))
        with nc.Block() as block:
            @block.vector
            def _(v):
                with v.Fori(0, T) as b:
                    c = Chain(v, rank_steps, b * 5)
                    c(v.tensor_scalar(mask[:, :], hi[:, 1, :], G.iota[0:P, ts(b, 1)], None, ALU.is_equal))
                    c(v.tensor_tensor_scan(scan[:, :], mask[:, :], zero[:, :], 0.0, ALU.add, ALU.add))
                    c(v.tensor_copy(cnt[:, ts(b, 1)], scan[:, EF - 1:EF]))
                    c(v.tensor_tensor(scan[:, :], scan[:, :], mask[:, :], ALU.mult))
                    c(v.tensor_tensor(place[:, :], place[:, :], scan[:, :], ALU.add))
                v.sem_inc(counted, 1)
                v.wait_ge(base_done, 2)
                c = Chain(v, first)
                c(v.tensor_scalar(tot[:, :], G.PS[0:P, 1, 0:T], float(EB * 128 - 1), None, ALU.add))
                c(v.tensor_copy(tot_i[:, :], tot[:, :]))
                c(v.tensor_scalar(tot_i[:, :], tot_i[:, :], (EB * 128).bit_length() - 1, None, ALU.arith_shift_right))
                c(v.tensor_copy(tot[:, :], tot_i[:, :]))
                c(v.tensor_tensor_scan(ends[:, :], tot[:, :], zero[:, 0:T], 0.0, ALU.add, ALU.add))
                c(v.tensor_tensor(base[:, :], ends[:, :], tot[:, :], ALU.subtract))
                c(v.tensor_scalar(base[:, :], base[:, :], float(EB * 128), -1.0, ALU.mult, ALU.add))
                c(v.tensor_tensor(base[:, :], base[:, :], G.PS[0:P, 0, 0:T], ALU.add))
                c(v.memset(bucket_f[:, :], 0.0))
                for b in range(T - 1):
                    c(v.scalar_tensor_tensor(out=bucket_f[:, :], in0=batch_no[:, :], scalar=ends[0:1, b:b + 1], in1=bucket_f[:, :],
                                             op0=ALU.is_ge, op1=ALU.add))
                c(v.tensor_copy(G.bucket[:, :], bucket_f[:, :]))
                with v.Fori(0, T) as b:
                    c = Chain(v, last_steps, b * 2)
                    c(v.tensor_scalar(mask[:, :], hi[:, 1, :], G.iota[0:P, ts(b, 1)], base[:, ts(b, 1)], ALU.is_equal, ALU.mult))
                    c(v.tensor_tensor(place[:, :], place[:, :], mask[:, :], ALU.add))
                c = Chain(v, order)
                c(v.tensor_copy(place_i[:, :], place[:, :]))
                c(v.tensor_scalar(low_i[:, :], place_i[:, :], 127, None, ALU.bitwise_and))
                c(v.tensor_scalar(place_i[:, :], place_i[:, :], 7, None, ALU.arith_shift_right))
                c(v.tensor_copy(mask[:, :], low_i[:, :]))
                c(v.tensor_copy(scan[:, :], place_i[:, :]))
                c(v.scalar_tensor_tensor(out=place[:, :], in0=mask[:, :], scalar=float(ET), in1=scan[:, :], op0=ALU.mult, op1=ALU.add))
                c(v.tensor_copy(place_i[:, :], place[:, :]))

            @block.tensor
            def _(pe):
                pe.wait_ge(counted, 1)
                pe.matmul(G.PS[0:P, 0, 0:T], G.before[:, :], cnt[:, :], start=True, stop=True).then_inc(base_done, 1)
                pe.matmul(G.PS[0:P, 1, 0:T], G.ones[0:P, 0:P], cnt[:, :], start=True, stop=True).then_inc(base_done, 1)
        SB = 10
        with Stage(nc) as s2:
            ix = [s2.sb(f"ix{j}", [P, SB], I32) for j in range(2)]
            row = [s2.sb(f"row{j}", [P, SB, 4], I32) for j in range(2)]
            rounds = s2.sem("rounds")
            copied, scattered, fetched = s2.sem("copied"), [s2.sem("scattered0"), s2.sem("scattered1")], s2.sem("fetched")
            oh_lo = [s2.sb(f"oh_lo{j}", [P, 2, 8, P], BF16) for j in range(2)]
            oh_hi = [s2.sb(f"oh_hi{j}", [P, 2, 8, T], BF16) for j in range(2)]
            Z = s2.sb("Z", [P, P], BF16)
            zeroed, hot, counted2, deg_done, deg_out = [s2.sem(x) for x in ("zeroed", "hot", "counted2", "deg", "degout")]
            low, low_made, low_stored = s2.sb("low", [P, N], BF16), s2.sem("low_made"), s2.sem("low_stored")
            with nc.Block() as block:
                @block.sync
                def _(sp):
                    sp.wait_ge(low_made, 1)
                    every = G.mask[0:N * N].rearrange("(n m) a -> n (m a)", m=N)
                    with sp.Fori(0, T) as t:
                        sp.dma_start(every[ts(t, P), :], low[:, :]).then_inc(low_stored, 16)
                    sp.wait_ge(low_stored, 16 * T)

                @block.gpsimd
                def _(pool):
                    pool.memset(low[:, :], NEG).then_inc(low_made, 1)
                    with pool.Fori(0, EF // (2 * SB)) as i:
                        for j in range(2):
                            g = i * 2 + j
                            pool.tensor_copy(ix[j][:, :], place_i[:, ts(g, SB)]).then_inc(copied, 1)
                            pool.tensor_copy(row[j][:, :, :], rows[:, ts(g, SB), :]).then_inc(copied, 1)
                            pool.wait_ge(copied, g * 2 + 2)
                            pool.sem_inc(rounds, 1)
                            for f in range(SB):
                                pool.indirect_dma_start(G.sorted[:, :], bass.IndirectOffsetOnAxis(ap=ix[j][:, f:f + 1], axis=0),
                                                        row[j][:, f, :], None).then_inc(scattered[j], 16)
                        for j in range(2):
                            pool.wait_ge(scattered[j], (i + 1) * 16 * SB)
                    pool.dma_start(G.edges[:, :, :], G.sorted.rearrange("(p j) w -> p j w", p=128)).then_inc(fetched, 16)
                    pool.wait_ge(fetched, 16)

                @block.vector
                def _(v):
                    v.memset(Z[:, :], 0.0).then_inc(zeroed, 1)
                    v.sem_inc(counted2, 2)
                    with v.Fori(0, EF // 16) as i:
                        for j in range(2):
                            g = i * 2 + j
                            v.wait_ge(counted2, g + 1)
                            for e in range(2):
                                part = lambda x: x[:, e, ts(g, 8)].unsqueeze(2)
                                v.tensor_tensor(oh_lo[j][:, e, :, :], G.iota[0:P, :].unsqueeze(1).to_broadcast([P, 8, P]),
                                                part(lo).to_broadcast([P, 8, P]), ALU.is_equal)
                                ins = v.tensor_tensor(oh_hi[j][:, e, :, :], G.iota[0:P, 0:T].unsqueeze(1).to_broadcast([P, 8, T]),
                                                      part(hi).to_broadcast([P, 8, T]), ALU.is_equal)
                            ins.then_inc(hot, 1)
                    v.wait_ge(deg_done, 1)
                    v.tensor_copy(G.out_deg[:, :], G.PS[0:P, 2, 0:T]).then_inc(deg_out, 1)
                    v.tensor_copy(G.in_deg[:, :], G.PS[0:P, 3, 0:T]).then_inc(deg_out, 1)

                @block.tensor
                def _(pe):
                    pe.wait_ge(zeroed, 1)
                    mm = lambda e, a, b, **k: pe.matmul(G.PS[0:P, 2 + e, 0:T], a, b, skip_group_check=True, **k)
                    for e in range(2):
                        mm(e, Z[:, :], Z[:, 0:T], start=True, stop=False)
                    with pe.Fori(0, EF // 16) as i:
                        for j in range(2):
                            pe.wait_ge(hot, i * 2 + j + 1)
                            for e in range(2):
                                for f in range(8):
                                    last = mm(e, oh_lo[j][:, e, f, :], oh_hi[j][:, e, f, :], start=False, stop=False)
                            last.then_inc(counted2, 1)
                    for e in range(2):
                        last = mm(e, Z[:, :], Z[:, 0:T], start=False, stop=True)
                    last.then_inc(deg_done, 1)


def mask_buffers(s):
    return [s.sb("places", [128, CHAINS, 4], I32)] + [s.sem(x) for x in ("places_copied", "mask_rounds", "zeros_put")]


def edge_mask(pool, G, own, lo, hi):
    ix, copied, rounds, scattered = own
    by_chain = G.keys[:, :].rearrange("p (c j) -> p c j", c=CHAINS)
    with pool.Fori(0, hi - lo) as i:
        pool.tensor_copy(ix[:, :, :], by_chain[:, :, ts(i + lo, 4)]).then_inc(copied, 1)
        pool.wait_ge(copied, i + 1)
        for j in range(4):
            pool.sem_inc(rounds, 1)
            for c in range(CHAINS):
                pool.indirect_dma_start(G.mask[:, :], bass.IndirectOffsetOnAxis(ap=ix[:, c, j:j + 1], axis=0),
                                        G.zero_b[:, 0:1], None).then_inc(scattered, 16)
            pool.wait_ge(scattered, i * (4 * 16 * CHAINS) + (j + 1) * 16 * CHAINS)


def segment_max(nc, G, rows, H, M):
    HALVES = ((0, 1563), (1563, N))
    W = HALVES[0][1]
    ring = 5
    with Stage(nc) as s:
        A = s.sb("A", [P, H, N])
        K = [s.sb(f"K{j}", [P, W], BF16) for j in range(ring)]
        junk = [s.sb(f"junk{j}", [P, W], BF16) for j in range(2)]
        red = s.sb("red", [P, U, H, 2])
        aload, read, reduced, turns, reduce_done = [s.sem(x) for x in ("aload", "read", "reduced", "turns", "reduce_done")]
        got = [s.sem(f"got{j}") for j in range(ring)]
        mask = G.mask[0:N * N].rearrange("(n m) a -> n (m a)", m=N)
        units = [(u, a) for u in range(U) for a in range(2)]
        with nc.Block() as block:
            @block.sync
            def _(sp):
                for h in range(H):
                    sp.dma_start(A[:, h, :], over(rows[h, 0:N], P)).then_inc(aload, 16)
                with sp.Fori(0, T // U) as i:
                    for n, (u, a) in enumerate(units):
                        lo, hi = HALVES[a]
                        sp.wait_ge(read, i * len(units) + n + 1)
                        sp.dma_start(K[n % ring][:, 0:hi - lo], mask[ts(i * U + u, P), lo:hi]).then_inc(got[n % ring], 16)

            @block.vector
            def _(v):
                v.sem_inc(read, ring)
                v.sem_inc(reduce_done, 2)
                v.wait_ge(aload, 16 * H)
                with v.Fori(0, T // U) as i:
                    for n, (u, a) in enumerate(units):
                        lo, hi = HALVES[a]
                        v.wait_ge(got[n % ring], (i * 2 + n // ring + 1) * 16)
                        for h in range(H):
                            m = n * H + h
                            v.wait_ge(reduce_done, i * len(units) * H + m + 1)
                            v.sem_inc(turns, 1)
                            v.tensor_tensor_reduce(junk[m % 2][:, 0:hi - lo], K[n % ring][:, 0:hi - lo], A[:, h, lo:hi], 1.0, NEG * 2,
                                                         ALU.add, ALU.max, red[:, u, h, a:a + 1]).then_inc(reduce_done, 1)
                        v.wait_ge(reduce_done, 2 + i * len(units) * H + (n + 1) * H)
                        v.sem_inc(read, 1)
                    v.tensor_reduce(M[:, ts(i, U), :], red[:, :, :, :], AX.X, ALU.max).then_inc(reduced, 1)
                    v.wait_ge(reduced, i + 1)


def aggregate(nc, G, table, W, H, DM, acc):
    WH = W + H
    wide = WH > 512
    NB = 2
    with Stage(nc) as s:
        ix = [s.sb(f"ix{j}", [128, EB, 4], I32) for j in range(RING)]
        R = [s.sb(f"R{j}", [128, EB, WH]) for j in range(RING)]
        hot = [s.sb(f"hot{j}", [128, EB, P]) for j in range(RING)]
        z = [s.sb(f"z{j}", [128, EB, H]) for j in range(2)] if H else None
        hotT = [s.sb(f"hotT{j}", [P, EB, 128]) for j in range(2)] if H else None
        copied, rounds, scores, exp_done, prep, mm_done, z_steps, put, hot_done, turned, turn_out, d_done = [
            s.sem(x) for x in ("copied", "rounds", "scores", "exp", "prep", "mm", "z_steps", "put", "hot", "turned",
                               "turn_out", "d")]
        got = [s.sem(f"got{j}") for j in range(RING)]
        turn_bank = lambda g: G.PS[0:P, 4 + g % 2, 0:EB * 128]
        d_bank = lambda g: G.PS[:, 6 + g % 2, 0:EB * 2 * H].rearrange("p (f h) -> p f h", h=2 * H)

        def wait(eng, sem, n):
            if not isinstance(n, int) or n > 0:
                eng.wait_ge(sem, n)

        def steps(eng, step):
            def of(base, turn):
                def at(d):
                    q, u = divmod(base + d, RING)
                    if isinstance(turn, int) and not 0 <= turn * RING + base + d < NG:
                        return None
                    return turn * RING + (base + d), u, turn + q
                return at
            for g in (-2, -1, 0, 1):
                step(of(g, 0))
            with eng.Fori(0, NG // RING - 1) as i:
                for u in range(RING):
                    step(of(u + 2, i))
            for g in range(NG - RING + 2, NG + 1):
                step(of(g, 0))

        with nc.Block() as block:
            @block.gpsimd
            def _(pool):
                def gather(g, u, first):
                    if not first:
                        pool.wait_ge(mm_done, g - (RING - 1))
                    pool.tensor_copy(ix[u][:, :, :], G.edges[:, ts(g, EB), :]).then_inc(copied, 1)
                    pool.wait_ge(copied, g + 1)
                    pool.sem_inc(rounds, 1)
                    for f in range(EB):
                        pool.indirect_dma_start(R[u][:, f, :], None, table[:, :],
                                                bass.IndirectOffsetOnAxis(ap=ix[u][:, f, 0:1], axis=0)).then_inc(got[u], 16)
                for u in range(RING):
                    gather(u, u, True)
                with pool.Fori(0, NG // RING - 1) as i:
                    for u in range(RING):
                        gather(i * RING + (RING + u), u, False)

            @block.scalar
            def _(act):
                def step(at):
                    if not H:
                        return
                    if at(2):
                        g, u, _ = at(2)
                        wait(act, turned, g + 1)
                        wait(act, d_done, g - 1)
                        act.activation(hotT[u % 2][:, :, :].rearrange("p f e -> p (f e)"), turn_bank(u), ACT.Copy).then_inc(turn_out, 1)
                    if at(1):
                        g, u, _ = at(1)
                        wait(act, scores, g + 1)
                        act.activation(R[u][:, :, W:WH], z[u % 2][:, :, :], ACT.Exp).then_inc(exp_done, 1)
                if H:
                    steps(act, step)

            @block.vector
            def _(v):
                def step(at):
                    if at(2):
                        g, u, _ = at(2)
                        wait(v, mm_done, g - (RING - 1))
                        v.tensor_tensor(hot[u][:, :, :], G.iota[:, :].unsqueeze(1).to_broadcast([128, EB, P]),
                                        G.edges[:, ts(g, EB), 2:3].bitcast(F32).to_broadcast([128, EB, P]),
                                        ALU.is_equal).then_inc(hot_done, 1)
                    if H and at(0):
                        g, u, _ = at(0)
                        wait(v, exp_done, g + 1)
                        r = R[u][:, :, 0:W].rearrange("p f (h c) -> p f h c", h=H)
                        v.tensor_tensor(r, r, R[u][:, :, W:WH].unsqueeze(3).to_broadcast([128, EB, H, W // H]), ALU.mult).then_inc(prep, 1)
                    if at(-1):
                        g, u, _ = at(-1)
                        b = v.value_load(G.bucket[0:1, ts(g, 1)], min_val=0, max_val=T - 1)
                        k = u % NB
                        wait(v, mm_done, g + 1)
                        wait(v, put, g)
                        to = acc[:, ts(b, 1), 0:WH].rearrange("p a w -> p (a w)")
                        if wide:
                            v.tensor_tensor(to.rearrange("p (a w) -> p a w", a=2), to.rearrange("p (a w) -> p a w", a=2),
                                            G.PS[0:P, 2 * k:2 * k + 2, 0:WH // 2], ALU.add).then_inc(put, 1)
                        else:
                            v.tensor_tensor(to, to, G.PS[0:P, k, 0:WH], ALU.add).then_inc(put, 1)
                    if H and at(1):
                        g, u, turn = at(1)
                        wait(v, d_done, g + 1)
                        wait(v, got[u], (turn + 1) * (16 * EB))
                        zj, D2 = z[u % 2][:, :, :], d_bank(u)
                        v.tensor_tensor(zj, R[u][:, :, W:WH], D2[:, :, 0:H], ALU.add).then_inc(z_steps, 1)
                        wait(v, z_steps, g * 3 + 1)
                        v.scalar_tensor_tensor(out=zj, in0=zj, scalar=0.2, in1=zj, op0=ALU.mult, op1=ALU.max).then_inc(z_steps, 1)
                        wait(v, z_steps, g * 3 + 2)
                        v.tensor_tensor(zj, zj, D2[:, :, H:2 * H], ALU.subtract).then_inc(z_steps, 1)
                        wait(v, z_steps, g * 3 + 3)
                        v.tensor_scalar(zj, zj, 0.0, None, ALU.min).then_inc(scores, 1)
                steps(v, step)

            @block.tensor
            def _(pe):
                def step(at):
                    if H and at(2):
                        g, u, _ = at(2)
                        wait(pe, hot_done, g + 1)
                        wait(pe, turn_out, g - 1)
                        for f in range(EB):
                            mm = pe.transpose(turn_bank(u)[:, ts(f, 128)], hot[u][:, f, :], G.ident[:, :])
                        mm.then_inc(turned, 1)
                    if H and at(1):
                        g, u, _ = at(1)
                        wait(pe, turn_out, g + 1)
                        wait(pe, scores, g - 1)
                        b = pe.value_load(G.bucket[0:1, ts(g, 1)], min_val=0, max_val=T - 1)
                        for f in range(EB):
                            mm = pe.matmul(d_bank(u)[:, f, :], hotT[u % 2][:, f, :], DM[:, ts(b, 1), :].rearrange("p a h -> p (a h)"),
                                           start=True, stop=True)
                        mm.then_inc(d_done, 1)
                    if at(0):
                        g, u, turn = at(0)
                        if H:
                            wait(pe, prep, g + 1)
                        else:
                            wait(pe, hot_done, g + 1)
                            wait(pe, got[u], (turn + 1) * (16 * EB))
                        k = u % NB
                        wait(pe, put, g - (NB - 1))
                        for f in range(EB):
                            ends = dict(start=(f == 0), stop=(f == EB - 1))
                            if wide:
                                for a in range(2):
                                    mm = pe.matmul(G.PS[0:P, 2 * k + a, 0:WH // 2], hot[u][:, f, :],
                                                   R[u][:, f, a * (WH // 2):(a + 1) * (WH // 2)], **ends)
                            else:
                                mm = pe.matmul(G.PS[0:P, k, 0:WH], hot[u][:, f, :], R[u][:, f, :], **ends)
                        mm.then_inc(mm_done, 1)
                steps(pe, step)


def store_rows(nc, pairs):
    with Stage(nc) as s:
        stored = s.sem("stored")
        with nc.Block() as block:
            @block.sync
            def _(sp):
                for to, a in pairs:
                    sp.dma_start(to.rearrange("(t p) d -> p t d", p=P), a).then_inc(stored, 16)
                sp.wait_ge(stored, 16 * len(pairs))


def score_weights(nc, G, wt, kc, W, H, a_src, a_dst, wa):
    C, wc, K = W // H, W // 128, kc * 128
    with Stage(nc) as s:
        A, Wt = s.sb("A", [128, wc, 2 * H]), s.sb("Wt", [128, wc, K])
        O = s.sb("O", [128, kc, 2 * H])
        zeroed, loaded, mm_done, copied, stored = [s.sem(x) for x in ("zeroed", "loaded", "mm", "copied", "stored")]
        with nc.Block() as block:
            @block.gpsimd
            def _(pool):
                pool.memset(A[:, :, :], 0.0).then_inc(zeroed, 1)

            @block.sync
            def _(sp):
                sp.dma_start(Wt[:, :, :], wt.rearrange("(c p) k -> p c k", p=128)).then_inc(loaded, 16)
                sp.wait_ge(zeroed, 1)
                n = 16
                for j, a in enumerate((a_src, a_dst)):
                    for r in range(0, W, min(C, 128)):
                        h, p0, m = r // C, r % 128, min(C, 128)
                        sp.dma_start(A[p0:p0 + m, r // 128, j * H + h:j * H + h + 1],
                                     a[r:r + m].rearrange("(p a) -> p a", a=1)).then_inc(loaded, 16)
                        n += 16
                s.n_loaded = n
                sp.wait_ge(copied, 1)
                sp.dma_start(wa[0:K, 0:2 * H].rearrange("(k p) h -> p k h", p=128), O[:, :, :]).then_inc(stored, 16)
                sp.wait_ge(stored, 16)

            @block.tensor
            def _(pe):
                pe.wait_ge(loaded, 16 + 16 * 2 * (W // min(C, 128)))
                for k in range(kc):
                    for c in range(wc):
                        mm = pe.matmul(G.PS[:, k, 0:2 * H], Wt[:, c, ts(k, 128)], A[:, c, :], start=(c == 0), stop=(c == wc - 1))
                mm.then_inc(mm_done, 1)

            @block.vector
            def _(v):
                v.wait_ge(mm_done, 1)
                v.tensor_copy(O[:, :, :], G.PS[:, 0:kc, 0:2 * H]).then_inc(copied, 1)


def gat(nc, G, src, kc, w, wt, a_src, a_dst, W, H, bias, acc, loops=False, eps=0.0, everywhere=False):
    C = W // H
    table = G.table[0:N * (W + H)].rearrange("(n w) -> n w", w=W + H)
    wa = G.wa[0:kc * 128 * 2 * H].rearrange("(k h) -> k h", h=2 * H)
    with Stage(nc) as s:
        AL, M = s.sb("AL", [P, T, 2 * H]), s.sb("M", [P, T, H])
        DM = s.sb("DM", [P, T, 2 * H])
        one, row, wide = s.sb("one", [P, 1]), s.sb("row", [1, 2]), s.sb("wide", [P, 1])
        wself = s.sb("wself", [P, T, H])
        Bw = s.sb("Bw", [P, W])
        score_weights(nc, G, wt, kc, W, H, a_src, a_dst, wa)
        project_rows(nc, G, src, kc, [(wa, 0)], 2 * H, AL)
        project_rows(nc, G, src, kc, [(w, 0)], W, acc[:, :, 0:W])
        store_rows(nc, [(table[:, 0:W], acc[:, :, 0:W]), (table[:, W:W + H], AL[:, :, 0:H])])
        vec_steps(nc, lambda c, v: c(v.tensor_copy(wself[:, :, :], AL[:, :, 0:H])))
        spread_gate(nc, G, wself, H, G.arows)
        segment_max(nc, G, G.arows, H, M)
        a_s, a_d = AL[:, :, 0:H], AL[:, :, H:2 * H]
        steps, ready, turned, exp_done = [s.sem(x) for x in ("steps", "ready", "turned", "exp")]
        with nc.Block() as block:
            @block.vector
            def _(v):
                c = Chain(v, steps)
                leaky = lambda x: v.scalar_tensor_tensor(out=x, in0=x, scalar=0.2, in1=x, op0=ALU.mult, op1=ALU.max)
                m = DM[:, :, H:2 * H]
                if loops:
                    c(v.tensor_tensor(M[:, :, :], M[:, :, :], a_s, ALU.max))
                c(v.tensor_copy(DM[:, :, 0:H], a_d))
                c(v.tensor_tensor(m, M[:, :, :], a_d, ALU.add))
                c(leaky(m))
                if everywhere:
                    c(v.tensor_reduce(one[:, :], m, AX.XY, ALU.max))
                    v.sem_inc(ready, 1)
                    v.wait_ge(turned, 1)
                    c(v.tensor_reduce(row[:, 0:1], G.PS[0:1, 0, 0:P], AX.X, ALU.max))
                    v.sem_inc(ready, 1)
                    v.wait_ge(turned, 2)
                    c(v.tensor_copy(wide[:, :], G.PS[0:P, 1, 0:1]))
                    c(v.tensor_copy(m, wide[:, :].unsqueeze(2).to_broadcast([P, T, H])))
                if loops:
                    c(v.tensor_tensor(wself[:, :, :], a_s, a_d, ALU.add))
                    c(leaky(wself[:, :, :]))
                    c(v.tensor_tensor(wself[:, :, :], wself[:, :, :], m, ALU.subtract))
                    v.sem_inc(ready, 1)
                    v.wait_ge(exp_done, 1)
                    for h in range(H):
                        r = acc[:, :, h * C:(h + 1) * C]
                        c(v.tensor_tensor(r, r, wself[:, :, h:h + 1].to_broadcast([P, T, C]), ALU.mult))
                    c(v.tensor_copy(acc[:, :, W:W + H], wself[:, :, :]))
                else:
                    c(v.memset(acc[:, :, :], 0.0))

            if everywhere:
                @block.tensor
                def _(pe):
                    pe.wait_ge(ready, 1)
                    pe.transpose(G.PS[0:1, 0, 0:P], one[:, :], G.ident[0:P, 0:P]).then_inc(turned, 1)
                    pe.wait_ge(ready, 2)
                    pe.matmul(G.PS[0:P, 1, 0:1], G.ones[0:1, 0:P], row[:, 0:1], start=True, stop=True).then_inc(turned, 1)
            if loops:
                @block.scalar
                def _(act):
                    act.wait_ge(ready, 1)
                    act.activation(wself[:, :, :], wself[:, :, :], ACT.Exp).then_inc(exp_done, 1)
        aggregate(nc, G, table, W, H, DM, acc)
        loaded, last = s.sem("loaded"), s.sem("last")
        with nc.Block() as block:
            @block.sync
            def _(sp):
                sp.dma_start(Bw[:, :], over(bias, P)).then_inc(loaded, 16)

            @block.vector
            def _(v):
                c = Chain(v, last)
                if eps:
                    c(v.tensor_scalar(acc[:, :, W:W + H], acc[:, :, W:W + H], eps, None, ALU.add))
                c(v.tensor_copy(M[:, :, :], acc[:, :, W:W + H]))
                c(v.reciprocal(M[:, :, :], M[:, :, :]))
                for h in range(H):
                    r = acc[:, :, h * C:(h + 1) * C]
                    c(v.tensor_tensor(r, r, M[:, :, h:h + 1].to_broadcast([P, T, C]), ALU.mult))
                v.wait_ge(loaded, 16)
                c(v.tensor_tensor(acc[:, :, 0:W], acc[:, :, 0:W], Bw[:, :].unsqueeze(1).to_broadcast([P, T, W]), ALU.add))


def gnn0(nc, G, I):
    table = G.table[0:N * D].rearrange("(n w) -> n w", w=D)
    with Stage(nc) as s:
        acc = s.sb("acc", [P, T, D])
        dg = s.sb("dg", [P, 2, T])
        Bw = s.sb("Bw", [P, D])
        steps, root = s.sem("steps"), s.sem("root")
        with nc.Block() as block:
            @block.vector
            def _(v):
                v.tensor_scalar(dg[:, 0, :], G.out_deg[:, :], 1.0, None, ALU.max).then_inc(steps, 1)
                v.tensor_scalar(dg[:, 1, :], G.in_deg[:, :], 1.0, None, ALU.max).then_inc(steps, 1)
                v.wait_ge(root, 1)
                v.reciprocal(dg[:, :, :], dg[:, :, :]).then_inc(steps, 1)

            @block.scalar
            def _(act):
                act.wait_ge(steps, 2)
                act.activation(dg[:, :, :], dg[:, :, :], ACT.Sqrt).then_inc(root, 1)
        project_rows(nc, G, G.xn, KD, [(I["L0_gnn_weight"], 0)], D, acc, mul=dg[:, 0, :])
        store_rows(nc, [(table, acc[:, :, :])])
        vec_steps(nc, lambda c, v: c(v.memset(acc[:, :, :], 0.0)))
        aggregate(nc, G, table, D, 0, None, acc)
        loaded, last = s.sem("loaded"), s.sem("last")
        with nc.Block() as block:
            @block.sync
            def _(sp):
                sp.dma_start(Bw[:, :], over(I["L0_gnn_bias"], P)).then_inc(loaded, 16)

            @block.vector
            def _(v):
                c = Chain(v, last)
                c(v.tensor_tensor(acc[:, :, :], acc[:, :, :], dg[:, 1, :].unsqueeze(2).to_broadcast([P, T, D]), ALU.mult))
                v.wait_ge(loaded, 16)
                c(v.tensor_tensor(acc[:, :, :], acc[:, :, :], Bw[:, :].unsqueeze(1).to_broadcast([P, T, D]), ALU.add))
        rows_to_cols(nc, G, acc, D, G.xT, add=True)


def gnn1(nc, G, I):
    p = lambda n: I["L1_gnn_" + n]
    flat = lambda n: p(n).rearrange("a h c -> (a h c)")
    with Stage(nc) as s:
        acc = s.sb("acc", [P, T, 516])
        gat(nc, G, G.xn, KD, p("W1_T"), p("W1"), flat("a_src1"), flat("a_dst1"), 512, 4, p("b1"), acc, eps=1e-16)
        elu_like(nc, flat3(acc), T * 516, False)
        h = s.sb("h", [128, 4, NC])
        rows_to_cols(nc, G, acc[:, :, 0:512], 512, h)
        acc = acc[:, :, 0:D + 1]
        gat(nc, G, h, 4, p("W2_T"), p("W2"), flat("a_src2"), flat("a_dst2"), D, 1, p("b2"), acc, eps=1e-16)
        rows_to_cols(nc, G, acc[:, :, 0:D], D, G.xT, add=True)


def gnn2(nc, G, I):
    p = lambda n: I["L2_gnn_" + n]
    flat = lambda n: p(n).rearrange("h c -> (h c)")
    with Stage(nc) as s:
        h = s.sb("h", [128, KD, NC])
        with Stage(nc) as s2:
            acc = s2.sb("acc", [P, T, D + 4])
            gat(nc, G, G.xn, KD, p("W1"), p("W1_T"), flat("a_src1"), flat("a_dst1"), D, 4, p("b1"), acc, loops=True)
            rows_to_cols(nc, G, acc[:, :, 0:D], D, h)
        elu_like(nc, flat3(h), KD * NC, False)
        acc = s.sb("acc2", [P, T, D + 1])
        gat(nc, G, h, KD, p("W2"), p("W2_T"), flat("a_src2"), flat("a_dst2"), D, 1, p("b2"), acc, loops=True)
        rows_to_cols(nc, G, acc[:, :, 0:D], D, G.xT, add=True)


def move_rows(nc, kind, far, index, near):
    with Stage(nc) as s:
        moved = s.sem("moved")
        with nc.Block() as block:
            @block.gpsimd
            def _(pool):
                for t in range(T):
                    at = bass.IndirectOffsetOnAxis(ap=index[:, t:t + 1], axis=0)
                    if kind == "scatter":
                        pool.indirect_dma_start(far[:, :], at, near[:, t, :], None).then_inc(moved, 16)
                    else:
                        pool.indirect_dma_start(near[:, t, :], None, far[:, :], at).then_inc(moved, 16)
                pool.wait_ge(moved, 16 * T)


def dma(nc, to, of):
    with Stage(nc) as s:
        done = s.sem("done")
        with nc.Block() as block:
            @block.sync
            def _(sp):
                sp.dma_start(to, of).then_inc(done, 16)
                sp.wait_ge(done, 16)


def load_rows(nc, far, near):
    with Stage(nc) as s:
        loaded = s.sem("loaded")
        with nc.Block() as block:
            @block.sync
            def _(sp):
                sp.dma_start(near, far.rearrange("(t p) d -> p t d", p=P)).then_inc(loaded, 16)
                sp.wait_ge(loaded, 16)


def act_cols(nc, x, func):
    with Stage(nc) as s:
        done = s.sem("done")
        with nc.Block() as block:
            @block.scalar
            def _(act):
                act.activation(x, x, func).then_inc(done, 1)


def conv(nc, G, src, w, b, out):
    taps = 4
    with Stage(nc) as s:
        Wc, Bc = s.sb("Wc", [128, KD, taps]), s.sb("Bc", [128, KD])
        loaded, steps = s.sem("loaded"), s.sem("steps")
        with nc.Block() as block:
            @block.sync
            def _(sp):
                sp.dma_start(Wc[:, :, :], w.rearrange("(k p) j -> p k j", p=128)).then_inc(loaded, 16)
                sp.dma_start(Bc[:, :], blocks(b)).then_inc(loaded, 16)

            @block.vector
            def _(v):
                v.wait_ge(loaded, 32)
                c = Chain(v, steps)
                for k in range(KD):
                    c(v.tensor_scalar(out[:, k, :], src[:, k, :], Wc[:, k, taps - 1:taps], Bc[:, k:k + 1], ALU.mult, ALU.add))
                    for j in range(taps - 1):
                        d = taps - 1 - j
                        c(v.scalar_tensor_tensor(out=out[:, k, d:NC], in0=src[:, k, 0:NC - d], scalar=Wc[:, k, j:j + 1],
                                                 in1=out[:, k, d:NC], op0=ALU.mult, op1=ALU.add))
        act_cols(nc, out[:, :, :], ACT.Silu)


def softplus_cols(nc, G, x):
    with Stage(nc) as s:
        y, w, l = s.sb("y", [128, KD, CW]), s.sb("w", [128, KD, CW]), s.sb("l", [128, KD, CW])
        d = s.sb("d", [128, KD, CW])
        steps, neg, exp_done, one, ln_done = [s.sem(x) for x in ("steps", "neg", "exp", "one", "ln")]
        a = lambda t: t[:, :, :]
        with nc.Block() as block:
            @block.vector
            def _(v):
                with v.Fori(0, NCH) as i:
                    xs = x[:, :, ts(i, CW)]
                    c = Chain(v, steps, i * 12)
                    c(v.tensor_scalar(a(y), xs, -1.0, None, ALU.mult))
                    v.tensor_tensor(a(y), a(y), xs, ALU.min).then_inc(neg, 1)
                    v.wait_ge(exp_done, i + 1)
                    c(v.tensor_scalar(a(w), a(y), 1.0, None, ALU.add))
                    v.sem_inc(one, 1)
                    c(v.tensor_scalar(a(d), a(y), -0.25, 1.0 / 3, ALU.mult, ALU.add))
                    c(v.tensor_tensor(a(d), a(d), a(y), ALU.mult))
                    c(v.scalar_tensor_tensor(out=a(d), in0=a(d), scalar=-0.5, in1=a(y), op0=ALU.add, op1=ALU.mult))
                    c(v.scalar_tensor_tensor(out=a(d), in0=a(d), scalar=1.0, in1=a(y), op0=ALU.add, op1=ALU.mult))
                    v.wait_ge(ln_done, i + 1)
                    c(v.tensor_scalar(a(w), a(y), 1.0 / 64, None, ALU.is_ge))
                    c(v.tensor_scalar(a(y), a(y), 1.0 / 64, None, ALU.is_lt))
                    c(v.tensor_tensor(a(l), a(l), a(w), ALU.mult))
                    c(v.tensor_tensor(a(d), a(d), a(y), ALU.mult))
                    c(v.tensor_tensor(a(l), a(l), a(d), ALU.add))
                    c(v.scalar_tensor_tensor(out=xs, in0=xs, scalar=0.0, in1=a(l), op0=ALU.max, op1=ALU.add))
                    assert c.n == 12

            @block.scalar
            def _(act):
                with act.Fori(0, NCH) as i:
                    act.wait_ge(neg, i + 1)
                    act.activation(a(y), a(y), ACT.Exp).then_inc(exp_done, 1)
                    act.wait_ge(one, i + 1)
                    act.activation(a(l), a(w), ACT.Ln).then_inc(ln_done, 1)


def state_scan(nc, G, xc, dt, BC, z, A_log, D_param, S, y):
    with Stage(nc) as s:
        A, Dp = s.sb("A", [128, KD, S]), s.sb("Dp", [128, KD])
        sel = s.sb("sel", [S, S, 128])
        last = s.sb("last", [128, KD, S])
        u = s.sb("u", [128, KD, CW])
        dA = [s.sb(f"dA{k}", [128, CW]) for k in range(2)]
        ex, dts = [s.sb(f"ex{k}", [128, CW]) for k in range(2)], s.sb("dts", [128, KD, CW])
        dB = s.sb("dB", [128, CW])
        h = s.sb("h", [128, CW])
        hc = [s.sb(f"hc{k}", [128, CW]) for k in range(2)]
        loaded, made, a_done, steps, spread, hc_done, dA_done, dA_used, summed, out_done, scan_done = [
            s.sem(x) for x in ("loaded", "made", "a", "steps", "spread", "hc", "dA", "dA_used", "summed", "out", "scan")]
        spread_free, y_steps, pe_turns = [s.sem(x) for x in ("spread_free", "y_steps", "pe_turns")]
        dt_copied, ex_done, pool_turns = [s.sem(x) for x in ("dt_copied", "ex", "pool_turns")]
        with nc.Block() as block:
            @block.sync
            def _(sp):
                sp.dma_start(A[:, :, :], A_log.rearrange("(k p) s -> p k s", p=128)).then_inc(loaded, 16)
                sp.dma_start(Dp[:, :], blocks(D_param)).then_inc(loaded, 16)

            @block.gpsimd
            def _(pool):
                pool.memset(sel[:, :, :], 0.0).then_inc(made, 1)
                pool.wait_ge(made, 1)
                pool.affine_select(out=sel[:, :, :], in_=sel[:, :, :], compare_op=ALU.not_equal, fill=1.0, base=0,
                                   pattern=[[-1, S], [0, 128]], channel_multiplier=1).then_inc(made, 1)
                pool.wait_ge(a_done, 2)
                with pool.Fori(0, NCH) as i:
                    pool.tensor_copy(dts[:, :, :], dt[:, :, ts(i, CW)]).then_inc(dt_copied, 1)
                    pool.wait_ge(dt_copied, i + 1)
                    for t in range(S):
                        for k in range(KD):
                            n = i * S * KD + t * KD + k
                            pool.wait_ge(dA_done, n + 1)
                            pool.sem_inc(pool_turns, 1)
                            pool.tensor_scalar(ex[k][:, :], dts[:, k, :], A[:, k, t:t + 1], -1e3, ALU.mult, ALU.max).then_inc(ex_done, 1)
                    pool.wait_ge(ex_done, (i + 1) * S * KD)

            @block.scalar
            def _(act):
                act.wait_ge(loaded, 32)
                act.activation(A[:, :, :], A[:, :, :], ACT.Exp).then_inc(a_done, 1)
                act.sem_inc(dA_done, 2)
                with act.Fori(0, NCH) as i:
                    for t in range(S):
                        for k in range(KD):
                            n = i * S * KD + t * KD + k
                            act.wait_ge(ex_done, n + 1)
                            act.wait_ge(dA_used, n + 1)
                            act.activation(dA[k][:, :], ex[k][:, :], ACT.Exp).then_inc(dA_done, 1)

            @block.tensor
            def _(pe):
                pe.wait_ge(made, 2)
                def add_up(i, t):
                    for k in range(KD):
                        pe.wait_ge(hc_done, i * S * KD + t * KD + k + 1)
                        pe.matmul(G.PS[:, 4 + k, 0:CW], G.ident[:, :], hc[k][:, :], start=(t == 0), stop=(t == S - 1)).then_inc(summed, 1)
                with pe.Fori(0, NCH) as i:
                    for t in range(S):
                        pe.wait_ge(spread_free, i * S + t + 1)
                        pe.sem_inc(pe_turns, 1)
                        for j in range(2):
                            mm = pe.matmul(G.PS[:, 2 * (t % 2) + j, 0:CW], sel[:, t, :], BC[j][:, 0, ts(i, CW)], start=True, stop=True)
                        mm.then_inc(spread, 1)
                        if t == 1:
                            pe.wait_ge(out_done, i + 1)
                        if t:
                            add_up(i, t - 1)
                    add_up(i, S - 1)

            @block.vector
            def _(v):
                v.sem_inc(spread_free, 2)
                v.sem_inc(out_done, 1)
                v.sem_inc(dA_used, 2)
                v.sem_inc(summed, 2)
                v.wait_ge(a_done, 1)
                v.tensor_scalar(A[:, :, :], A[:, :, :], -1.0, None, ALU.mult).then_inc(a_done, 1)
                v.memset(last[:, :, :], 0.0).then_inc(scan_done, 1)
                v.wait_ge(scan_done, 1)
                with v.Fori(0, NCH) as i:
                    c = Chain(v, steps, i * (1 + 3 * S * KD))
                    c(v.tensor_tensor(u[:, :, :], dt[:, :, ts(i, CW)], xc[:, :, ts(i, CW)], ALU.mult))
                    for t in range(S):
                        v.wait_ge(spread, i * S + t + 1)
                        for k in range(KD):
                            n = i * S * KD + t * KD + k
                            c(v.tensor_tensor(dB[:, :], u[:, k, :], G.PS[:, 2 * (t % 2), 0:CW], ALU.mult))
                            v.wait_ge(dA_done, 2 + n + 1)
                            c(v.tensor_tensor_scan(h[:, :], dA[k][:, :], dB[:, :], last[:, k, t:t + 1], ALU.mult, ALU.add))
                            v.sem_inc(dA_used, 1)
                            c(v.tensor_copy(last[:, k, t:t + 1], h[:, CW - 1:CW]))
                            v.wait_ge(summed, n + 1)
                            v.tensor_tensor(hc[k][:, :], h[:, :], G.PS[:, 2 * (t % 2) + 1, 0:CW], ALU.mult).then_inc(hc_done, 1)
                            v.wait_ge(hc_done, n + 1)
                            if k == KD - 1:
                                v.sem_inc(spread_free, 1)
                    v.wait_ge(summed, 2 + (i + 1) * S * KD)
                    for k in range(KD):
                        v.scalar_tensor_tensor(out=y[:, k, ts(i, CW)], in0=xc[:, k, ts(i, CW)], scalar=Dp[:, k:k + 1],
                                               in1=G.PS[:, 4 + k, 0:CW], op0=ALU.mult, op1=ALU.add).then_inc(y_steps, 1)
                    v.wait_ge(y_steps, (i + 1) * 2)
                    v.tensor_tensor(y[:, :, ts(i, CW)], y[:, :, ts(i, CW)], z[:, :, ts(i, CW)], ALU.mult).then_inc(out_done, 1)


def gnn3(nc, G, I):
    p = lambda n: I["L3_gnn_" + n]
    S, R = 16, 16
    far = G.table[0:N * D].rearrange("(n w) -> n w", w=D)
    with Stage(nc) as s:
        place, place_i, key = s.sb("place", [P, T]), s.sb("place_i", [P, T], I32), s.sb("key", [P, T])
        noise = s.sb("noise", [P, T])
        load_rows(nc, I["node_vec"].rearrange("(n a) -> n a", a=1), noise[:, :].unsqueeze(2))
        vec_steps(nc, lambda c, v: c(v.tensor_tensor(key[:, :], G.out_deg[:, :], noise[:, :], ALU.add)))
        rank(nc, G, key, G.key_row, place)
        vec_steps(nc, lambda c, v: c(v.tensor_copy(place_i[:, :], place[:, :])))
        with Stage(nc) as s2:
            xc, z = s2.sb("xc", [128, KD, NC]), s2.sb("z", [128, KD, NC])
            with Stage(nc) as s3:
                xp = s3.sb("xp", [128, KD, NC])
                with Stage(nc) as s4:
                    rows = s4.sb("rows", [P, T, D])
                    cols_to_rows(nc, G, G.xn, rows)
                    move_rows(nc, "scatter", far, place_i, rows)
                    load_rows(nc, far, rows[:, :, :])
                    rows_to_cols(nc, G, rows, D, xp)
                raw = s3.sb("raw", [128, KD, NC])
                w = p("in_proj_w_T")
                dense_cols(nc, G, xp, KD, w[:, 0:D], KD, raw)
                dense_cols(nc, G, xp, KD, w[:, D:2 * D], KD, z)
                act_cols(nc, z[:, :, :], ACT.Silu)
                conv(nc, G, raw, p("conv_w"), p("conv_b"), xc)
            dt = s2.sb("dt", [128, KD, NC])
            w = p("x_proj_w_T")
            with Stage(nc) as s3:
                low = s3.sb("low", [R, 1, NC])
                dense_cols(nc, G, xc, KD, w[:, 0:R], 1, low, mp=R)
                dense_cols(nc, G, low, 1, p("dt_proj_w_T"), KD, dt, bias=p("dt_proj_b"), kp=R)
            softplus_cols(nc, G, dt)
            BC = [s2.sb(f"BC{j}", [S, 1, NC]) for j in range(2)]
            for j in range(2):
                dense_cols(nc, G, xc, KD, w[:, R + j * S:R + (j + 1) * S], 1, BC[j], mp=S)
            state_scan(nc, G, xc, dt, BC, z, p("A_log"), p("D_param"), S, xc)
            dense_cols(nc, G, xc, KD, p("out_proj_w_T"), KD, z)
            rows = s2.sb("rows", [P, T, D])
            cols_to_rows(nc, G, z, rows)
            store_rows(nc, [(far, rows[:, :, :])])
        with Stage(nc) as s2:
            ha = s2.sb("ha", [128, KD, NC])
            copy_cols(nc, flat3(ha), flat3(G.xn))
            with Stage(nc) as s3:
                rows = s3.sb("rows", [P, T, D])
                move_rows(nc, "gather", far, place_i, rows)
                rows_to_cols(nc, G, rows, D, ha, add=True)
            norm_cols(nc, G, ha, ha, gain=p("ln_global_g"), shift=p("ln_global_b"))
            dma(nc, G.aside, flat3(ha))
        hl = s.sb("hl", [128, KD, NC])
        with Stage(nc) as s2:
            acc = s2.sb("acc", [P, T, D + 4])
            flat = lambda n: p(n).rearrange("h c -> (h c)")
            gat(nc, G, G.xn, KD, p("gat_w_T"), p("gat_w"), flat("gat_a_src"), flat("gat_a_tgt"), D, 4, p("gat_b"), acc,
                eps=1e-16, everywhere=True)
            rows_to_cols(nc, G, acc[:, :, 0:D], D, hl)
        ha, g = s.sb("ha", [128, KD, NC]), s.sb("g", [128, KD, NC])
        dma(nc, flat3(ha), G.aside)
        add_cols(nc, flat3(hl), flat3(G.xn))
        elu_like(nc, flat3(hl), KD * NC, False)
        norm_cols(nc, G, hl, hl, gain=p("ln_local_g"), shift=p("ln_local_b"))
        dense_cols(nc, G, hl, KD, p("wl_T"), KD, g)
        dense_cols(nc, G, ha, KD, p("wg_T"), KD, g, add=True)
        act_cols(nc, g[:, :, :], ACT.Sigmoid)

        def blend(c, v):
            c(v.tensor_tensor(flat3(hl), flat3(hl), flat3(ha), ALU.subtract))
            c(v.tensor_tensor(flat3(hl), flat3(hl), flat3(g), ALU.mult))
            c(v.tensor_tensor(flat3(hl), flat3(hl), flat3(ha), ALU.add))
            c(v.tensor_copy(flat3(g), flat3(hl)))
        vec_steps(nc, blend)
        one_ffn(nc, G, hl, KD, p("ff1_w_T"), p("ff1_b"), p("ff2_w_T"), p("ff2_b"), 512, ACT.Relu, g)
        norm_cols(nc, G, g, G.xT, gain=p("ln2_g"), shift=p("ln2_b"), add=G.xT)


GNN = {0: gnn0, 2: gnn1, 4: gnn2, 6: gnn3}
MIX = {0: mix0, 2: mix1, 4: mix2, 6: mix3}


def build(nc, I, out):
    class G:
        pass
    with ExitStack() as mem:
        mem.enter_context(nc.allow_non_contiguous_dma(reason="biases, a feature to a partition"))
        sb = lambda name, shape, dt=F32: mem.enter_context(nc.sbuf_tensor(name, shape, dt))
        G.xT, G.xn = sb("xT", [128, KD, NC]), sb("xn", [128, KD, NC])
        G.ident, G.ones, G.mean = sb("ident", [128, 128]), sb("ones", [128, 128]), sb("mean", [128, 128])
        G.blockmask, G.before, G.upto = sb("blockmask", [128, 128]), sb("before", [P, P]), sb("upto", [P, P])
        G.after = sb("after", [P, P])
        G.iota, G.iota_i, G.eps = sb("iota", [128, P]), sb("iota_i", [128, P], I32), sb("eps", [128, 1])
        G.zero = sb("zero", [128, CW])
        G.PS = mem.enter_context(nc.psum_tensor("PS", [128, 8, 512], F32))
        dram = lambda name, shape, dt=F32: nc.dram_tensor(name, shape, dt, kind="Internal").ap()
        G.gate = dram("gate_rows", (8, NC))
        G.key_row, G.zeros_row = dram("key_row", (N,)), dram("zeros_row", (512,))
        G.edges, G.bucket = sb("edges", [128, ET, 4], I32), sb("bucket", [1, NG], I32)
        G.out_deg, G.in_deg = sb("out_deg", [P, T]), sb("in_deg", [P, T])
        G.sorted = dram("sorted_edges", (ET * 128, 4), I32)
        G.table, G.wa = dram("table", (N * 516,)), dram("wa", (512 * 8,))
        G.slots, G.results = dram("slots", (24 * 384 + N, D)), dram("results", (24 * 384, D))
        G.aside = dram("aside", (128, KD * NC))
        G.arows, G.mask = dram("arows", (4, NC)), dram("mask", (N * N + CHAINS * 128, 1), BF16)
        G.zero_b, G.keys = sb("zero_b", [128, 1], BF16), sb("keys", [128, ET], I32)
        setup(nc, G, I["x"])
        with Stage(nc) as s:
            done = s.sem("done")
            with nc.Block() as block:
                @block.vector
                def _(v):
                    v.memset(G.zero_b[:, :], 0.0)
                    v.memset(G.zero[:, :], 0.0).then_inc(done, 1)

                @block.sync
                def _(sp):
                    sp.wait_ge(done, 1)
                    sp.dma_start(G.gate[0:8, N:NC], G.zero[0:8, 0:NC - N]).then_inc(done, 16)
                    sp.wait_ge(done, 17)
        p = lambda name: I[name]
        for k in range(BLOCKS):
            if k == 0:
                sort_edges(nc, G, I)
                mask_keys(nc, G)
            if k in MIX:
                norm_cols(nc, G, G.xT, G.xn)
                GNN[k](nc, G, I)
                MIX[k](nc, G, I)
            if k == 1:
                with Stage(nc) as s:
                    L = s.sb("L", [P, T, 8])
                    norm_cols(nc, G, G.xT, G.xn)
                    project_rows(nc, G, G.xn, KD, [(p("L0_ffn_Wr"), 0)], 8, L, [(p("L0_ffn_br"), 0)])
                    softmax_gates(nc, G, L, 8)
                    spread_gate(nc, G, L, 8, G.gate)
                bn_ffn(nc, G, I, G.xT)
            if k == 5:
                top_k_ffn(nc, G, I)
            if k == 3:
                shared = [p("L1_ffn_" + a).rearrange("(a k) f -> a k f" if a[0] == "W" else "(a f) -> a f", a=1)
                          for a in ("W1s", "b1s", "W2s", "b2s")]
                routed_ffn(nc, G, I, p("L1_ffn_Wr"), None, [p("L1_ffn_W1p"), p("L1_ffn_b1p"), p("L1_ffn_W2p"), p("L1_ffn_b2p"), 1024],
                           8, 2, ACT.Gelu, 384)
                ffn(nc, G, G.xn, KD, *shared, 1024, ACT.Gelu, G.xT, 1, None)
            if k == 7:
                routed_ffn(nc, G, I, p("L3_ffn_gate_w"), p("L3_ffn_gate_b"),
                           [p("L3_ffn_w1"), p("L3_ffn_b1"), p("L3_ffn_w2"), p("L3_ffn_b2"), 1024], 8, 1, ACT.Relu, 512)
        finish(nc, G, out)


def kernel(**inputs):
    import numpy as np
    import concourse.bacc as bacc
    from concourse.bass_utils import run_bass_kernel_spmd

    nc = bacc.Bacc("TRN2", target_bir_lowering=False, num_devices=1)
    turned = ["L1_gnn_W1", "L1_gnn_W2", "L2_gnn_W1", "L2_gnn_W2", "L3_gnn_gat_w", "L3_gnn_in_proj_w", "L3_gnn_x_proj_w",
              "L3_gnn_dt_proj_w", "L3_gnn_out_proj_w", "L3_gnn_wl", "L3_gnn_wg", "L3_gnn_ff1_w", "L3_gnn_ff2_w"]
    arrays, aps = {}, {}
    for name, a in list(inputs.items()) + [(n + "_T", np.asarray(inputs[n]).T) for n in turned]:
        if name in ("edge_weight", "L2_mix_t", "L2_ffn_attention_mask"):
            continue
        a = np.ascontiguousarray(a)
        arrays["in_" + name] = a
        aps[name] = nc.dram_tensor("in_" + name, a.shape, mybir.dt.from_np(a.dtype), kind="ExternalInput").ap()
    out = nc.dram_tensor("out_x", (N, D), F32, kind="ExternalOutput").ap()
    build(nc, aps, out)
    return run_bass_kernel_spmd(nc, [arrays], core_ids=[0]).results[0]["out_x"]
```
